# Optimizing a Trainium2 kernel written in Bass

```python
import numpy as np
import jax
import jax.numpy as jnp

def _softmax(x, axis=-1):
    return jax.nn.softmax(x, axis=axis)

def _gelu(x):
    return jax.nn.gelu(x, approximate=True)

def _silu(x):
    return jax.nn.silu(x)

def _sigmoid(x):
    return jax.nn.sigmoid(x)

def _layernorm(x, axis=-1, eps=1e-05):
    m = jnp.mean(x, axis=axis, keepdims=True)
    v = jnp.var(x, axis=axis, keepdims=True)
    return (x - m) / jnp.sqrt(v + eps)

def _scatter_add(tgt, idx, src, axis=0):
    return tgt.at[idx].add(src)

def _segment_sum(src, seg, n):
    return jax.ops.segment_sum(src, seg, n)
kernel_name = 'mk_decoder_postln_d2_seqx_r8_528cd2'

def setup_inputs(seed: int=0):
    np.random.seed(seed)
    _w = jnp.asarray

    def _rec_inputs():
        import jax
        import jax.numpy as jnp
        _rk = jax.random.key(seed)
        x = -0.0002928 + 1 * jax.random.normal(jax.random.fold_in(_rk, 1), (16, 64, 128), jnp.float32)
        _lenS = 64 - jax.random.randint(jax.random.fold_in(_rk, 7), (16,), 0, max(1, 64 // 4) + 1, jnp.int32)
        _lenS2 = 64 - jax.random.randint(jax.random.fold_in(_rk, 8), (16,), 0, max(1, 64 // 4) + 1, jnp.int32)
        _ctx_1024P = jax.random.normal(jax.random.fold_in(_rk, 11), (16, 16, 128), jnp.float32)
        _ctx_1024c = jax.random.dirichlet(jax.random.fold_in(_rk, 511), 0.3 * jnp.ones((16,), jnp.float32), (16, 64))
        _ctx_1024t = jnp.einsum('bsk,bkd->bsd', _ctx_1024c, _ctx_1024P)
        _ctx_1024t = _ctx_1024t * jax.lax.rsqrt(jnp.mean(jnp.square(_ctx_1024t)) + 1e-12) * 0.953939
        ctx_1024 = -1.39393e-06 + 0.999914 * (_ctx_1024t + 0.3 * jax.random.normal(jax.random.fold_in(_rk, 611), (16, 64, 128), jnp.float32))
        return (x, ctx_1024)
    x, ctx_1024 = _rec_inputs()

    def _L0_attn_setup():
        import jax, jax.numpy as jnp
        import numpy as np
        B, S, D, H = (2, 256, 128, 16)
        HD = D // H
        FF = 512
        NUM_ITERS = 8
        DT = 0.1
        LN_EPS = 1e-05

        def _ln(x, g, b):
            m = jnp.mean(x, axis=-1, keepdims=True)
            v = jnp.var(x, axis=-1, keepdims=True)
            return (x - m) * jax.lax.rsqrt(v + LN_EPS) * g + b

        def _forward(x, qkv_w, qkv_b, out_w, out_b, g_attn, b_attn, g1, b1, g2, b2, w_ctx, w_x, b_inl, ff_w1, ff_b1, ff_w2, ff_b2):
            b, s, d = x.shape
            xn = _ln(x, g_attn, b_attn)
            qkv = (xn @ qkv_w + qkv_b).reshape(b, s, 3, H, HD)
            qkv = jnp.transpose(qkv, (2, 0, 3, 1, 4))
            q, k, v = (qkv[0], qkv[1], qkv[2])
            scores = jnp.einsum('bhqd,bhkd->bhqk', q, k) / np.sqrt(HD).astype(np.float32)
            causal = jnp.triu(jnp.ones((s, s), dtype=bool), 1)
            scores = jnp.where(causal[None, None], -jnp.inf, scores)
            attn_w = jax.nn.softmax(scores, axis=-1)
            attn = jnp.einsum('bhqk,bhkd->bhqd', attn_w, v)
            attn = jnp.transpose(attn, (0, 2, 1, 3)).reshape(b, s, d)
            attn = attn @ out_w + out_b
            x = x + attn
            ctx = attn.reshape(b * s, d)
            xs = _ln(x, g1, b1).reshape(b * s, d)
            vs = jnp.zeros_like(xs)

            def step(carry, _):
                xs, vs = carry
                u = jnp.tanh(ctx @ w_ctx + xs @ w_x + b_inl)
                vn = vs + DT * (u - xs - vs)
                xn_ = xs + DT * vn
                return ((xn_, vn), None)
            (xs, vs), _ = jax.lax.scan(step, (xs, vs), None, length=NUM_ITERS)
            x = x + xs.reshape(b, s, d)
            h = _ln(x, g2, b2)
            h = jax.nn.gelu(h @ ff_w1 + ff_b1, approximate=False)
            x = x + (h @ ff_w2 + ff_b2)
            return x
        key = jax.random.key(seed)
        ks = jax.random.split(key, 16)

        def xav(k, shape):
            lim = np.sqrt(6.0 / (shape[0] + shape[1]))
            return jax.random.uniform(k, shape, minval=-lim, maxval=lim, dtype=jnp.float32)
        return {'x': jax.random.normal(ks[0], (B, S, D), dtype=jnp.float32), 'qkv_w': xav(ks[1], (D, 3 * D)), 'qkv_b': jnp.zeros((3 * D,), jnp.float32), 'out_w': xav(ks[2], (D, D)), 'out_b': jnp.zeros((D,), jnp.float32), 'g_attn': jnp.ones((D,), jnp.float32), 'b_attn': jnp.zeros((D,), jnp.float32), 'g1': jnp.ones((D,), jnp.float32), 'b1': jnp.zeros((D,), jnp.float32), 'g2': jnp.ones((D,), jnp.float32), 'b2': jnp.zeros((D,), jnp.float32), 'w_ctx': xav(ks[3], (D, D)), 'w_x': xav(ks[4], (D, D)), 'b_inl': jnp.zeros((D,), jnp.float32), 'ff_w1': xav(ks[5], (D, FF)), 'ff_b1': jnp.zeros((FF,), jnp.float32), 'ff_w2': xav(ks[6], (FF, D)), 'ff_b2': jnp.zeros((D,), jnp.float32)}
    _L0_attn_all = _L0_attn_setup()
    _L0_attn_in = {k: v for k, v in _L0_attn_all.items() if k in ('qkv_w', 'qkv_b', 'out_w', 'out_b', 'g_attn', 'b_attn', 'g1', 'b1', 'g2', 'b2', 'w_ctx', 'w_x', 'b_inl', 'ff_w1', 'ff_b1', 'ff_w2', 'ff_b2')}
    del _L0_attn_all

    def _L0_xattn_setup():
        import jax, jax.numpy as jnp
        import numpy as np
        import math

        def _neighbor_stack(x):
            prev = jnp.pad(x[:, :-1], ((0, 0), (1, 0), (0, 0), (0, 0)))
            nxt = jnp.pad(x[:, 1:], ((0, 0), (0, 1), (0, 0), (0, 0)))
            return jnp.stack([prev, x, nxt], axis=2)

        def local_attention(q, kv, Wq, Wkv, Wo, w):
            b, L, d_model = q.shape
            d_head = Wkv.shape[1] // 2
            h = d_model // d_head
            nc = L // w
            qp = (q @ Wq).reshape(b, L, h, d_head) / math.sqrt(d_head)
            kvp = kv @ Wkv
            k, v = (kvp[..., :d_head], kvp[..., d_head:])
            cq = qp.reshape(b, nc, w, h, d_head)
            k3 = _neighbor_stack(k.reshape(b, nc, w, d_head))
            v3 = _neighbor_stack(v.reshape(b, nc, w, d_head))
            scores = jnp.einsum('bcxhd,bcpyd->bcxhpy', cq, k3)
            probs = jax.nn.softmax(scores.reshape(b, nc, w, h, 3 * w), axis=-1)
            probs = probs.reshape(b, nc, w, h, 3, w)
            ctx = jnp.einsum('bcxhpy,bcpyd->bcxhd', probs, v3)
            ctx = ctx.reshape(b, L, d_model)
            return ctx @ Wo
        key = jax.random.key(seed)
        k1, k2, k3, k4, k5 = jax.random.split(key, 5)
        b, L, d_model, n_head = (1, 512, 128, 16)
        d_head = d_model // n_head
        scale = 0.02
        return {'q': jax.random.normal(k1, (b, L, d_model), dtype=jnp.float32), 'kv': jax.random.normal(k2, (b, L, d_model), dtype=jnp.float32), 'Wq': jax.random.normal(k3, (d_model, d_model), dtype=jnp.float32) * scale, 'Wkv': jax.random.normal(k4, (d_model, 2 * d_head), dtype=jnp.float32) * scale, 'Wo': jax.random.normal(k5, (d_model, d_model), dtype=jnp.float32) * scale, 'w': 64}
    _L0_xattn_all = _L0_xattn_setup()
    _L0_xattn_in = {k: v for k, v in _L0_xattn_all.items() if k in ('Wq', 'Wkv', 'Wo')}
    del _L0_xattn_all

    def _L0_ffn_setup():
        import jax, jax.numpy as jnp
        import numpy as np
        B, S, D_MODEL, D_HIDDEN = (4, 256, 128, 512)

        def act_quant(x):
            scale = 127.0 / jnp.clip(jnp.max(jnp.abs(x), axis=-1, keepdims=True), 1e-05)
            return jnp.clip(jnp.round(x * scale), -128, 127) / scale

        def weight_quant(w):
            scale = 1.0 / jnp.clip(jnp.mean(jnp.abs(w)), 1e-05)
            return jnp.clip(jnp.round(w * scale), -1, 1) / scale

        def bit_linear(x, w):
            xq = x + jax.lax.stop_gradient(act_quant(x) - x)
            wq = w + jax.lax.stop_gradient(weight_quant(w) - w)
            return jnp.einsum('bsd,hd->bsh', xq, wq)

        def depthwise_conv1d(x_bcl, w, b):
            y = jax.lax.conv_general_dilated(x_bcl, w, window_strides=(1,), padding=[(1, 1)], dimension_numbers=('NCH', 'OIH', 'NCH'), feature_group_count=x_bcl.shape[1])
            return y + b[None, :, None]
        key = jax.random.key(seed)
        ks = jax.random.split(key, 5)
        lim1 = 1.0 / np.sqrt(D_MODEL)
        lim2 = 1.0 / np.sqrt(D_HIDDEN)
        limc = 1.0 / np.sqrt(3.0)
        return {'x': jax.random.normal(ks[0], (B, S, D_MODEL), dtype=jnp.float32), 'w1': jax.random.uniform(ks[1], (D_HIDDEN, D_MODEL), jnp.float32, -lim1, lim1), 'conv_w': jax.random.uniform(ks[2], (D_HIDDEN, 1, 3), jnp.float32, -limc, limc), 'conv_b': jax.random.uniform(ks[3], (D_HIDDEN,), jnp.float32, -limc, limc), 'w2': jax.random.uniform(ks[4], (D_MODEL, D_HIDDEN), jnp.float32, -lim2, lim2)}
    _L0_ffn_all = _L0_ffn_setup()
    _L0_ffn_in = {k: v for k, v in _L0_ffn_all.items() if k in ('w1', 'conv_w', 'conv_b', 'w2')}
    del _L0_ffn_all

    def _L1_attn_setup():
        import jax, jax.numpy as jnp
        import numpy as np
        B, P, D = (8, 128, 128)
        H, N = (16, 64)
        key = jax.random.key(seed)
        k1, k2, k3 = jax.random.split(key, 3)
        inputs = jax.random.normal(k1, (B, P, D), dtype=jnp.float32)
        w_qkv = jax.random.normal(k2, (H, 3, D, N), dtype=jnp.float32) * 0.05
        w_o = jax.random.normal(k3, (N * H, D), dtype=jnp.float32) * 0.05
        return {'inputs': inputs, 'w_qkv': w_qkv, 'w_o': w_o}
    _L1_attn_all = _L1_attn_setup()
    _L1_attn_in = {k: v for k, v in _L1_attn_all.items() if k in ('w_qkv', 'w_o')}
    del _L1_attn_all

    def _L1_xattn_setup():
        import jax, jax.numpy as jnp
        import numpy as np
        D_MODEL = 128
        N_HEADS = 16
        HEAD_DIM = D_MODEL // N_HEADS
        key = jax.random.key(seed)
        k1, k2, k3, k4, k5, k6 = jax.random.split(key, 6)
        B, T_q, T_kv = (4, 128, 512)
        s = 1.0 / np.sqrt(D_MODEL)
        return {'query': jax.random.normal(k1, (B, T_q, D_MODEL), dtype=jnp.float32), 'kv_source': jax.random.normal(k2, (B, T_kv, D_MODEL), dtype=jnp.float32), 'w_q': jax.random.normal(k3, (D_MODEL, D_MODEL), dtype=jnp.float32) * s, 'w_k': jax.random.normal(k4, (D_MODEL, D_MODEL), dtype=jnp.float32) * s, 'w_v': jax.random.normal(k5, (D_MODEL, D_MODEL), dtype=jnp.float32) * s, 'w_o': jax.random.normal(k6, (D_MODEL, D_MODEL), dtype=jnp.float32) * s}
    _L1_xattn_all = _L1_xattn_setup()
    _L1_xattn_in = {k: v for k, v in _L1_xattn_all.items() if k in ('w_q', 'w_k', 'w_v', 'w_o')}
    del _L1_xattn_all

    def _L1_ffn_setup():
        import jax, jax.numpy as jnp
        import numpy as np
        EMBED = 128
        HEADS = 16
        HEAD_DIM = EMBED // HEADS
        NUM_EXPERTS = 8
        TOP_K = 2
        HIDDEN = (int(2 * (4 * EMBED) / 3) + 63) // 64 * 64
        SEQ = 256
        BATCH = 2
        ROPE_BASE = 10000.0
        EPS = 1e-06

        def _rope_tables(seq_len, dim):
            inv_freq = 1.0 / ROPE_BASE ** (np.arange(0, dim, 2, dtype=np.float32) / dim)
            t = np.arange(seq_len, dtype=np.float32)
            freqs = np.einsum('i,j->ij', t, inv_freq)
            emb = np.concatenate([freqs, freqs], axis=-1)
            return (jnp.asarray(np.cos(emb)), jnp.asarray(np.sin(emb)))

        def _rotate_half(x):
            x1, x2 = jnp.split(x, 2, axis=-1)
            return jnp.concatenate([-x2, x1], axis=-1)

        def _rmsnorm(x, w):
            return x * jax.lax.rsqrt(jnp.mean(x * x, axis=-1, keepdims=True) + EPS) * w

        def _attention(x, wq, wk, wv, wo):
            B, S, _ = x.shape
            q = (x @ wq).reshape(B, S, HEADS, HEAD_DIM).transpose(0, 2, 1, 3)
            k = (x @ wk).reshape(B, S, HEADS, HEAD_DIM).transpose(0, 2, 1, 3)
            v = (x @ wv).reshape(B, S, HEADS, HEAD_DIM).transpose(0, 2, 1, 3)
            cos, sin = _rope_tables(S, HEAD_DIM)
            cos = cos[None, None]
            sin = sin[None, None]
            q = q * cos + _rotate_half(q) * sin
            k = k * cos + _rotate_half(k) * sin
            scale = HEAD_DIM ** (-0.5)
            scores = jnp.einsum('bhqd,bhkd->bhqk', q, k) * scale
            causal = jnp.triu(jnp.ones((S, S), bool), k=1)
            scores = jnp.where(causal, -jnp.inf, scores)
            attn = jax.nn.softmax(scores, axis=-1)
            out = jnp.einsum('bhqk,bhkd->bhqd', attn, v)
            out = out.transpose(0, 2, 1, 3).reshape(B, S, EMBED)
            return out @ wo

        def _moe(x, w_router, wg, wu, wd):
            B, S, E = x.shape
            xf = x.reshape(-1, E)
            logits = xf @ w_router
            probs = jax.nn.softmax(logits, axis=-1)
            topw, topi = jax.lax.top_k(probs, TOP_K)
            topw = topw / jnp.sum(topw, axis=-1, keepdims=True)
            combine = jnp.sum(jax.nn.one_hot(topi, NUM_EXPERTS, dtype=xf.dtype) * topw[..., None], axis=1)
            g = jax.nn.silu(jnp.einsum('td,xdh->txh', xf, wg))
            u = jnp.einsum('td,xdh->txh', xf, wu)
            eo = jnp.einsum('txh,xhd->txd', g * u, wd)
            out = jnp.einsum('txd,tx->td', eo, combine)
            return out.reshape(B, S, E)
        key = jax.random.key(seed)
        ks = jax.random.split(key, 12)
        s = 0.02
        return {'x': jax.random.normal(ks[0], (BATCH, SEQ, EMBED), jnp.float32), 'wq': jax.random.normal(ks[1], (EMBED, EMBED), jnp.float32) * s, 'wk': jax.random.normal(ks[2], (EMBED, EMBED), jnp.float32) * s, 'wv': jax.random.normal(ks[3], (EMBED, EMBED), jnp.float32) * s, 'wo': jax.random.normal(ks[4], (EMBED, EMBED), jnp.float32) * s, 'w_router': jax.random.normal(ks[5], (EMBED, NUM_EXPERTS), jnp.float32) * s, 'wg': jax.random.normal(ks[6], (NUM_EXPERTS, EMBED, HIDDEN), jnp.float32) * s, 'wu': jax.random.normal(ks[7], (NUM_EXPERTS, EMBED, HIDDEN), jnp.float32) * s, 'wd': jax.random.normal(ks[8], (NUM_EXPERTS, HIDDEN, EMBED), jnp.float32) * s, 'g1': jnp.ones((EMBED,), jnp.float32), 'g2': jnp.ones((EMBED,), jnp.float32)}
    _L1_ffn_all = _L1_ffn_setup()
    _L1_ffn_in = {k: v for k, v in _L1_ffn_all.items() if k in ('wq', 'wk', 'wv', 'wo', 'w_router', 'wg', 'wu', 'wd', 'g1', 'g2')}
    del _L1_ffn_all
    return {'x': x, 'ctx_1024': ctx_1024, 'L0_attn_qkv_w': _L0_attn_in['qkv_w'], 'L0_attn_qkv_b': _L0_attn_in['qkv_b'], 'L0_attn_out_w': _L0_attn_in['out_w'], 'L0_attn_out_b': _L0_attn_in['out_b'], 'L0_attn_g_attn': _L0_attn_in['g_attn'], 'L0_attn_b_attn': _L0_attn_in['b_attn'], 'L0_attn_g1': _L0_attn_in['g1'], 'L0_attn_b1': _L0_attn_in['b1'], 'L0_attn_g2': _L0_attn_in['g2'], 'L0_attn_b2': _L0_attn_in['b2'], 'L0_attn_w_ctx': _L0_attn_in['w_ctx'], 'L0_attn_w_x': _L0_attn_in['w_x'], 'L0_attn_b_inl': _L0_attn_in['b_inl'], 'L0_attn_ff_w1': _L0_attn_in['ff_w1'], 'L0_attn_ff_b1': _L0_attn_in['ff_b1'], 'L0_attn_ff_w2': _L0_attn_in['ff_w2'], 'L0_attn_ff_b2': _L0_attn_in['ff_b2'], 'L0_xattn_Wq': _L0_xattn_in['Wq'], 'L0_xattn_Wkv': _L0_xattn_in['Wkv'], 'L0_xattn_Wo': _L0_xattn_in['Wo'], 'L0_ffn_w1': _L0_ffn_in['w1'], 'L0_ffn_conv_w': _L0_ffn_in['conv_w'], 'L0_ffn_conv_b': _L0_ffn_in['conv_b'], 'L0_ffn_w2': _L0_ffn_in['w2'], 'L1_attn_w_qkv': _L1_attn_in['w_qkv'], 'L1_attn_w_o': _L1_attn_in['w_o'], 'L1_xattn_w_q': _L1_xattn_in['w_q'], 'L1_xattn_w_k': _L1_xattn_in['w_k'], 'L1_xattn_w_v': _L1_xattn_in['w_v'], 'L1_xattn_w_o': _L1_xattn_in['w_o'], 'L1_ffn_wq': _L1_ffn_in['wq'], 'L1_ffn_wk': _L1_ffn_in['wk'], 'L1_ffn_wv': _L1_ffn_in['wv'], 'L1_ffn_wo': _L1_ffn_in['wo'], 'L1_ffn_w_router': _L1_ffn_in['w_router'], 'L1_ffn_wg': _L1_ffn_in['wg'], 'L1_ffn_wu': _L1_ffn_in['wu'], 'L1_ffn_wd': _L1_ffn_in['wd'], 'L1_ffn_g1': _L1_ffn_in['g1'], 'L1_ffn_g2': _L1_ffn_in['g2']}

def reference(x, ctx_1024, L0_attn_qkv_w, L0_attn_qkv_b, L0_attn_out_w, L0_attn_out_b, L0_attn_g_attn, L0_attn_b_attn, L0_attn_g1, L0_attn_b1, L0_attn_g2, L0_attn_b2, L0_attn_w_ctx, L0_attn_w_x, L0_attn_b_inl, L0_attn_ff_w1, L0_attn_ff_b1, L0_attn_ff_w2, L0_attn_ff_b2, L0_xattn_Wq, L0_xattn_Wkv, L0_xattn_Wo, L0_ffn_w1, L0_ffn_conv_w, L0_ffn_conv_b, L0_ffn_w2, L1_attn_w_qkv, L1_attn_w_o, L1_xattn_w_q, L1_xattn_w_k, L1_xattn_w_v, L1_xattn_w_o, L1_ffn_wq, L1_ffn_wk, L1_ffn_wv, L1_ffn_wo, L1_ffn_w_router, L1_ffn_wg, L1_ffn_wu, L1_ffn_wd, L1_ffn_g1, L1_ffn_g2):
    import jax
    import jax.numpy as jnp

    def _L0_attn_ref(x, qkv_w, qkv_b, out_w, out_b, g_attn, b_attn, g1, b1, g2, b2, w_ctx, w_x, b_inl, ff_w1, ff_b1, ff_w2, ff_b2):
        import jax, jax.numpy as jnp
        import numpy as np
        B, S, D, H = (2, 256, 128, 16)
        HD = D // H
        FF = 512
        NUM_ITERS = 8
        DT = 0.1
        LN_EPS = 1e-05

        def _ln(x, g, b):
            m = jnp.mean(x, axis=-1, keepdims=True)
            v = jnp.var(x, axis=-1, keepdims=True)
            return (x - m) * jax.lax.rsqrt(v + LN_EPS) * g + b

        def _forward(x, qkv_w, qkv_b, out_w, out_b, g_attn, b_attn, g1, b1, g2, b2, w_ctx, w_x, b_inl, ff_w1, ff_b1, ff_w2, ff_b2):
            b, s, d = x.shape
            xn = _ln(x, g_attn, b_attn)
            qkv = (xn @ qkv_w + qkv_b).reshape(b, s, 3, H, HD)
            qkv = jnp.transpose(qkv, (2, 0, 3, 1, 4))
            q, k, v = (qkv[0], qkv[1], qkv[2])
            scores = jnp.einsum('bhqd,bhkd->bhqk', q, k) / np.sqrt(HD).astype(np.float32)
            causal = jnp.triu(jnp.ones((s, s), dtype=bool), 1)
            scores = jnp.where(causal[None, None], -jnp.inf, scores)
            attn_w = jax.nn.softmax(scores, axis=-1)
            attn = jnp.einsum('bhqk,bhkd->bhqd', attn_w, v)
            attn = jnp.transpose(attn, (0, 2, 1, 3)).reshape(b, s, d)
            attn = attn @ out_w + out_b
            x = x + attn
            ctx = attn.reshape(b * s, d)
            xs = _ln(x, g1, b1).reshape(b * s, d)
            vs = jnp.zeros_like(xs)

            def step(carry, _):
                xs, vs = carry
                u = jnp.tanh(ctx @ w_ctx + xs @ w_x + b_inl)
                vn = vs + DT * (u - xs - vs)
                xn_ = xs + DT * vn
                return ((xn_, vn), None)
            (xs, vs), _ = jax.lax.scan(step, (xs, vs), None, length=NUM_ITERS)
            x = x + xs.reshape(b, s, d)
            h = _ln(x, g2, b2)
            h = jax.nn.gelu(h @ ff_w1 + ff_b1, approximate=False)
            x = x + (h @ ff_w2 + ff_b2)
            return x
        return _forward(x, qkv_w, qkv_b, out_w, out_b, g_attn, b_attn, g1, b1, g2, b2, w_ctx, w_x, b_inl, ff_w1, ff_b1, ff_w2, ff_b2)

    def _L0_xattn_ref(q, kv, Wq, Wkv, Wo, w):
        import jax, jax.numpy as jnp
        import numpy as np
        import math

        def _neighbor_stack(x):
            prev = jnp.pad(x[:, :-1], ((0, 0), (1, 0), (0, 0), (0, 0)))
            nxt = jnp.pad(x[:, 1:], ((0, 0), (0, 1), (0, 0), (0, 0)))
            return jnp.stack([prev, x, nxt], axis=2)

        def local_attention(q, kv, Wq, Wkv, Wo, w):
            b, L, d_model = q.shape
            d_head = Wkv.shape[1] // 2
            h = d_model // d_head
            nc = L // w
            qp = (q @ Wq).reshape(b, L, h, d_head) / math.sqrt(d_head)
            kvp = kv @ Wkv
            k, v = (kvp[..., :d_head], kvp[..., d_head:])
            cq = qp.reshape(b, nc, w, h, d_head)
            k3 = _neighbor_stack(k.reshape(b, nc, w, d_head))
            v3 = _neighbor_stack(v.reshape(b, nc, w, d_head))
            scores = jnp.einsum('bcxhd,bcpyd->bcxhpy', cq, k3)
            probs = jax.nn.softmax(scores.reshape(b, nc, w, h, 3 * w), axis=-1)
            probs = probs.reshape(b, nc, w, h, 3, w)
            ctx = jnp.einsum('bcxhpy,bcpyd->bcxhd', probs, v3)
            ctx = ctx.reshape(b, L, d_model)
            return ctx @ Wo
        return local_attention(q, kv, Wq, Wkv, Wo, w)

    def _L0_ffn_ref(x, w1, conv_w, conv_b, w2):
        import jax, jax.numpy as jnp
        import numpy as np
        B, S, D_MODEL, D_HIDDEN = (4, 256, 128, 512)

        def act_quant(x):
            scale = 127.0 / jnp.clip(jnp.max(jnp.abs(x), axis=-1, keepdims=True), 1e-05)
            return jnp.clip(jnp.round(x * scale), -128, 127) / scale

        def weight_quant(w):
            scale = 1.0 / jnp.clip(jnp.mean(jnp.abs(w)), 1e-05)
            return jnp.clip(jnp.round(w * scale), -1, 1) / scale

        def bit_linear(x, w):
            xq = x + jax.lax.stop_gradient(act_quant(x) - x)
            wq = w + jax.lax.stop_gradient(weight_quant(w) - w)
            return jnp.einsum('bsd,hd->bsh', xq, wq)

        def depthwise_conv1d(x_bcl, w, b):
            y = jax.lax.conv_general_dilated(x_bcl, w, window_strides=(1,), padding=[(1, 1)], dimension_numbers=('NCH', 'OIH', 'NCH'), feature_group_count=x_bcl.shape[1])
            return y + b[None, :, None]
        h = bit_linear(x, w1)
        h = depthwise_conv1d(h.transpose(0, 2, 1), conv_w, conv_b)
        h = h.transpose(0, 2, 1)
        h = jax.nn.silu(h)
        return bit_linear(h, w2)

    def _L1_attn_ref(inputs, w_qkv, w_o):
        import jax, jax.numpy as jnp
        import numpy as np
        B, P, D = (8, 128, 128)
        H, N = (16, 64)
        proj = jnp.einsum('bpv,havn->bhapn', inputs, w_qkv)
        q = proj[:, :, 0]
        k = proj[:, :, 1]
        v = proj[:, :, 2]
        head_dim = q.shape[-1]
        scale = 1.0 / jnp.sqrt(jnp.asarray(head_dim, dtype=jnp.float32))
        scores = jnp.einsum('bhqn,bhkn->bhqk', q, k) * scale
        attn = jax.nn.softmax(scores, axis=-1)
        out = jnp.einsum('bhqk,bhkn->bhqn', attn, v)
        b, h, p, n = out.shape
        concat = out.transpose(0, 2, 1, 3).reshape(b, p, h * n)
        return jnp.einsum('bpi,ij->bpj', concat, w_o)

    def _L1_xattn_ref(query, kv_source, w_q, w_k, w_v, w_o):
        import jax, jax.numpy as jnp
        import numpy as np
        D_MODEL = 128
        N_HEADS = 16
        HEAD_DIM = D_MODEL // N_HEADS
        B, T_q, _ = query.shape
        T_kv = kv_source.shape[1]
        q = (query @ w_q.T).reshape(B, T_q, N_HEADS, HEAD_DIM)
        k = (kv_source @ w_k.T).reshape(B, T_kv, N_HEADS, HEAD_DIM)
        v = (kv_source @ w_v.T).reshape(B, T_kv, N_HEADS, HEAD_DIM)
        scale = HEAD_DIM ** (-0.5)
        attn = jax.nn.softmax(jnp.einsum('bqhd,bkhd->bhqk', q, k) * scale, axis=-1)
        out = jnp.einsum('bhqk,bkhd->bqhd', attn, v).reshape(B, T_q, D_MODEL)
        return out @ w_o.T

    def _L1_ffn_ref(x, wq, wk, wv, wo, w_router, wg, wu, wd, g1, g2):
        import jax, jax.numpy as jnp
        import numpy as np
        EMBED = 128
        HEADS = 16
        HEAD_DIM = EMBED // HEADS
        NUM_EXPERTS = 8
        TOP_K = 2
        HIDDEN = (int(2 * (4 * EMBED) / 3) + 63) // 64 * 64
        SEQ = 256
        BATCH = 2
        ROPE_BASE = 10000.0
        EPS = 1e-06

        def _rope_tables(seq_len, dim):
            inv_freq = 1.0 / ROPE_BASE ** (np.arange(0, dim, 2, dtype=np.float32) / dim)
            t = np.arange(seq_len, dtype=np.float32)
            freqs = np.einsum('i,j->ij', t, inv_freq)
            emb = np.concatenate([freqs, freqs], axis=-1)
            return (jnp.asarray(np.cos(emb)), jnp.asarray(np.sin(emb)))

        def _rotate_half(x):
            x1, x2 = jnp.split(x, 2, axis=-1)
            return jnp.concatenate([-x2, x1], axis=-1)

        def _rmsnorm(x, w):
            return x * jax.lax.rsqrt(jnp.mean(x * x, axis=-1, keepdims=True) + EPS) * w

        def _attention(x, wq, wk, wv, wo):
            B, S, _ = x.shape
            q = (x @ wq).reshape(B, S, HEADS, HEAD_DIM).transpose(0, 2, 1, 3)
            k = (x @ wk).reshape(B, S, HEADS, HEAD_DIM).transpose(0, 2, 1, 3)
            v = (x @ wv).reshape(B, S, HEADS, HEAD_DIM).transpose(0, 2, 1, 3)
            cos, sin = _rope_tables(S, HEAD_DIM)
            cos = cos[None, None]
            sin = sin[None, None]
            q = q * cos + _rotate_half(q) * sin
            k = k * cos + _rotate_half(k) * sin
            scale = HEAD_DIM ** (-0.5)
            scores = jnp.einsum('bhqd,bhkd->bhqk', q, k) * scale
            causal = jnp.triu(jnp.ones((S, S), bool), k=1)
            scores = jnp.where(causal, -jnp.inf, scores)
            attn = jax.nn.softmax(scores, axis=-1)
            out = jnp.einsum('bhqk,bhkd->bhqd', attn, v)
            out = out.transpose(0, 2, 1, 3).reshape(B, S, EMBED)
            return out @ wo

        def _moe(x, w_router, wg, wu, wd):
            B, S, E = x.shape
            xf = x.reshape(-1, E)
            logits = xf @ w_router
            probs = jax.nn.softmax(logits, axis=-1)
            topw, topi = jax.lax.top_k(probs, TOP_K)
            topw = topw / jnp.sum(topw, axis=-1, keepdims=True)
            combine = jnp.sum(jax.nn.one_hot(topi, NUM_EXPERTS, dtype=xf.dtype) * topw[..., None], axis=1)
            g = jax.nn.silu(jnp.einsum('td,xdh->txh', xf, wg))
            u = jnp.einsum('td,xdh->txh', xf, wu)
            eo = jnp.einsum('txh,xhd->txd', g * u, wd)
            out = jnp.einsum('txd,tx->td', eo, combine)
            return out.reshape(B, S, E)
        h = x + _attention(_rmsnorm(x, g1), wq, wk, wv, wo)
        y = h + _moe(_rmsnorm(h, g2), w_router, wg, wu, wd)
        return y
    x = _layernorm(x + _L0_attn_ref(x, L0_attn_qkv_w, L0_attn_qkv_b, L0_attn_out_w, L0_attn_out_b, L0_attn_g_attn, L0_attn_b_attn, L0_attn_g1, L0_attn_b1, L0_attn_g2, L0_attn_b2, L0_attn_w_ctx, L0_attn_w_x, L0_attn_b_inl, L0_attn_ff_w1, L0_attn_ff_b1, L0_attn_ff_w2, L0_attn_ff_b2), axis=-1)
    x = _layernorm(x + _L0_xattn_ref(x, ctx_1024, L0_xattn_Wq, L0_xattn_Wkv, L0_xattn_Wo, 64), axis=-1)
    x = _layernorm(x + _L0_ffn_ref(x, L0_ffn_w1, L0_ffn_conv_w, L0_ffn_conv_b, L0_ffn_w2), axis=-1)
    x = _layernorm(x + _L1_attn_ref(x, L1_attn_w_qkv, L1_attn_w_o), axis=-1)
    x = _layernorm(x + _L1_xattn_ref(x, ctx_1024, L1_xattn_w_q, L1_xattn_w_k, L1_xattn_w_v, L1_xattn_w_o), axis=-1)
    x = _layernorm(x + _L1_ffn_ref(x, L1_ffn_wq, L1_ffn_wk, L1_ffn_wv, L1_ffn_wo, L1_ffn_w_router, L1_ffn_wg, L1_ffn_wu, L1_ffn_wd, L1_ffn_g1, L1_ffn_g2), axis=-1)
    return x

_drawn_inputs = setup_inputs


def setup_inputs(seed=0):
    import zlib

    import numpy as np

    out = dict(_drawn_inputs(seed))
    spreads = {'L0_attn_qkv_b': (0.0, 0.1),
     'L0_attn_out_b': (0.0, 0.1),
     'L0_attn_g_attn': (1.0, 0.2),
     'L0_attn_b_attn': (0.0, 0.1),
     'L0_attn_g1': (1.0, 0.2),
     'L0_attn_b1': (0.0, 0.1),
     'L0_attn_g2': (1.0, 0.2),
     'L0_attn_b2': (0.0, 0.391),
     'L0_attn_b_inl': (0.0, 0.8),
     'L0_attn_ff_b1': (0.0, 0.1),
     'L0_attn_ff_b2': (0.0, 0.1),
     'L1_ffn_g1': (1.0, 0.6),
     'L1_ffn_g2': (1.0, 0.6)}
    factors = {'L0_attn_w_ctx': 2.935,
     'L0_xattn_Wq': 8.0,
     'L0_xattn_Wkv': 5.947,
     'L0_xattn_Wo': 5.364,
     'L1_ffn_wq': 8.0,
     'L1_ffn_wk': 8.0,
     'L1_ffn_wv': 3.849,
     'L1_ffn_wo': 3.849,
     'L1_ffn_w_router': 8.0,
     'L1_ffn_wg': 8.0,
     'L1_ffn_wu': 8.0,
     'L1_ffn_wd': 8.0}
    for name, (base, spread) in spreads.items():
        noise = np.random.default_rng([zlib.crc32(name.encode()), seed]).standard_normal(out[name].shape)
        drawn = base * np.exp(spread * noise) if base else spread * noise
        out[name] = jnp.asarray(drawn.astype(out[name].dtype))
    for name, factor in factors.items():
        out[name] = (out[name] * factor).astype(out[name].dtype)
    return out
```

```python
from contextlib import ExitStack, contextmanager

import numpy as np

import concourse.bass as bass
from concourse import mybir

F32 = mybir.dt.float32
BF16 = mybir.dt.bfloat16
U32 = mybir.dt.uint32
ALU = mybir.AluOpType
ACT = mybir.ActivationFunctionType
AX = mybir.AxisListType.X

P = 128
B, S, D = 16, 64, 128
NTOK = B * S
NT = NTOK // P
HALF = NTOK // 2
TH = NT // 2
H, HD = 16, 8
FF = 512
NC = FF // P
NP1, N1 = 8, 64
NE, HID = 8, 384
HC = HID // P
NPAR = 14 + 2 * NC
ROUND = 1.5 * 2.0**23
MASKED = -1e30


class Chip:

    def __init__(self, nc, stack):
        self.nc, self.stack, self.buf = nc, stack, {}
        self.current, self.past, self.stage = [], [], 0

    def sb(self, name, shape, dt=F32):
        self.buf[name] = self.stack.enter_context(self.nc.sbuf_tensor(name, [P, *shape], dt))
        return self.buf[name]

    def __getitem__(self, name):
        return self.buf[name]


def stage_semaphores(nc, ch, *names):
    sems = [nc.alloc_semaphore(f"{n}_{ch.stage}") for n in names]
    ch.current += sems
    return sems


@contextmanager
def stage_block(nc, ch):
    if ch.past:
        nc.clear_and_free_semaphores(ch.past)
    with nc.Block() as block:
        yield block
    ch.past, ch.current = ch.current, []
    ch.stage += 1


def tile_cols(t, n=P):
    return bass.ds(t * n, n)


def load_inputs(nc, ch, ins, cst):
    def line(v):
        return v.rearrange("(a n) -> a n", a=1)

    def row(v):
        return v.rearrange("(a n) -> a n", a=1).to_broadcast([P, v.shape[0]])

    prow = ch["prow"]
    plain = [
        (ch["X"][:, :, :], ins["x"].rearrange("(t b) s d -> (b s) t d", b=2)),
        (ch["identf"][:, :], cst["identf"]),
        (ch["A"][:, :, :], ins["ctx_1024"].rearrange("(t b) s d -> (b s) t d", b=2)),
        (ch["causalf"][:, :], cst["causal"]), (ch["head_of"][:, :], cst["head_of"]),
        (ch["cos"][:, :], cst["cos"]), (ch["sin"][:, :], cst["sin"]),
        (ch["wqkv0"][:, :], ins["L0_attn_qkv_w"]), (ch["wo0"][:, :], ins["L0_attn_out_w"]),
        (ch["wctx"][:, :], ins["L0_attn_w_ctx"]), (ch["wx"][:, :], ins["L0_attn_w_x"]),
        (ch["ffw1"][:, :], ins["L0_attn_ff_w1"]),
        (ch["ffw2"][:, :, :], ins["L0_attn_ff_w2"].rearrange("(c p) d -> p c d", p=P)),
        (ch["xwq"][:, :], ins["L0_xattn_Wq"]), (ch["xwkv"][:, :], ins["L0_xattn_Wkv"]),
        (ch["xwo"][:, :], ins["L0_xattn_Wo"]),
        (ch["bw1"][:, :, :], ins["L0_ffn_w1"].rearrange("(c p) d -> p c d", p=P)),
        (ch["bw2"][:, :], ins["L0_ffn_w2"]),
        (ch["convw"][:, :, :], ins["L0_ffn_conv_w"].rearrange("(c p) a k -> p c (a k)", p=P)),
        (ch["ywo"][:, 0, :], ins["L1_xattn_w_q"]), (ch["ywo"][:, 1, :], ins["L1_xattn_w_k"]),
        (ch["ywo"][:, 2, :], ins["L1_xattn_w_v"]), (ch["ywo"][:, 3, :], ins["L1_xattn_w_o"]),
        (ch["mwq"][:, :], ins["L1_ffn_wq"]), (ch["mwk"][:, :], ins["L1_ffn_wk"]),
        (ch["mwv"][:, :], ins["L1_ffn_wv"]), (ch["mwo"][:, :], ins["L1_ffn_wo"]),
        (ch["wrout"][:, :], ins["L1_ffn_w_router"]),
        (ch["iota8"][:, :], cst["iota8"]),
        (ch["rows"][:, 0, :], row(ins["L0_attn_qkv_b"][2 * D:3 * D])),
        (ch["rows"][:, 1, :], row(ins["L0_attn_out_b"])),
        (ch["rows"][:, 2, :], row(ins["L0_attn_ff_b2"])),
    ]
    for n, name in enumerate(["L0_attn_g_attn", "L0_attn_b_attn", "L0_attn_g1", "L0_attn_b1", "L0_attn_g2",
                              "L0_attn_b2", "L0_attn_b_inl", "L0_attn_out_b", "L1_ffn_g1", "L1_ffn_g2"]):
        plain.append((prow[n:n + 1, :], line(ins[name])))
    for n in range(4):
        for b in range(2):
            plain.append((prow[10 + n:11 + n, 64 * b:64 * b + 64], line(ins["L0_attn_qkv_b"][64 * n:64 * n + 64])))
    plain.append((prow[14:14 + NC, :], ins["L0_attn_ff_b1"].rearrange("(c p) -> c p", p=P)))
    plain.append((prow[14 + NC:NPAR, :], ins["L0_ffn_conv_b"].rearrange("(c p) -> c p", p=P)))
    with ExitStack() as st:
        loaded, small_done, absum_done, total_done, scaled, ternary, turned, kept, ctx_turned, ones_set = stage_semaphores(
            nc, ch, "loaded", "small_done", "absum_done", "total_done", "scaled", "ternary", "turned", "kept",
            "ctx_turned", "ones_set")
        psum = ch["psum"]
        block = st.enter_context(stage_block(nc, ch))
        all_loaded = 16 * len(plain)

        @block.sync
        def _(sp):
            for dst, src in plain[0::2]:
                sp.dma_start(dst, src).then_inc(loaded, 16)

        @block.gpsimd
        def _(pool):
            pool.memset(ch["minus_half"][:, :], -0.5).then_inc(small_done, 1)
            pool.memset(ch["Qd"][:, :, :, :], 0.0).then_inc(small_done, 1)
            pool.memset(ch["Vd"][:, :, :, :, :], 0.0).then_inc(small_done, 1)
            pool.wait_ge(small_done, 3)
            pool.wait_ge(loaded, all_loaded)
            for m in range(2):
                pool.tensor_copy(ch["xwkr"][:, m, :].rearrange("p (h d) -> p h d", d=HD),
                                 ch["xwkv"][:, m * HD:(m + 1) * HD].unsqueeze(1).to_broadcast([P, H, HD]))\
                    .then_inc(small_done, 1)
            for m, w in enumerate(("mwq", "mwk")):
                src = ch[w][:, :].rearrange("p (h r d) -> p h r d", r=2, d=HD // 2)
                dst = ch["mrot"][:, m, :].rearrange("p (h r d) -> p h r d", r=2, d=HD // 2)
                pool.tensor_scalar(dst[:, :, 0, :], src[:, :, 1, :], -1.0, None, ALU.mult).then_inc(small_done, 1)
                pool.tensor_copy(dst[:, :, 1, :], src[:, :, 0, :]).then_inc(small_done, 1)
            pool.wait_ge(small_done, 9)
            pool.tensor_copy(ch["identb"][:, :], ch["identf"][:, :]).then_inc(small_done, 1)
            pool.tensor_copy(ch["causal"][:, :], ch["causalf"][:, :]).then_inc(small_done, 1)
            pool.wait_ge(small_done, 11)

        @block.scalar
        def _(act):
            for dst, src in plain[1::2]:
                act.dma_start(dst, src).then_inc(loaded, 16)
            for half in range(2):
                act.wait_ge(ctx_turned, half + 1)
                act.activation(ch["CT"][:, half * HALF:(half + 1) * HALF], psum[:, half, :], ACT.Copy).then_inc(kept, 1)
            act.wait_ge(ctx_turned, 3)
            act.activation(ch["yw"][:, :], psum[:, 2, :], ACT.Copy).then_inc(kept, 1)
            act.wait_ge(ctx_turned, 4)
            act.activation(ch["params"][:, :], psum[:, 6, 0:NPAR], ACT.Copy).then_inc(kept, 1)
            act.wait_ge(kept, 4)

        @block.vector
        def _(dve):
            dve.memset(ch["ones"][:, :], 1.0).then_inc(ones_set, 1)
            dve.wait_ge(loaded, all_loaded)
            dve.tensor_reduce(ch["absum"][:, 0:1], ch["bw1"][:, :, :].rearrange("p c d -> p (c d)"), AX, ALU.add,
                              apply_absolute_value=True).then_inc(absum_done, 1)
            dve.tensor_reduce(ch["absum"][:, 1:2], ch["bw2"][:, :], AX, ALU.add,
                              apply_absolute_value=True).then_inc(absum_done, 1)
            dve.wait_ge(total_done, 1)
            dve.tensor_scalar(ch["wmean"][:, :], psum[:, 3, 0:2], 1.0 / (FF * D), 1e-5, ALU.mult, ALU.max)\
                .then_inc(scaled, 1)
            dve.wait_ge(scaled, 1)
            dve.reciprocal(ch["winv"][:, :], ch["wmean"][:, :]).then_inc(scaled, 1)
            dve.wait_ge(scaled, 2)
            for m, w in enumerate((ch["bw1"][:, :, :].rearrange("p c d -> p (c d)"), ch["bw2"][:, :])):
                dve.tensor_scalar(w, w, ch["winv"][:, m:m + 1], ROUND, ALU.mult, ALU.add).then_inc(scaled, 1)
                dve.wait_ge(scaled, 3 + 2 * m)
                dve.tensor_scalar(w, w, -ROUND, 1.0, ALU.add, ALU.min).then_inc(scaled, 1)
                dve.wait_ge(scaled, 4 + 2 * m)
                dve.tensor_scalar(ch["wtern"][:, m, :], w, -1.0, None, ALU.max).then_inc(ternary, 1)
            dve.wait_ge(turned, 1)
            for m in range(2):
                dve.tensor_copy(ch["wternT"][:, m, :], psum[:, 4 + m, 0:FF // 2].bitcast(BF16)).then_inc(ternary, 1)
            dve.wait_ge(ternary, 4)

        @block.tensor
        def _(pe):
            pe.wait_ge(loaded, all_loaded)
            for half in range(2):
                for i in range(TH):
                    mm = pe.transpose(psum[:, half, i * P:(i + 1) * P], ch["A"][:, half * TH + i, :], ch["identf"][:, :])
                mm.then_inc(ctx_turned, 1)
            for i in range(4):
                mm = pe.transpose(psum[:, 2, i * P:(i + 1) * P], ch["ywo"][:, i, :], ch["identf"][:, :])
            mm.then_inc(ctx_turned, 1)
            pe.transpose(psum[:, 6, 0:NPAR], prow[0:NPAR, :], ch["identf"][0:NPAR, 0:NPAR]).then_inc(ctx_turned, 1)
            pe.wait_ge(absum_done, 2)
            pe.wait_ge(ones_set, 1)
            pe.matmul(psum[:, 3, 0:2], ch["ones"][:, :], ch["absum"][:, :], start=True, stop=True).then_inc(total_done, 1)
            pe.wait_ge(ternary, 2)
            pe.wait_ge(small_done, 10)
            for m in range(2):
                for c in range(NC):
                    mm = pe.transpose(psum[:, 4 + m, c * 64:(c + 1) * 64].bitcast(BF16),
                                      ch["wtern"][:, m, c * P:(c + 1) * P], ch["identb"][:, :])
            mm.then_inc(turned, 1)


def norm(nc, ch, src, dst, featT=None, gain=None, shift=None, eps=1e-5, rms=False, out=None):
    psum, par = ch["psum"], ch["params"]
    mv, rstd, var = ch["mv"], ch["rstd"], ch["var"]
    with ExitStack() as st:
        stats_done, agg_done, var_done, root_done, normed, turned, stored = stage_semaphores(
            nc, ch, "stats_done", "agg_done", "var_done", "root_done", "normed", "turned", "stored")
        block = st.enter_context(stage_block(nc, ch))

        @block.vector
        def _(dve):
            for t in range(NT):
                dve.bn_stats(ch["stats"][:, t, :], src[:, t, :]).then_inc(stats_done, 1)
            for t in range(NT):
                dve.wait_ge(stats_done, t + 1)
                dve.bn_aggr(mv[:, t, :], ch["stats"][:, t, :]).then_inc(agg_done, 1)
            dve.wait_ge(agg_done, NT)
            if rms:
                dve.tensor_tensor(var[:, :], mv[:, :, 0], mv[:, :, 0], ALU.mult).then_inc(var_done, 1)
                dve.wait_ge(var_done, 1)
                dve.scalar_tensor_tensor(out=var[:, :], in0=var[:, :], scalar=eps, in1=mv[:, :, 1], op0=ALU.add,
                                         op1=ALU.add).then_inc(var_done, 1)
            else:
                dve.tensor_scalar(var[:, :], mv[:, :, 1], eps, None, ALU.add).then_inc(var_done, 2)
            dve.wait_ge(root_done, 1)
            for t in range(NT):
                if rms:
                    dve.tensor_scalar(dst[:, t, :], src[:, t, :], rstd[:, t:t + 1], None, ALU.mult).then_inc(normed, 1)
                else:
                    dve.tensor_scalar(dst[:, t, :], src[:, t, :], mv[:, t, 0:1], rstd[:, t:t + 1], ALU.subtract,
                                      ALU.mult).then_inc(normed, 1)
            dve.wait_ge(normed, NT)

        @block.gpsimd
        def _(pool):
            pool.wait_ge(var_done, 2)
            pool.tensor_tensor(rstd[:, :], var[:, :], ch["minus_half"][:, :], ALU.pow).then_inc(root_done, 1)

        if featT is not None:
            @block.tensor
            def _(pe):
                for half in range(2):
                    for i in range(TH):
                        t = half * TH + i
                        pe.wait_ge(normed, t + 1)
                        mm = pe.transpose(psum[:, half, i * P:(i + 1) * P], dst[:, t, :], ch["identf"][:, :])
                    mm.then_inc(turned, 1)

            @block.scalar
            def _(act):
                for half in range(2):
                    act.wait_ge(turned, half + 1)
                    cols = featT[:, half * HALF:(half + 1) * HALF]
                    scale = par[:, gain:gain + 1] if gain is not None else 1.0
                    bias = par[:, shift:shift + 1] if shift is not None else 0.0
                    act.activation(cols, psum[:, half, :], ACT.Identity, scale=scale, bias=bias).then_inc(stored, 1)
                act.wait_ge(stored, 2)

        if out is not None:
            @block.sync
            def _(sp):
                rows = out.rearrange("(t b) s d -> (b s) t d", b=2)
                for half in range(2):
                    sp.wait_ge(normed, TH * (half + 1))
                    sp.dma_start(rows[:, half * TH:(half + 1) * TH, :], dst[:, half * TH:(half + 1) * TH, :])\
                        .then_inc(stored, 16)
                sp.wait_ge(stored, 32)


def small_qkv(nc, ch, wq, wk, wv, srcq, srckv, bias=False, rotated=None):
    psum, par = ch["psum"], ch["params"]
    QK = (ch["QP"], ch["KP"])

    def packed(src, b):
        return src[:, :].rearrange("p (t b s) -> p b t s", b=2, s=S)[:, b]

    with ExitStack() as st:
        qk_done, qk_kept, v_done, v_kept, rot_done, rot_kept, mixed, mixed_k = stage_semaphores(
            nc, ch, "qk_done", "qk_kept", "v_done", "v_kept", "rot_done", "rot_kept", "mixed", "mixed_k")
        block = st.enter_context(stage_block(nc, ch))

        def four(pe, weights, done, free=None):
            for m in range(2):
                src = srcq if m == 0 else srckv
                for half in range(2):
                    if free is not None:
                        pe.wait_ge(free, 2 * m + half + 1)
                    for b in range(2):
                        mm = pe.matmul(psum[64 * b:64 * b + 64, 2 * m + half, :],
                                       weights[m][:, 64 * half:64 * half + 64], packed(src, b), start=True, stop=True)
                    mm.then_inc(done, 1)

        @block.tensor
        def _(pe):
            four(pe, (wq, wk), qk_done)
            for half in range(2):
                for i in range(TH):
                    mm = pe.matmul(psum[:, 4 + half, i * P:(i + 1) * P], srckv[:, tile_cols(half * TH + i)], wv,
                                   start=True, stop=True)
                mm.then_inc(v_done, 1)
            if rotated is not None:
                four(pe, rotated, rot_done, qk_kept)

        @block.scalar
        def _(act):
            for n in range(4):
                act.wait_ge(qk_done, n + 1)
                act.activation(QK[n // 2][:, n % 2, :], psum[:, n, :], ACT.Identity,
                               bias=par[:, 10 + n:11 + n] if bias else 0.0).then_inc(qk_kept, 1)
            if rotated is not None:
                for n in range(4):
                    act.wait_ge(rot_done, n + 1)
                    act.activation(ch["rot"][:, n, :], psum[:, n, :], ACT.Copy).then_inc(rot_kept, 1)
                act.wait_ge(rot_kept, 4)
            act.wait_ge(qk_kept, 4)

        @block.vector
        def _(dve):
            for half in range(2):
                dve.wait_ge(v_done, half + 1)
                v = ch["V"][:, half * TH:(half + 1) * TH, :]
                p = psum[:, 4 + half, :].rearrange("p (t d) -> p t d", d=D)
                if bias:
                    dve.tensor_tensor(v, p, ch["rows"][:, 0, :].unsqueeze(1).to_broadcast([P, TH, D]), ALU.add)\
                        .then_inc(v_kept, 1)
                else:
                    dve.tensor_copy(v, p).then_inc(v_kept, 1)
            if rotated is not None:
                for n in range(4):
                    x = QK[n // 2][:, n % 2, :].rearrange("p (t s) -> p t s", s=S)
                    r = ch["rot"][:, n, :].rearrange("p (t s) -> p t s", s=S)
                    dve.wait_ge(qk_kept, n + 1)
                    dve.tensor_tensor(x, x, ch["cos"][:, :].unsqueeze(1).to_broadcast([P, NT, S]), ALU.mult)\
                        .then_inc(mixed, 1)
                    dve.wait_ge(mixed_k, n + 1)
                    dve.wait_ge(mixed, 2 * n + 1)
                    dve.tensor_tensor(x, x, r, ALU.add).then_inc(mixed, 1)
                dve.wait_ge(mixed, 8)
            dve.wait_ge(v_kept, 2)

        if rotated is not None:
            @block.gpsimd
            def _(pool):
                for n in range(4):
                    r = ch["rot"][:, n, :].rearrange("p (t s) -> p t s", s=S)
                    pool.wait_ge(rot_kept, n + 1)
                    pool.tensor_tensor(r, r, ch["sin"][:, :].unsqueeze(1).to_broadcast([P, NT, S]), ALU.mult)\
                        .then_inc(mixed_k, 1)


def small_attention(nc, ch, causal=False, zero_keys=0):
    psum = ch["psum"]
    scale = float(HD) ** -0.5
    Qd, Kx, Vd, Pr, PT, mx, den, rden = (ch[n] for n in ("Qd", "Kx", "Vd", "Pr", "PT", "mx", "den", "rden"))
    pad, AT = ch["pad"], ch["AT"]
    with ExitStack() as st:
        (keys_spread, query_placed, scores_done, max_done, pad_max, centred, exp_done, pad_done, sum_done, sum_pad,
         inverse_done, probs_done, turned, turned_kept, values_placed, pv_done, out_kept) = stage_semaphores(
            nc, ch, "keys_spread", "query_placed", "scores_done", "max_done", "pad_max", "centred", "exp_done",
            "pad_done", "sum_done", "sum_pad", "inverse_done", "probs_done", "turned", "turned_kept",
            "values_placed", "pv_done", "out_kept")
        block = st.enter_context(stage_block(nc, ch))

        def pairs(eng, before, step, last):
            before()
            with eng.Fori(0, NT // 2 - 1) as i:
                step(2 * i, 0, True, True)
                step(2 * i + 1, 1, True, True)
            step(NT - 2, 0, True, False)
            step(NT - 1, 1, False, False)
            last()

        @block.gpsimd
        def _(pool):
            def spread_keys(t, s):
                pool.wait_ge(scores_done, t + 1)
                k = ch["KP"][:, :, tile_cols(t, S)]
                pool.tensor_tensor(Kx[:, s, :, :, :], k.unsqueeze(2).to_broadcast([P, 2, 8, S]),
                                   ch["head_of"][:, :].unsqueeze(1).unsqueeze(3).to_broadcast([P, 2, 8, S]),
                                   ALU.mult).then_inc(keys_spread, 1)

            def normalise(t, s):
                pool.wait_ge(inverse_done, t + 1)
                pool.tensor_tensor(Pr[:, s, :, :], Pr[:, s, :, :],
                                   rden[:, s, :].unsqueeze(2).to_broadcast([P, H, S]), ALU.mult)\
                    .then_inc(probs_done, 1)

            def before():
                spread_keys(0, 0)
                spread_keys(1, 1)

            def step(t, s, one, two):
                normalise(t, s)
                if two:
                    spread_keys(t + 2, s)

            pairs(pool, before, step, lambda: None)

        @block.scalar
        def _(act):
            def place_query(t, s):
                act.wait_ge(scores_done, t + 1)
                for b in range(2):
                    rows = slice(64 * b, 64 * b + 64)
                    act.activation(Qd[rows, s, :, 64 * b:64 * b + 64], ch["QP"][rows, :, tile_cols(t, S)], ACT.Copy)\
                        .then_inc(query_placed, 1)

            def place_values(t, s):
                act.wait_ge(pv_done, t + 1)
                for b in range(2):
                    for odd in range(2):
                        src = ch["V"][64 * b:64 * b + 64, bass.ds(t, 1), :].rearrange(
                            "p a (g m o d) -> p (a g) m o d", g=4, m=2, o=2)[:, :, :, odd, :]
                        dst = Vd[64 * odd:64 * odd + 64, s, b, :, :].rearrange("p g (a d) -> p g a d", d=HD)
                        act.activation(dst[:, :, odd:odd + 7:6, :], src, ACT.Copy).then_inc(values_placed, 1)

            def exponentials(t, s):
                act.wait_ge(centred, t + 3)
                act.activation(Pr[:, s, :, :], Pr[:, s, :, :], ACT.Exp, scale=scale).then_inc(exp_done, 1)
                if zero_keys:
                    act.activation(pad[:, s, :], mx[:, s, :], ACT.Exp, scale=-scale).then_inc(pad_done, 1)

            def keep_turned(t, s):
                act.wait_ge(turned, t + 3)
                act.wait_ge(pv_done, t + 1)
                for m in range(2):
                    act.activation(PT[:, s, 4 * m:4 * m + 4, :].rearrange("p h q -> p (h q)"), psum[:, 4 + m, :],
                                   ACT.Copy).then_inc(turned_kept, 1)

            def keep_out(t, s):
                act.wait_ge(pv_done, t + 3)
                act.activation(AT[:, tile_cols(t)], psum[:, 6 + s, 0:P], ACT.Copy).then_inc(out_kept, 1)

            def before():
                act.sem_inc(out_kept, 2)
                act.sem_inc(turned_kept, 2)
                for t in range(2):
                    place_query(t, t)
                    place_values(t, t)
                exponentials(0, 0)

            def step(t, s, one, two):
                if one:
                    exponentials(t + 1, 1 - s)
                keep_turned(t, s)
                if two:
                    place_query(t + 2, s)
                keep_out(t, s)
                if two:
                    place_values(t + 2, s)

            pairs(act, before, step, lambda: act.wait_ge(out_kept, NT + 2))

        @block.vector
        def _(dve):
            def centre(t, s):
                dve.wait_ge(scores_done, t + 3)
                sc = psum[:, 2 * s:2 * s + 2, :].rearrange("p a (h k) -> p (a h) k", k=S)
                dve.tensor_reduce(mx[:, s, :], sc, AX, ALU.max).then_inc(max_done, 1)
                dve.wait_ge(max_done, t + 1)
                if zero_keys:
                    dve.tensor_scalar(mx[:, s, :], mx[:, s, :], 0.0, None, ALU.max).then_inc(pad_max, 1)
                    dve.wait_ge(pad_max, t + 1)
                dve.wait_ge(turned, t + 1)
                dve.tensor_tensor(Pr[:, s, :, :], sc, mx[:, s, :].unsqueeze(2).to_broadcast([P, H, S]),
                                  ALU.subtract).then_inc(centred, 1)

            def invert(t, s):
                dve.wait_ge(exp_done, t + 1)
                dve.tensor_reduce(den[:, s, :], Pr[:, s, :, :], AX, ALU.add).then_inc(sum_done, 1)
                dve.wait_ge(sum_done, t + 1)
                if zero_keys:
                    dve.wait_ge(pad_done, t + 1)
                    dve.scalar_tensor_tensor(out=den[:, s, :], in0=pad[:, s, :], scalar=float(zero_keys),
                                             in1=den[:, s, :], op0=ALU.mult, op1=ALU.add).then_inc(sum_pad, 1)
                    dve.wait_ge(sum_pad, t + 1)
                dve.reciprocal(rden[:, s, :], den[:, s, :]).then_inc(inverse_done, 1)

            def step(t, s, one, two):
                if one:
                    centre(t + 1, 1 - s)
                invert(t, s)

            def before():
                dve.sem_inc(centred, 2)
                centre(0, 0)

            pairs(dve, before, step, lambda: None)

        @block.tensor
        def _(pe):
            def scores(t, s):
                pe.wait_ge(keys_spread, t + 1)
                pe.wait_ge(query_placed, 2 * t + 2)
                pe.wait_ge(centred, t + 1)
                for half in range(2):
                    bank = psum[:, 2 * s + half, :]
                    if causal:
                        pe.matmul(bank, ch["identb"][:, :], ch["causal"][:, :].unsqueeze(1).to_broadcast([P, 8, S]),
                                  start=True, stop=False)
                    mm = pe.matmul(bank, Qd[:, s, half, :], Kx[:, s, half, :, :].rearrange("p h k -> p (h k)"),
                                   start=not causal, stop=True)
                mm.then_inc(scores_done, 1)

            def turn(t, s):
                pe.wait_ge(probs_done, t + 1)
                pe.wait_ge(turned_kept, 2 * t + 2)
                for hp in range(8):
                    mm = pe.transpose(psum[:, 4 + hp // 4, (hp % 4) * P:(hp % 4 + 1) * P],
                                      Pr[:, s, 2 * hp:2 * hp + 2, :].rearrange("p h k -> p (h k)"), ch["identf"][:, :])
                mm.then_inc(turned, 1)

            def values(t, s):
                pe.wait_ge(turned_kept, 2 * t + 4)
                pe.wait_ge(values_placed, 4 * t + 4)
                pe.wait_ge(out_kept, t + 1)
                for b in range(2):
                    for m in range(2):
                        for g in range(4):
                            mm = pe.matmul(psum[32 * g:32 * g + 32, 6 + s, 64 * b:64 * b + 64], Vd[:, s, b, g, 32 * m:32 * m + 32],
                                           PT[:, s, 2 * g + m, 64 * b:64 * b + 64], start=(m == 0), stop=(m == 1))
                mm.then_inc(pv_done, 1)

            def before():
                pe.sem_inc(scores_done, 2)
                pe.sem_inc(pv_done, 2)
                pe.sem_inc(turned, 2)
                scores(0, 0)
                scores(1, 1)

            def step(t, s, one, two):
                turn(t, s)
                if two:
                    scores(t + 2, s)
                values(t, s)

            pairs(pe, before, step, lambda: None)


def project_add(nc, ch, wo, dst, adds, featT=None, feat_bias=None):
    psum, AT = ch["psum"], ch["AT"]
    with ExitStack() as st:
        proj_done, added, feat_done, feat_kept = stage_semaphores(nc, ch, "proj_done", "added", "feat_done",
                                                                  "feat_kept")
        block = st.enter_context(stage_block(nc, ch))

        @block.tensor
        def _(pe):
            for half in range(2):
                for i in range(TH):
                    mm = pe.matmul(psum[:, half, i * P:(i + 1) * P], AT[:, tile_cols(half * TH + i)], wo,
                                   start=True, stop=True)
                mm.then_inc(proj_done, 1)
            if featT is not None:
                for half in range(2):
                    pe.matmul(psum[:, 2 + half, :], wo, AT[:, half * HALF:(half + 1) * HALF], start=True, stop=True)\
                        .then_inc(feat_done, 1)

        @block.vector
        def _(dve):
            n = 0
            for half in range(2):
                dve.wait_ge(proj_done, half + 1)
                cols = slice(half * TH, (half + 1) * TH)
                cur = psum[:, half, :].rearrange("p (t d) -> p t d", d=D)
                for a in adds:
                    if n and cur is not None and n % len(adds):
                        dve.wait_ge(added, n)
                    term = a[:, cols, :] if len(a.shape) == 3 else a.unsqueeze(1).to_broadcast([P, TH, D])
                    dve.tensor_tensor(dst[:, cols, :], cur, term, ALU.add).then_inc(added, 1)
                    cur = dst[:, cols, :]
                    n += 1
            dve.wait_ge(added, n)

        if featT is not None:
            @block.scalar
            def _(act):
                for half in range(2):
                    act.wait_ge(feat_done, half + 1)
                    act.activation(featT[:, half * HALF:(half + 1) * HALF], psum[:, 2 + half, :], ACT.Identity,
                                   bias=ch["params"][:, feat_bias:feat_bias + 1]).then_inc(feat_kept, 1)
                act.wait_ge(feat_kept, 2)


def inner_steps(nc, ch, steps=8, dt=0.1):
    psum, xs, ctx = ch["psum"], ch["XT"], ch["LT"]
    with ExitStack() as st:
        w, u, drift, slowed, pulled = (st.enter_context(nc.sbuf_tensor(n, [P, 2, HALF], F32))
                                       for n in ("w", "u", "drift", "slowed", "pulled"))
        pre_done, tanh_done, speed_done, state_done, parts_done, drift_done = (
            stage_semaphores(nc, ch, f"{n}0", f"{n}1") for n in
            ("pre_done", "tanh_done", "speed_done", "state_done", "parts_done", "drift_done"))
        (cleared,) = stage_semaphores(nc, ch, "cleared")
        block = st.enter_context(stage_block(nc, ch))

        def half_of(a, h):
            return a[:, h * HALF:(h + 1) * HALF]

        @block.tensor
        def _(pe):
            with pe.Fori(0, steps) as i:
                for h in range(2):
                    pe.wait_ge(tanh_done[h], i + 1)
                    pe.matmul(psum[:, h, :], ch["wctx"][:, :], half_of(ctx, h), start=True, stop=False)
                    pe.wait_ge(state_done[h], i + 1)
                    pe.matmul(psum[:, h, :], ch["wx"][:, :], half_of(xs, h), start=False, stop=True)\
                        .then_inc(pre_done[h], 1)

        @block.scalar
        def _(act):
            def parts(h, i):
                act.wait_ge(state_done[h], i + 1)
                act.wait_ge(drift_done[h], i + 1)
                act.activation(slowed[:, h, :], w[:, h, :], ACT.Copy, scale=1.0 - dt).then_inc(parts_done[h], 1)
                act.activation(pulled[:, h, :], half_of(xs, h), ACT.Copy, scale=dt * dt).then_inc(parts_done[h], 1)

            def squash(h, i):
                act.wait_ge(pre_done[h], i + 1)
                act.wait_ge(speed_done[h], i + 1)
                act.activation(u[:, h, :], psum[:, h, :], ACT.Tanh, bias=ch["params"][:, 6:7])\
                    .then_inc(tanh_done[h], 1)

            for h in range(2):
                act.sem_inc(tanh_done[h], 1)
            act.wait_ge(cleared, 1)
            parts(0, 0)
            with act.Fori(0, steps) as i:
                squash(0, i)
                parts(1, i)
                squash(1, i)
                parts(0, i + 1)

        @block.gpsimd
        def _(pool):
            def drifts(h, i):
                pool.wait_ge(parts_done[h], 2 * i + 2)
                pool.wait_ge(speed_done[h], i + 1)
                pool.tensor_tensor(drift[:, h, :], slowed[:, h, :], pulled[:, h, :], ALU.subtract)\
                    .then_inc(drift_done[h], 1)

            pool.memset(w[:, :, :], 0.0).then_inc(cleared, 1)
            for h in range(2):
                pool.sem_inc(drift_done[h], 1)
            drifts(0, 0)
            with pool.Fori(0, steps) as i:
                drifts(1, i)
                drifts(0, i + 1)

        @block.vector
        def _(dve):
            for h in range(2):
                dve.sem_inc(speed_done[h], 1)
                dve.sem_inc(state_done[h], 1)
            with dve.Fori(0, steps) as i:
                for h in range(2):
                    dve.wait_ge(tanh_done[h], i + 2)
                    dve.wait_ge(drift_done[h], i + 2)
                    dve.scalar_tensor_tensor(out=w[:, h, :], in0=u[:, h, :], scalar=dt * dt, in1=drift[:, h, :],
                                             op0=ALU.mult, op1=ALU.add).then_inc(speed_done[h], 1)
                    dve.wait_ge(speed_done[h], i + 2)
                    dve.tensor_tensor(half_of(xs, h), half_of(xs, h), w[:, h, :], ALU.add)\
                        .then_inc(state_done[h], 1)


def turn_add(nc, ch, featT, dst, add):
    psum = ch["psum"]
    with ExitStack() as st:
        turned, added = stage_semaphores(nc, ch, "turned", "added")
        block = st.enter_context(stage_block(nc, ch))

        @block.tensor
        def _(pe):
            for half in range(2):
                for i in range(TH):
                    mm = pe.transpose(psum[:, half, i * P:(i + 1) * P], featT[:, tile_cols(half * TH + i)],
                                      ch["identf"][:, :])
                mm.then_inc(turned, 1)

        @block.vector
        def _(dve):
            for half in range(2):
                dve.wait_ge(turned, half + 1)
                cols = slice(half * TH, (half + 1) * TH)
                dve.tensor_tensor(dst[:, cols, :], psum[:, half, :].rearrange("p (t d) -> p t d", d=D),
                                  add[:, cols, :], ALU.add).then_inc(added, 1)
            dve.wait_ge(added, 2)


def gelu_mlp(nc, ch, x0, x2, dst):
    psum, XT = ch["psum"], ch["XT"]
    with ExitStack() as st:
        hidden = st.enter_context(nc.sbuf_tensor("hidden", [P, NC, NTOK], F32))
        up_done, gelu_done, down_done, rest_done, added = stage_semaphores(
            nc, ch, "up_done", "gelu_done", "down_done", "rest_done", "added")
        block = st.enter_context(stage_block(nc, ch))

        @block.tensor
        def _(pe):
            for half in range(2):
                for c in range(NC):
                    if half:
                        pe.wait_ge(gelu_done, c + 1)
                    pe.matmul(psum[:, c, :], ch["ffw1"][:, c * P:(c + 1) * P], XT[:, half * HALF:(half + 1) * HALF],
                              start=True, stop=True).then_inc(up_done, 1)
            for half in range(2):
                pe.wait_ge(gelu_done, NC * (half + 1))
                for i in range(TH):
                    for c in range(NC):
                        mm = pe.matmul(psum[:, 4 + half, i * P:(i + 1) * P], hidden[:, c, tile_cols(half * TH + i)],
                                       ch["ffw2"][:, c, :], start=(c == 0), stop=(c == NC - 1))
                mm.then_inc(down_done, 1)

        @block.scalar
        def _(act):
            for n in range(2 * NC):
                half, c = divmod(n, NC)
                act.wait_ge(up_done, n + 1)
                act.activation(hidden[:, c, half * HALF:(half + 1) * HALF], psum[:, c, :], ACT.Gelu,
                               bias=ch["params"][:, 14 + c:15 + c]).then_inc(gelu_done, 1)

        @block.vector
        def _(dve):
            dve.tensor_tensor(dst[:, :, :], x0[:, :, :], x2[:, :, :], ALU.add).then_inc(rest_done, 1)
            dve.wait_ge(rest_done, 1)
            dve.tensor_tensor(dst[:, :, :], dst[:, :, :], ch["rows"][:, 2, :].unsqueeze(1).to_broadcast([P, NT, D]),
                              ALU.add).then_inc(rest_done, 1)
            dve.wait_ge(rest_done, 2)
            for half in range(2):
                dve.wait_ge(down_done, half + 1)
                cols = slice(half * TH, (half + 1) * TH)
                dve.tensor_tensor(dst[:, cols, :], psum[:, 4 + half, :].rearrange("p (t d) -> p t d", d=D),
                                  dst[:, cols, :], ALU.add).then_inc(added, 1)
            dve.wait_ge(added, 2)


def quantize(dve, chain, at, dst, src, tmp, scale, clipped=True):
    dve.tensor_scalar(tmp, src, scale, ROUND, ALU.mult, ALU.add).then_inc(chain, 1)
    dve.wait_ge(chain, at + 1)
    dve.tensor_scalar(tmp, tmp, ROUND + 127.0, ROUND - 128.0, ALU.min, ALU.max).then_inc(chain, 1)
    dve.wait_ge(chain, at + 2)
    return dve.tensor_scalar(dst, tmp, -ROUND, None, ALU.add)


def quantized_ffn(nc, ch, x, dst):
    psum, identf, identb = ch["psum"], ch["identf"], ch["identb"]
    wT = ch["wternT"]
    w1T, w2T = wT[:, 0, :], wT[:, 1, :].rearrange("p (c d) -> p c d", d=D)
    with ExitStack() as st:
        def sb(n, shape, dt=F32):
            return st.enter_context(nc.sbuf_tensor(n, [P, *shape], dt))

        xq, xqT = sb("xq", [NT, D], BF16), sb("xqT", [NTOK], BF16)
        tmp, row_scale = sb("tmp", [NTOK]), sb("row_scale", [NTOK])
        amax, inv, back = sb("amax", [2, NT]), sb("inv", [2, NT]), sb("back", [2, NT])
        grid, mix = sb("grid", [2, NTOK]), sb("mix", [NC, NTOK])
        hq, hqT = sb("hq", [2, FF], BF16), sb("hqT", [2, FF], BF16)
        htmp = sb("htmp", [2, FF])
        (chain, x_quantized, x_turned, x_kept, rows_done, rows_kept, hid_done, grid_done, centre_done, conv_done,
         silu_done, h_turned, h_quantized, hq_turned, hq_kept, down_done, added) = stage_semaphores(
            nc, ch, "chain", "x_quantized", "x_turned", "x_kept", "rows_done", "rows_kept", "hid_done", "grid_done",
            "centre_done", "conv_done", "silu_done", "h_turned", "h_quantized", "hq_turned", "hq_kept", "down_done",
            "added")
        block = st.enter_context(stage_block(nc, ch))
        UNITS = 2 * NC

        def seqs(a, c, half):
            return a[:, c, half * HALF:(half + 1) * HALF].rearrange("p (b s) -> p b s", s=S)

        def add_tile(dve, t):
            dve.wait_ge(down_done, t + 1)
            dve.scalar_tensor_tensor(out=dst[:, t, :], in0=psum[:, 6 + t % 2, 0:D], scalar=back[:, 1, t:t + 1],
                                     in1=x[:, t, :], op0=ALU.mult, op1=ALU.add).then_inc(added, 1)

        @block.vector
        def _(dve):
            n = 0

            def own(ins):
                nonlocal n
                ins.then_inc(chain, 1)
                n += 1
                dve.wait_ge(chain, n)

            own(dve.tensor_reduce(amax[:, 0, :], x[:, :, :], AX, ALU.max, apply_absolute_value=True))
            own(dve.tensor_scalar(amax[:, 0, :], amax[:, 0, :], 1e-5, None, ALU.max))
            own(dve.reciprocal(inv[:, 0, :], amax[:, 0, :]))
            own(dve.tensor_scalar(inv[:, 0, :], inv[:, 0, :], 127.0, None, ALU.mult))
            own(dve.tensor_scalar(back[:, 0, :], amax[:, 0, :], ch["wmean"][:, 0:1], 1.0 / 127.0, ALU.mult, ALU.mult))
            for t in range(NT):
                own(dve.tensor_scalar(tmp[:, tile_cols(t)], x[:, t, :], inv[:, 0, t:t + 1], ROUND, ALU.mult, ALU.add))
            own(dve.tensor_scalar(tmp[:, :], tmp[:, :], ROUND + 127.0, ROUND - 128.0, ALU.min, ALU.max))
            dve.tensor_scalar(xq[:, :, :].rearrange("p t d -> p (t d)"), tmp[:, :], -ROUND, None, ALU.add)\
                .then_inc(x_quantized, 1)
            for u in range(UNITS):
                c, half = divmod(u, 2)
                dve.wait_ge(rows_kept, 2)
                dve.wait_ge(hid_done, u + 1)
                if u >= 2:
                    dve.wait_ge(centre_done, u - 1)
                cols = slice(half * HALF, (half + 1) * HALF)
                dve.tensor_tensor(grid[:, u % 2, 0:HALF], psum[:, u % 2, :], row_scale[:, cols], ALU.mult)\
                    .then_inc(grid_done, 1)
                dve.wait_ge(grid_done, u + 1)
                dve.wait_ge(centre_done, u + 1)
                g = grid[:, u % 2, 0:HALF].rearrange("p (b s) -> p b s", s=S)
                y = seqs(mix, c, half)
                dve.scalar_tensor_tensor(out=y[:, :, 1:S], in0=g[:, :, 0:S - 1], scalar=ch["convw"][:, c, 0:1],
                                         in1=y[:, :, 1:S], op0=ALU.mult, op1=ALU.add).then_inc(conv_done, 1)
                dve.wait_ge(conv_done, 2 * u + 1)
                dve.scalar_tensor_tensor(out=y[:, :, 0:S - 1], in0=g[:, :, 1:S], scalar=ch["convw"][:, c, 2:3],
                                         in1=y[:, :, 0:S - 1], op0=ALU.mult, op1=ALU.add).then_inc(conv_done, 1)
            for t in range(NT):
                s = t % 2
                dve.wait_ge(h_turned, t + 1)
                own(dve.tensor_reduce(amax[:, 1, t:t + 1], psum[:, 2 + s, :], AX, ALU.max, apply_absolute_value=True))
                own(dve.tensor_scalar(amax[:, 1, t:t + 1], amax[:, 1, t:t + 1], 1e-5, None, ALU.max))
                own(dve.reciprocal(inv[:, 1, t:t + 1], amax[:, 1, t:t + 1]))
                own(dve.tensor_scalar(inv[:, 1, t:t + 1], inv[:, 1, t:t + 1], 127.0, None, ALU.mult))
                own(dve.tensor_scalar(back[:, 1, t:t + 1], amax[:, 1, t:t + 1], ch["wmean"][:, 1:2], 1.0 / 127.0,
                                      ALU.mult, ALU.mult))
                quantize(dve, chain, n, hq[:, s, :], psum[:, 2 + s, :], htmp[:, s, :], inv[:, 1, t:t + 1])\
                    .then_inc(h_quantized, 1)
                n += 2
                if t:
                    add_tile(dve, t - 1)
            add_tile(dve, NT - 1)
            dve.wait_ge(added, NT)

        @block.scalar
        def _(act):
            act.wait_ge(x_turned, 1)
            act.activation(xqT[:, :], psum[:, 4, :].bitcast(BF16), ACT.Copy).then_inc(x_kept, 1)
            for half in range(2):
                act.wait_ge(rows_done, half + 1)
                act.activation(row_scale[:, half * HALF:(half + 1) * HALF], psum[:, 6 + half, :], ACT.Copy)\
                    .then_inc(rows_kept, 1)

            def silu(u):
                c, half = divmod(u, 2)
                act.wait_ge(conv_done, 2 * u + 2)
                a = mix[:, c, half * HALF:(half + 1) * HALF]
                act.activation(a, a, ACT.Silu).then_inc(silu_done, 1)

            for u in range(UNITS):
                c, half = divmod(u, 2)
                act.wait_ge(grid_done, u + 1)
                act.activation(mix[:, c, half * HALF:(half + 1) * HALF], grid[:, u % 2, 0:HALF], ACT.Identity,
                               scale=ch["convw"][:, c, 1:2], bias=ch["params"][:, 14 + NC + c:15 + NC + c]).then_inc(centre_done, 1)
                if u:
                    silu(u - 1)
            silu(UNITS - 1)
            for t in range(NT):
                act.wait_ge(hq_turned, t + 1)
                if t >= 2:
                    act.wait_ge(down_done, t - 1)
                act.activation(hqT[:, t % 2, :], psum[:, 4 + t % 2, 0:FF // 2].bitcast(BF16), ACT.Copy)\
                    .then_inc(hq_kept, 1)

        @block.tensor
        def _(pe):
            pe.wait_ge(x_quantized, 1)
            for t in range(NT):
                mm = pe.transpose(psum[:, 4, t * 64:(t + 1) * 64].bitcast(BF16), xq[:, t, :], identb[:, :])
            mm.then_inc(x_turned, 1)
            for half in range(2):
                for i in range(TH):
                    t = half * TH + i
                    mm = pe.matmul(psum[:, 6 + half, i * P:(i + 1) * P], back[:, 0, t:t + 1].to_broadcast([P, P]),
                                   identf[:, :], start=True, stop=True)
                mm.then_inc(rows_done, 1)
            pe.wait_ge(x_kept, 1)
            for u in range(UNITS):
                c, half = divmod(u, 2)
                if u >= 2:
                    pe.wait_ge(grid_done, u - 1)
                pe.matmul(psum[:, u % 2, :], w1T[:, c * P:(c + 1) * P], xqT[:, half * HALF:(half + 1) * HALF],
                          start=True, stop=True).then_inc(hid_done, 1)

            def turn_hidden(t):
                pe.wait_ge(silu_done, UNITS - 1 if t < TH else UNITS)
                if t >= 2:
                    pe.wait_ge(h_quantized, t - 1)
                for c in range(NC):
                    mm = pe.transpose(psum[:, 2 + t % 2, c * P:(c + 1) * P], mix[:, c, tile_cols(t)], identf[:, :])
                mm.then_inc(h_turned, 1)

            turn_hidden(0)
            for t in range(NT):
                if t + 1 < NT:
                    turn_hidden(t + 1)
                pe.wait_ge(h_quantized, t + 1)
                pe.wait_ge(rows_kept, 2)
                if t >= 2:
                    pe.wait_ge(hq_kept, t - 1)
                for c in range(NC):
                    mm = pe.transpose(psum[:, 4 + t % 2, c * 64:(c + 1) * 64].bitcast(BF16),
                                      hq[:, t % 2, c * P:(c + 1) * P], identb[:, :])
                mm.then_inc(hq_turned, 1)
                pe.wait_ge(hq_kept, t + 1)
                if t >= 2:
                    pe.wait_ge(added, t - 1)
                for c in range(NC):
                    mm = pe.matmul(psum[:, 6 + t % 2, 0:D], hqT[:, t % 2, c * P:(c + 1) * P], w2T[:, c, :],
                                   start=(c == 0), stop=(c == NC - 1))
                mm.then_inc(down_done, 1)


def wide_attention(nc, ch, w_qkv, w_o, dst):
    psum, XT = ch["psum"], ch["XT"]
    Pr, PT, mx, den, rden = (ch[n] for n in ("Pr", "PT", "mx", "den", "rden"))
    with ExitStack() as st:
        def sb(n, shape):
            return st.enter_context(nc.sbuf_tensor(n, [P, *shape], F32))

        W, Wo = sb("W", [2, 3, 2, N1]), sb("Wo", [2, D])
        QK, Vp, ctx = sb("QK", [2, 2, NTOK]), sb("Vp", [2, 2, NT, N1]), sb("ctx", [2, NTOK])
        loaded = stage_semaphores(nc, ch, "loaded0", "loaded1")
        (qk_done, qk_kept, v_done, v_kept, scores_done, max_done, centred, exp_done, sum_done, inverse_done,
         probs_done, turned, turned_kept, pv_done, ctx_kept, out_done, added) = stage_semaphores(
            nc, ch, "qk_done", "qk_kept", "v_done", "v_kept", "scores_done", "max_done", "centred", "exp_done",
            "sum_done", "inverse_done", "probs_done", "turned", "turned_kept", "pv_done", "ctx_kept", "out_done",
            "added")
        (waited,) = stage_semaphores(nc, ch, "waited")
        block = st.enter_context(stage_block(nc, ch))

        def pairs(eng, before, step):
            before()
            with eng.Fori(0, NP1 // 2 - 1) as i:
                step(2 * i, i, 0, True, True)
                step(2 * i + 1, i, 1, True, True)
            step(NP1 - 2, NP1 // 2 - 1, 0, True, False)
            step(NP1 - 1, NP1 // 2 - 1, 1, False, False)

        @block.sync
        def _(sp):
            def load(j, s):
                sp.wait_ge(out_done, j + 1)
                for par in range(2):
                    h = 2 * j + par
                    sp.dma_start(W[:, s, :, par, :], w_qkv[bass.ds(h, 1)].rearrange("h a v n -> v (h a) n"))\
                        .then_inc(loaded[s], 16)
                sp.dma_start(Wo[:, s, :], w_o[bass.ds(j * P, P), :]).then_inc(loaded[s], 16)

            load(0, 0)
            load(1, 1)
            with sp.Fori(1, NP1 // 2) as i:
                load(2 * i, 0)
                load(2 * i + 1, 1)

        @block.tensor
        def _(pe):
            def project(j, i, s):
                pe.wait_ge(loaded[s], 48 * i + 48)
                for m in range(2):
                    for half in range(2):
                        pe.wait_ge(qk_kept, 4 * j + 2 * m + half + 3)
                        pe.matmul(psum[:, half, :], W[:, s, m, :, :].rearrange("p a n -> p (a n)"),
                                  XT[:, half * HALF:(half + 1) * HALF], start=True, stop=True).then_inc(qk_done, 1)
                pe.wait_ge(ctx_kept, 2 * j + 2)
                for half in range(2):
                    for i4 in range(TH):
                        mm = pe.matmul(psum[:, 2 + half, i4 * P:(i4 + 1) * P], XT[:, tile_cols(half * TH + i4)],
                                       W[:, s, 2, :, :].rearrange("p a n -> p (a n)"), start=True, stop=True)
                    mm.then_inc(v_done, 1)

            def scores(j, s):
                pe.wait_ge(qk_kept, 4 * j + 8)
                pe.wait_ge(centred, j + 1)
                pe.sem_inc(waited, 1)
                for t in range(NT):
                    for b in range(2):
                        for par in range(2):
                            rows, cols = slice(64 * par, 64 * par + 64), slice(t * P + 64 * b, t * P + 64 * b + 64)
                            mm = pe.matmul(psum[64 * b:64 * b + 64, 4 + par, t * S:(t + 1) * S],
                                           QK[rows, s, 0, cols], QK[rows, s, 1, cols], start=True, stop=True)
                mm.then_inc(scores_done, 1)

            def turn(j, s):
                pe.wait_ge(probs_done, j + 1)
                pe.wait_ge(added, 2 * j + 2)
                for t in range(NT):
                    mm = pe.transpose(psum[:, 6 + t // TH, (t % TH) * P:(t % TH + 1) * P],
                                      Pr[:, s, 2 * t:2 * t + 2, :].rearrange("p a k -> p (a k)"), ch["identf"][:, :])
                mm.then_inc(turned, 1)

            def values(j, s, ahead):
                pe.wait_ge(turned_kept, 2 * j + 2)
                pe.wait_ge(v_kept, 4 * j + 4 + 4 * ahead)
                pe.sem_inc(waited, 1)
                for t in range(NT):
                    for b in range(2):
                        for par in range(2):
                            rows = slice(64 * par, 64 * par + 64)
                            col = (t % TH) * P + 64 * b
                            mm = pe.matmul(psum[rows, 2 + t // TH, col:col + 64], Vp[rows, s, b, t, :],
                                           PT[rows, s, t, 64 * b:64 * b + 64], start=True, stop=True)
                mm.then_inc(pv_done, 1)

            def output(j, s):
                pe.wait_ge(ctx_kept, 2 * j + 6)
                for half in range(2):
                    for i4 in range(TH):
                        mm = pe.matmul(psum[:, 6 + half, i4 * P:(i4 + 1) * P], ctx[:, s, tile_cols(half * TH + i4)],
                                       Wo[:, s, :], start=True, stop=True)
                mm.then_inc(out_done, 1)

            def before():
                pe.sem_inc(out_done, 2)
                pe.sem_inc(scores_done, 2)
                pe.sem_inc(pv_done, 2)
                pe.sem_inc(turned, 2)
                project(0, 0, 0)
                scores(0, 0)

            def step(j, i, s, one, two):
                if one:
                    project(j + 1, i + s, 1 - s)
                turn(j, s)
                values(j, s, 1 if one else 0)
                if one:
                    scores(j + 1, 1 - s)
                output(j, s)

            pairs(pe, before, step)

        @block.scalar
        def _(act):
            def keep_qk(j, s):
                act.wait_ge(scores_done, j + 1)
                for m in range(2):
                    for half in range(2):
                        act.wait_ge(qk_done, 4 * j + 2 * m + half + 1)
                        act.activation(QK[:, s, m, half * HALF:(half + 1) * HALF], psum[:, half, :], ACT.Copy)\
                            .then_inc(qk_kept, 1)

            def keep_values(j, s):
                act.wait_ge(pv_done, j + 1)
                act.wait_ge(v_done, 2 * j + 2)
                v = psum[:, 2:4, :].rearrange("p a (t c n) -> p (a t) c n", c=2, n=N1)
                for b in range(2):
                    for par in range(2):
                        act.activation(Vp[64 * par:64 * par + 64, s, b, :, :], v[64 * b:64 * b + 64, :, par, :],
                                       ACT.Copy).then_inc(v_kept, 1)

            def exponentials(j, s):
                act.wait_ge(centred, j + 2)
                act.activation(Pr[:, s, :, :], Pr[:, s, :, :], ACT.Exp, scale=float(N1) ** -0.5).then_inc(exp_done, 1)

            def keep_turned(j, s):
                act.wait_ge(turned, j + 3)
                act.wait_ge(pv_done, j + 1)
                for m in range(2):
                    act.activation(PT[:, s, 4 * m:4 * m + 4, :].rearrange("p h q -> p (h q)"), psum[:, 6 + m, :],
                                   ACT.Copy).then_inc(turned_kept, 1)

            def before():
                act.sem_inc(qk_kept, 4)
                keep_qk(0, 0)
                keep_values(0, 0)

            def step(j, i, s, one, two):
                exponentials(j, s)
                if one:
                    keep_qk(j + 1, 1 - s)
                    keep_values(j + 1, 1 - s)
                keep_turned(j, s)

            pairs(act, before, step)

        @block.gpsimd
        def _(pool):
            def step(j, i, s, one, two):
                pool.wait_ge(inverse_done, j + 1)
                pool.tensor_tensor(Pr[:, s, :, :], Pr[:, s, :, :], rden[:, s, :].unsqueeze(2).to_broadcast([P, 16, S]),
                                   ALU.mult).then_inc(probs_done, 1)

            pairs(pool, lambda: None, step)

        @block.vector
        def _(dve):
            def centre(j, s):
                dve.wait_ge(scores_done, j + 3)
                sc = psum[:, 4:6, :].rearrange("p a (t k) -> p a t k", k=S)
                dve.tensor_reduce(mx[:, s, :].rearrange("p (a t) -> p a t", a=2), sc, AX, ALU.max)\
                    .then_inc(max_done, 1)
                dve.wait_ge(max_done, j + 1)
                dve.wait_ge(turned, j + 1)
                m = mx[:, s, :].rearrange("p (a t) -> p a t", a=2).unsqueeze(3).to_broadcast([P, 2, NT, S])
                dve.tensor_tensor(Pr[:, s, :, :].rearrange("p (t a) k -> p a t k", a=2), sc, m, ALU.subtract)\
                    .then_inc(centred, 1)

            def before():
                dve.sem_inc(centred, 1)
                dve.sem_inc(ctx_kept, 4)
                dve.sem_inc(added, 2)
                centre(0, 0)

            def step(j, i, s, one, two):
                dve.wait_ge(exp_done, j + 1)
                dve.tensor_reduce(den[:, s, :], Pr[:, s, :, :], AX, ALU.add).then_inc(sum_done, 1)
                dve.wait_ge(sum_done, j + 1)
                dve.reciprocal(rden[:, s, :], den[:, s, :]).then_inc(inverse_done, 1)
                dve.wait_ge(pv_done, j + 3)
                dve.wait_ge(out_done, j + 1)
                for half in range(2):
                    dve.tensor_copy(ctx[:, s, half * HALF:(half + 1) * HALF], psum[:, 2 + half, :])\
                        .then_inc(ctx_kept, 1)
                if one:
                    centre(j + 1, 1 - s)
                dve.wait_ge(out_done, j + 3)
                for half in range(2):
                    rows = dst[:, half * TH:(half + 1) * TH, :]
                    dve.wait_ge(added, 2 * j + half + 1)
                    dve.tensor_tensor(rows, psum[:, 6 + half, :].rearrange("p (t d) -> p t d", d=D), rows, ALU.add)\
                        .then_inc(added, 1)

            pairs(dve, before, step)


def route(nc, ch):
    psum, XT, iota = ch["psum"], ch["XT"], ch["iota8"]
    with ExitStack() as st:
        def sb(n, shape, dt=F32):
            return st.enter_context(nc.sbuf_tensor(n, [P, *shape], dt))

        prob, top, at, atf = sb("prob", [NT, NE]), sb("top", [NT, 8]), sb("at", [NT, 8], U32), sb("atf", [NT, 8])
        hi, total, pick = sb("hi", [NT]), sb("total", [NT]), sb("pick", [2, NT, NE])
        logits_done, chain, exp_done = stage_semaphores(nc, ch, "logits_done", "chain", "exp_done")
        block = st.enter_context(stage_block(nc, ch))

        @block.tensor
        def _(pe):
            for t in range(NT):
                mm = pe.matmul(psum[:, 0, t * NE:(t + 1) * NE], XT[:, tile_cols(t)], ch["wrout"][:, :], start=True,
                               stop=True)
            mm.then_inc(logits_done, 1)

        @block.scalar
        def _(act):
            act.wait_ge(chain, 2)
            act.activation(prob[:, :, :], prob[:, :, :], ACT.Exp).then_inc(exp_done, 1)

        @block.vector
        def _(dve):
            n = 0

            def own(*ins):
                nonlocal n
                for x in ins:
                    x.then_inc(chain, 1)
                n += len(ins)
                dve.wait_ge(chain, n)

            def wide(a):
                return a.unsqueeze(2).to_broadcast([P, NT, NE])

            dve.wait_ge(logits_done, 1)
            logits = psum[:, 0, 0:NT * NE].rearrange("p (t e) -> p t e", e=NE)
            own(dve.tensor_reduce(hi[:, :], logits, AX, ALU.max))
            own(dve.tensor_tensor(prob[:, :, :], logits, wide(hi[:, :]), ALU.subtract))
            dve.wait_ge(exp_done, 1)
            own(dve.tensor_reduce(total[:, :], prob[:, :, :], AX, ALU.add))
            own(dve.reciprocal(total[:, :], total[:, :]))
            own(dve.tensor_tensor(prob[:, :, :], prob[:, :, :], wide(total[:, :]), ALU.mult))
            own(*[dve.max(top[:, t, :], prob[:, t, :]) for t in range(NT)])
            own(*[dve.max_index(at[:, t, :], top[:, t, :], prob[:, t, :]) for t in range(NT)])
            own(dve.tensor_copy(atf[:, :, :], at[:, :, :]))
            own(dve.tensor_tensor(total[:, :], top[:, :, 0], top[:, :, 1], ALU.add))
            own(dve.reciprocal(total[:, :], total[:, :]))
            for k in range(2):
                own(dve.tensor_tensor(pick[:, k, :, :], wide(atf[:, :, k]),
                                      iota[:, :].unsqueeze(1).to_broadcast([P, NT, NE]), ALU.is_equal))
                own(dve.tensor_tensor(pick[:, k, :, :], pick[:, k, :, :], wide(top[:, :, k]), ALU.mult))
            own(dve.tensor_tensor(pick[:, 0, :, :], pick[:, 0, :, :], pick[:, 1, :, :], ALU.add))
            own(dve.tensor_tensor(ch["comb"][:, :, :], pick[:, 0, :, :], wide(total[:, :]), ALU.mult))


def experts(nc, ch, wg, wu, wd, dst):
    psum, XT, comb = ch["psum"], ch["XT"], ch["comb"]
    with ExitStack() as st:
        def sb(n, shape):
            return st.enter_context(nc.sbuf_tensor(n, [P, *shape], F32))

        Wg, Wu, Wd = sb("Wg", [2, HID]), sb("Wu", [2, HID]), sb("Wd", [2, HC, D])
        sg, prod = sb("sg", [HC, HALF]), sb("prod", [2, HC, HALF])
        loaded = stage_semaphores(nc, ch, "loaded0", "loaded1")
        gate_done, up_done, silu_done, prod_done, down_done, added = stage_semaphores(
            nc, ch, "gate_done", "up_done", "silu_done", "prod_done", "down_done", "added")
        block = st.enter_context(stage_block(nc, ch))

        def units(eng, step):
            with eng.Fori(0, NE // 2 - 1) as i:
                for k in range(4):
                    step(4 * i + k, i, k, True)
            for k in range(4):
                step(2 * NE - 4 + k, NE // 2 - 1, k, k < 3)

        @block.sync
        def _(sp):
            def load(e, s):
                sp.dma_start(Wg[:, s, :].unsqueeze(1), wg[bass.ds(e, 1)].rearrange("e d n -> d e n")).then_inc(loaded[s], 16)
                sp.dma_start(Wu[:, s, :].unsqueeze(1), wu[bass.ds(e, 1)].rearrange("e d n -> d e n")).then_inc(loaded[s], 16)
                sp.dma_start(Wd[:, s, :, :], wd[bass.ds(e, 1)].rearrange("e (c p) d -> p (e c) d", p=P))\
                    .then_inc(loaded[s], 16)

            load(0, 0)
            load(1, 1)
            with sp.Fori(1, NE // 2) as i:
                for s in range(2):
                    sp.wait_ge(down_done, 4 * i + 2 * s)
                    load(2 * i + s, s)

        @block.tensor
        def _(pe):
            def up(u, i, k):
                s, half = (k // 2) % 2, k % 2
                pe.wait_ge(loaded[s], 48 * i + 48)
                rhs = XT[:, half * HALF:(half + 1) * HALF]
                for c in range(HC):
                    pe.wait_ge(silu_done, 3 * u + c + 1)
                    pe.matmul(psum[:, c, :], Wg[:, s, c * P:(c + 1) * P], rhs, start=True, stop=True)\
                        .then_inc(gate_done, 1)
                    pe.wait_ge(prod_done, 3 * u + c + 1)
                    pe.matmul(psum[:, HC + c, :], Wu[:, s, c * P:(c + 1) * P], rhs, start=True, stop=True)\
                        .then_inc(up_done, 1)

            def down(u, k):
                s = k // 2
                pe.wait_ge(prod_done, 3 * u + 6)
                pe.wait_ge(added, 4 * u + 4)
                for i4 in range(TH):
                    for c in range(HC):
                        mm = pe.matmul(psum[:, 6 + k % 2, i4 * P:(i4 + 1) * P], prod[:, k % 2, c, tile_cols(i4)],
                                       Wd[:, s, c, :], start=(c == 0), stop=(c == HC - 1))
                mm.then_inc(down_done, 1)

            def step(u, i, k, ahead):
                if ahead:
                    up(u + 1, i + (k + 1) // 4, (k + 1) % 4)
                down(u, k)

            pe.sem_inc(down_done, 2)
            up(0, 0, 0)
            units(pe, step)

        @block.scalar
        def _(act):
            def gate(u, k):
                for c in range(HC):
                    act.wait_ge(gate_done, 3 * u + c + 1)
                    act.wait_ge(prod_done, 3 * u + c + 1)
                    act.activation(sg[:, c, :], psum[:, c, :], ACT.Silu).then_inc(silu_done, 1)

            act.sem_inc(silu_done, 3)
            gate(0, 0)
            units(act, lambda u, i, k, ahead: gate(u + 1, (k + 1) % 4) if ahead else None)

        @block.vector
        def _(dve):
            def multiply(u, k):
                dve.wait_ge(down_done, u + 1)
                for c in range(HC):
                    dve.wait_ge(silu_done, 3 * u + c + 4)
                    dve.wait_ge(up_done, 3 * u + c + 1)
                    dve.tensor_tensor(prod[:, k % 2, c, :], psum[:, HC + c, :], sg[:, c, :], ALU.mult)\
                        .then_inc(prod_done, 1)

            def add(u, i, k):
                half = k % 2
                dve.wait_ge(down_done, u + 3)
                dve.wait_ge(added, 4 * u + 4)
                for i4 in range(TH):
                    t = half * TH + i4
                    dve.scalar_tensor_tensor(out=dst[:, t, :], in0=psum[:, 6 + half, i4 * P:(i4 + 1) * P],
                                             scalar=comb[:, t, bass.ds(2 * i + k // 2, 1)], in1=dst[:, t, :],
                                             op0=ALU.mult, op1=ALU.add).then_inc(added, 1)

            def step(u, i, k, ahead):
                if ahead:
                    multiply(u + 1, (k + 1) % 4)
                add(u, i, k)

            dve.sem_inc(prod_done, 3)
            dve.sem_inc(added, 8)
            multiply(0, 0)
            units(dve, step)


def decoder(nc, ins, cst, out):
    with ExitStack() as stack:
        ch = Chip(nc, stack)
        ch.buf["psum"] = stack.enter_context(nc.psum_tensor("psum", [P, 8, 512], F32))
        for name in ("X", "A", "R"):
            ch.sb(name, [NT, D])
        for name in ("XT", "CT", "AT", "LT"):
            ch.sb(name, [NTOK])
        for name in ("QP", "KP"):
            ch.sb(name, [2, HALF])
        ch.sb("V", [NT, D])
        ch.sb("rot", [4, HALF])
        ch.sb("Kx", [2, 2, 8, S])
        ch.sb("Qd", [2, 2, P])
        ch.sb("Vd", [2, 2, 4, 64])
        ch.sb("Pr", [2, H, S])
        ch.sb("PT", [2, 8, P])
        for name in ("mx", "den", "rden", "pad"):
            ch.sb(name, [2, H])
        ch.sb("stats", [NT, 6])
        ch.sb("mv", [NT, 2])
        for name in ("rstd", "var", "minus_half"):
            ch.sb(name, [NT])
        ch.sb("identf", [P])
        ch.sb("identb", [P], BF16)
        ch.sb("ones", [P])
        ch.sb("causal", [S], BF16)
        ch.sb("causalf", [S])
        ch.sb("head_of", [8])
        ch.sb("iota8", [NE])
        ch.sb("cos", [S])
        ch.sb("sin", [S])
        ch.sb("wqkv0", [3 * D])
        for name in ("wo0", "wctx", "wx", "xwq", "xwo", "mwq", "mwk", "mwv", "mwo"):
            ch.sb(name, [D])
        ch.sb("xwkv", [2 * HD])
        ch.sb("xwkr", [2, D])
        ch.sb("ffw1", [FF])
        ch.sb("ffw2", [NC, D])
        ch.sb("bw1", [NC, D])
        ch.sb("bw2", [FF])
        ch.sb("wtern", [2, FF], BF16)
        ch.sb("wternT", [2, FF], BF16)
        ch.sb("convw", [NC, 3])
        ch.sb("absum", [2])
        ch.sb("wmean", [2])
        ch.sb("winv", [2])
        ch.sb("ywo", [4, D])
        ch.sb("yw", [4 * D])
        ch.sb("mrot", [2, D])
        ch.sb("wrout", [NE])
        ch.sb("comb", [NT, NE])
        ch.sb("rows", [3, D])
        ch.sb("prow", [P])
        ch.sb("params", [NPAR])
        X, R, A, XT, CT, LT = (ch[n] for n in ("X", "R", "A", "XT", "CT", "LT"))

        load_inputs(nc, ch, ins, cst)
        w = ch["wqkv0"]
        norm(nc, ch, X, R, XT, gain=0, shift=1)
        small_qkv(nc, ch, w[:, 0:D], w[:, D:2 * D], w[:, 2 * D:3 * D], XT, XT, bias=True)
        small_attention(nc, ch, causal=True)
        project_add(nc, ch, ch["wo0"][:, :], A, [X, ch["rows"][:, 1, :]], featT=LT, feat_bias=7)
        norm(nc, ch, A, R, XT, gain=2, shift=3)
        inner_steps(nc, ch)
        turn_add(nc, ch, XT, A, A)
        norm(nc, ch, A, R, XT, gain=4, shift=5)
        gelu_mlp(nc, ch, X, A, R)
        norm(nc, ch, R, X, XT)
        small_qkv(nc, ch, ch["xwq"][:, :], ch["xwkr"][:, 0, :], ch["xwkr"][:, 1, :], XT, CT)
        small_attention(nc, ch, zero_keys=2 * S)
        project_add(nc, ch, ch["xwo"][:, :], R, [X])
        norm(nc, ch, R, X)
        quantized_ffn(nc, ch, X, R)
        norm(nc, ch, R, X, XT)
        wide_attention(nc, ch, ins["L1_attn_w_qkv"], ins["L1_attn_w_o"], X)
        norm(nc, ch, X, X, XT)
        yw = ch["yw"]
        small_qkv(nc, ch, yw[:, 0:D], yw[:, D:2 * D], yw[:, 2 * D:3 * D], XT, CT)
        small_attention(nc, ch)
        project_add(nc, ch, yw[:, 3 * D:4 * D], R, [X])
        norm(nc, ch, R, X)
        norm(nc, ch, X, R, XT, gain=8, eps=1e-6, rms=True)
        small_qkv(nc, ch, ch["mwq"][:, :], ch["mwk"][:, :], ch["mwv"][:, :], XT, XT,
                  rotated=(ch["mrot"][:, 0, :], ch["mrot"][:, 1, :]))
        small_attention(nc, ch, causal=True)
        project_add(nc, ch, ch["mwo"][:, :], R, [X])
        norm(nc, ch, R, A, XT, gain=9, eps=1e-6, rms=True)
        route(nc, ch)
        experts(nc, ch, ins["L1_ffn_wg"], ins["L1_ffn_wu"], ins["L1_ffn_wd"], R)
        sum_rows(nc, ch, R, X)
        norm(nc, ch, R, X, out=out)
        nc.clear_and_free_semaphores(ch.past)


def sum_rows(nc, ch, dst, add):
    with ExitStack() as st:
        (added,) = stage_semaphores(nc, ch, "added")
        block = st.enter_context(stage_block(nc, ch))

        @block.vector
        def _(dve):
            dve.tensor_tensor(dst[:, :, :], dst[:, :, :], add[:, :, :], ALU.add).then_inc(added, 1)
            dve.wait_ge(added, 1)


def constants():
    p = np.arange(P)
    inv_freq = 1.0 / 10000.0 ** (np.arange(0, HD, 2, dtype=np.float32) / HD)
    freqs = np.einsum("i,j->ij", np.arange(S, dtype=np.float32), inv_freq)
    emb = np.concatenate([freqs, freqs], axis=-1)
    return {
        "identf": np.eye(P, dtype=np.float32),
        "causal": np.where(np.arange(S)[None, :] > (p % S)[:, None], MASKED, 0.0).astype(np.float32),
        "head_of": ((p[:, None] // HD) % 8 == np.arange(8)[None, :]).astype(np.float32),
        "iota8": np.tile(np.arange(NE, dtype=np.float32), (P, 1)),
        "cos": np.ascontiguousarray(np.cos(emb).astype(np.float32)[:, p % HD].T),
        "sin": np.ascontiguousarray(np.sin(emb).astype(np.float32)[:, p % HD].T),
    }


def kernel(**inputs):
    import numpy as _np
    import concourse.bacc as _bacc
    from concourse import mybir as _mybir
    from concourse.bass_utils import run_bass_kernel_spmd as _run

    nc = _bacc.Bacc("TRN2", target_bir_lowering=False, num_devices=1)
    arrays, ins, cst = {}, {}, {}
    for group, given in ((ins, inputs), (cst, constants())):
        for name, a in given.items():
            a = _np.ascontiguousarray(a)
            arrays[f"in_{name}_dram"] = a
            group[name] = nc.dram_tensor(f"in_{name}_dram", a.shape, _mybir.dt.from_np(a.dtype),
                                         kind="ExternalInput").ap()
    out = nc.dram_tensor("out_0_dram", (B, S, D), F32, kind="ExternalOutput").ap()
    decoder(nc, ins, cst, out)
    r = _run(nc, [arrays], core_ids=[0])
    return r.results[0]["out_0_dram"]
```

```python
from contextlib import ExitStack, contextmanager

import numpy as np

import concourse.bass as bass
from concourse import mybir

F32 = mybir.dt.float32
BF16 = mybir.dt.bfloat16
F32R = mybir.dt.float32r
U32 = mybir.dt.uint32
ALU = mybir.AluOpType
ACT = mybir.ActivationFunctionType
AX = mybir.AxisListType.X

P = 128
B, S, D = 16, 64, 128
NTOK = B * S
NT = NTOK // P
HALF = NTOK // 2
TH = NT // 2
H, HD = 16, 8
FF = 512
NC = FF // P
NP1, N1 = 8, 64
NE, HID = 8, 384
HC = HID // P
NPAR = 14 + 2 * NC
ROUND = 1.5 * 2.0**23
MASKED = -1e30


class Chip:

    def __init__(self, nc, stack):
        self.nc, self.stack, self.buf = nc, stack, {}
        self.current, self.past, self.stage = [], [], 0

    def sb(self, name, shape, dt=F32):
        self.buf[name] = self.stack.enter_context(self.nc.sbuf_tensor(name, [P, *shape], dt))
        return self.buf[name]

    def __getitem__(self, name):
        return self.buf[name]


def stage_semaphores(nc, ch, *names):
    sems = [nc.alloc_semaphore(f"{n}_{ch.stage}") for n in names]
    ch.current += sems
    return sems


@contextmanager
def stage_block(nc, ch):
    if ch.past:
        nc.clear_and_free_semaphores(ch.past)
    with nc.Block() as block:
        yield block
    ch.past, ch.current = ch.current, []
    ch.stage += 1


def tile_cols(t, n=P):
    return bass.ds(t * n, n)


def load_inputs(nc, ch, ins, cst):
    def line(v):
        return v.rearrange("(a n) -> a n", a=1)

    def row(v):
        return v.rearrange("(a n) -> a n", a=1).to_broadcast([P, v.shape[0]])

    prow = ch["prow"]
    first = [
        (ch["X"][:, :, :], ins["x"].rearrange("(t b) s d -> (b s) t d", b=2)),
        (ch["identf"][:, :], cst["identf"]),
        (ch["wqkv0"][:, :], ins["L0_attn_qkv_w"]),
        (ch["causalf"][:, :], cst["causal"]), (ch["head_of"][:, :], cst["head_of"]),
        (ch["rows"][:, 0, :], row(ins["L0_attn_qkv_b"][2 * D:3 * D])),
    ]
    for n, name in enumerate(["L0_attn_g_attn", "L0_attn_b_attn", "L0_attn_g1", "L0_attn_b1", "L0_attn_g2",
                              "L0_attn_b2", "L0_attn_b_inl", "L0_attn_out_b", "L1_ffn_g1", "L1_ffn_g2"]):
        first.append((prow[n:n + 1, :], line(ins[name])))
    first.append((prow[10:14, :].rearrange("n (b d) -> n b d", b=2),
                  ins["L0_attn_qkv_b"][0:2 * D].rearrange("(n a d) -> n a d", a=1, d=64).to_broadcast([4, 2, 64])))
    first.append((prow[14:14 + NC, :], ins["L0_attn_ff_b1"].rearrange("(c p) -> c p", p=P)))
    first.append((prow[14 + NC:NPAR, :], ins["L0_ffn_conv_b"].rearrange("(c p) -> c p", p=P)))
    later = [
        (ch["wo0"][:, :], ins["L0_attn_out_w"]),
        (ch["rows"][:, 1, :], row(ins["L0_attn_out_b"])),
        (ch["wctx"][:, :], ins["L0_attn_w_ctx"]), (ch["wx"][:, :], ins["L0_attn_w_x"]),
        (ch["ffw1"][:, :], ins["L0_attn_ff_w1"]),
        (ch["ffw2"][:, :, :], ins["L0_attn_ff_w2"].rearrange("(c p) d -> p c d", p=P)),
        (ch["rows"][:, 2, :], row(ins["L0_attn_ff_b2"])),
        (ch["C"][:, :, :], ins["ctx_1024"].rearrange("(t b) s d -> (b s) t d", b=2)),
        (ch["xwq"][:, :], ins["L0_xattn_Wq"]), (ch["xwkv"][:, :], ins["L0_xattn_Wkv"]),
        (ch["xwo"][:, :], ins["L0_xattn_Wo"]),
        (ch["bw1"][:, :, :], ins["L0_ffn_w1"].rearrange("(c p) d -> p c d", p=P)),
        (ch["bw2"][:, :], ins["L0_ffn_w2"]),
        (ch["convw"][:, :, :], ins["L0_ffn_conv_w"].rearrange("(c p) a k -> p c (a k)", p=P)),
        (ch["cos"][:, :], cst["cos"]), (ch["sin"][:, :], cst["sin"]),
        (ch["iota8"][:, :], cst["iota8"]),
        (ch["ywo"][:, 0, :], ins["L1_xattn_w_q"]), (ch["ywo"][:, 1, :], ins["L1_xattn_w_k"]),
        (ch["ywo"][:, 2, :], ins["L1_xattn_w_v"]), (ch["ywo"][:, 3, :], ins["L1_xattn_w_o"]),
        (ch["mwq"][:, :], ins["L1_ffn_wq"]), (ch["mwk"][:, :], ins["L1_ffn_wk"]),
        (ch["mwv"][:, :], ins["L1_ffn_wv"]), (ch["mwo"][:, :], ins["L1_ffn_wo"]),
        (ch["wrout"][:, :], ins["L1_ffn_w_router"]),
    ]
    for e in range(2):
        for n, name in enumerate(("L1_ffn_wg", "L1_ffn_wu")):
            later.append((ch["We"][:, e, n * HID:(n + 1) * HID], ins[name][e]))
        later.append((ch["Wd"][:, e, :, :], ins["L1_ffn_wd"][e].rearrange("(c p) d -> p c d", p=P)))
    with ExitStack() as st:
        loaded, small_done, ones_set, turned, kept = stage_semaphores(
            nc, ch, "loaded", "small_done", "ones_set", "turned", "kept")
        psum = ch["psum"]
        block = st.enter_context(stage_block(nc, ch))
        all_loaded = 16 * len(first)

        @block.sync
        def _(sp):
            for dst, src in first[0::2]:
                sp.dma_start(dst, src).then_inc(loaded, 16)

        @block.gpsimd
        def _(pool):
            pool.memset(ch["minus_half"][:, :], -0.5).then_inc(small_done, 1)
            pool.memset(ch["Qd"][:, :, :, :], 0.0).then_inc(small_done, 1)
            pool.memset(ch["Vd"][:, :, :, :, :], 0.0).then_inc(small_done, 1)
            pool.wait_ge(loaded, all_loaded)
            pool.tensor_copy(ch["identb"][:, :], ch["identf"][:, :]).then_inc(small_done, 1)
            pool.tensor_copy(ch["causal"][:, :], ch["causalf"][:, :]).then_inc(small_done, 1)
            pool.wait_ge(small_done, 5)

        @block.scalar
        def _(act):
            for dst, src in first[1::2]:
                act.dma_start(dst, src).then_inc(loaded, 16)
            act.wait_ge(turned, 1)
            act.activation(ch["params"][:, :], psum[:, 6, 0:NPAR], ACT.Copy).then_inc(kept, 1)
            act.wait_ge(kept, 1)

        @block.vector
        def _(dve):
            dve.memset(ch["ones"][:, :], 1.0).then_inc(ones_set, 1)
            dve.wait_ge(ones_set, 1)

        @block.tensor
        def _(pe):
            pe.wait_ge(loaded, all_loaded)
            pe.transpose(psum[:, 6, 0:NPAR], prow[0:NPAR, :], ch["identf"][0:NPAR, 0:NPAR]).then_inc(turned, 1)
    return later


def norm(nc, ch, src, dst, featT=None, gain=None, shift=None, eps=1e-5, rms=False, out=None):
    psum, par = ch["psum"], ch["params"]
    mv, rstd, var = ch["mv"], ch["rstd"], ch["var"]
    with ExitStack() as st:
        stats_done, agg_done, var_done, root_done, normed, turned, stored = stage_semaphores(
            nc, ch, "stats_done", "agg_done", "var_done", "root_done", "normed", "turned", "stored")
        block = st.enter_context(stage_block(nc, ch))

        @block.vector
        def _(dve):
            for t in range(NT):
                dve.bn_stats(ch["stats"][:, t, :], src[:, t, :]).then_inc(stats_done, 1)
            for t in range(NT):
                dve.wait_ge(stats_done, t + 1)
                dve.bn_aggr(mv[:, t, :], ch["stats"][:, t, :]).then_inc(agg_done, 1)
            dve.wait_ge(agg_done, NT)
            if rms:
                dve.tensor_tensor(var[:, :], mv[:, :, 0], mv[:, :, 0], ALU.mult).then_inc(var_done, 1)
                dve.wait_ge(var_done, 1)
                dve.scalar_tensor_tensor(out=var[:, :], in0=var[:, :], scalar=eps, in1=mv[:, :, 1], op0=ALU.add,
                                         op1=ALU.add).then_inc(var_done, 1)
            else:
                dve.tensor_scalar(var[:, :], mv[:, :, 1], eps, None, ALU.add).then_inc(var_done, 2)
            dve.wait_ge(root_done, 1)
            for t in range(NT):
                if rms:
                    dve.tensor_scalar(dst[:, t, :], src[:, t, :], rstd[:, t:t + 1], None, ALU.mult).then_inc(normed, 1)
                else:
                    dve.tensor_scalar(dst[:, t, :], src[:, t, :], mv[:, t, 0:1], rstd[:, t:t + 1], ALU.subtract,
                                      ALU.mult).then_inc(normed, 1)
            dve.wait_ge(normed, NT)

        @block.gpsimd
        def _(pool):
            pool.wait_ge(var_done, 2)
            pool.tensor_tensor(rstd[:, :], var[:, :], ch["minus_half"][:, :], ALU.pow).then_inc(root_done, 1)

        if featT is not None:
            @block.tensor
            def _(pe):
                for half in range(2):
                    for i in range(TH):
                        t = half * TH + i
                        pe.wait_ge(normed, t + 1)
                        mm = pe.transpose(psum[:, half, i * P:(i + 1) * P], dst[:, t, :], ch["identf"][:, :])
                    mm.then_inc(turned, 1)

            @block.scalar
            def _(act):
                for half in range(2):
                    act.wait_ge(turned, half + 1)
                    cols = featT[:, half * HALF:(half + 1) * HALF]
                    scale = par[:, gain:gain + 1] if gain is not None else 1.0
                    bias = par[:, shift:shift + 1] if shift is not None else 0.0
                    act.activation(cols, psum[:, half, :], ACT.Identity, scale=scale, bias=bias).then_inc(stored, 1)
                act.wait_ge(stored, 2)

        if out is not None:
            @block.sync
            def _(sp):
                rows = out.rearrange("(t b) s d -> (b s) t d", b=2)
                for half in range(2):
                    sp.wait_ge(normed, TH * (half + 1))
                    sp.dma_start(rows[:, half * TH:(half + 1) * TH, :], dst[:, half * TH:(half + 1) * TH, :])\
                        .then_inc(stored, 16)
                sp.wait_ge(stored, 32)


def small_qkv(nc, ch, wq, wk, wv, srcq, srckv, bias=False, rotated=None):
    psum, par = ch["psum"], ch["params"]
    QK = (ch["QP"], ch["KP"])

    def packed(src, b):
        return src[:, :].rearrange("p (t b s) -> p b t s", b=2, s=S)[:, b]

    with ExitStack() as st:
        qk_done, qk_kept, v_done, v_kept, rot_done, rot_kept, mixed, mixed_k = stage_semaphores(
            nc, ch, "qk_done", "qk_kept", "v_done", "v_kept", "rot_done", "rot_kept", "mixed", "mixed_k")
        block = st.enter_context(stage_block(nc, ch))

        def four(pe, weights, done, free=None):
            for m in range(2):
                src = srcq if m == 0 else srckv
                for half in range(2):
                    if free is not None:
                        pe.wait_ge(free, 2 * m + half + 1)
                    for b in range(2):
                        mm = pe.matmul(psum[64 * b:64 * b + 64, 2 * m + half, :],
                                       weights[m][:, 64 * half:64 * half + 64], packed(src, b), start=True, stop=True)
                    mm.then_inc(done, 1)

        @block.tensor
        def _(pe):
            four(pe, (wq, wk), qk_done)
            for half in range(2):
                for i in range(TH):
                    mm = pe.matmul(psum[:, 4 + half, i * P:(i + 1) * P], srckv[:, tile_cols(half * TH + i)], wv,
                                   start=True, stop=True)
                mm.then_inc(v_done, 1)
            if rotated is not None:
                four(pe, rotated, rot_done, qk_kept)

        @block.scalar
        def _(act):
            for n in range(4):
                act.wait_ge(qk_done, n + 1)
                act.activation(QK[n // 2][:, n % 2, :], psum[:, n, :], ACT.Identity,
                               bias=par[:, 10 + n:11 + n] if bias else 0.0).then_inc(qk_kept, 1)
            if rotated is not None:
                for n in range(4):
                    act.wait_ge(rot_done, n + 1)
                    act.activation(ch["rot"][:, n, :], psum[:, n, :], ACT.Copy).then_inc(rot_kept, 1)
                act.wait_ge(rot_kept, 4)
            act.wait_ge(qk_kept, 4)

        @block.vector
        def _(dve):
            for half in range(2):
                dve.wait_ge(v_done, half + 1)
                v = ch["V"][:, half * TH:(half + 1) * TH, :]
                p = psum[:, 4 + half, :].rearrange("p (t d) -> p t d", d=D)
                if bias:
                    dve.tensor_tensor(v, p, ch["rows"][:, 0, :].unsqueeze(1).to_broadcast([P, TH, D]), ALU.add)\
                        .then_inc(v_kept, 1)
                else:
                    dve.tensor_copy(v, p).then_inc(v_kept, 1)
            if rotated is not None:
                for n in range(4):
                    x = QK[n // 2][:, n % 2, :].rearrange("p (t s) -> p t s", s=S)
                    r = ch["rot"][:, n, :].rearrange("p (t s) -> p t s", s=S)
                    dve.wait_ge(qk_kept, n + 1)
                    dve.tensor_tensor(x, x, ch["cos"][:, :].unsqueeze(1).to_broadcast([P, NT, S]), ALU.mult)\
                        .then_inc(mixed, 1)
                    dve.wait_ge(mixed_k, n + 1)
                    dve.wait_ge(mixed, 2 * n + 1)
                    dve.tensor_tensor(x, x, r, ALU.add).then_inc(mixed, 1)
                dve.wait_ge(mixed, 8)
            dve.wait_ge(v_kept, 2)

        if rotated is not None:
            @block.gpsimd
            def _(pool):
                for n in range(4):
                    r = ch["rot"][:, n, :].rearrange("p (t s) -> p t s", s=S)
                    pool.wait_ge(rot_kept, n + 1)
                    pool.tensor_tensor(r, r, ch["sin"][:, :].unsqueeze(1).to_broadcast([P, NT, S]), ALU.mult)\
                        .then_inc(mixed_k, 1)


def small_attention(nc, ch, causal=False, zero_keys=0, loads=()):
    psum = ch["psum"]
    scale = float(HD) ** -0.5
    Qd, Kx, Vd, Pr, Pn, PT, mx, den, rden = (ch[n] for n in ("Qd", "Kx", "Vd", "Pr", "Pn", "PT", "mx", "den", "rden"))
    pad, AT = ch["pad"], ch["AT"]
    with ExitStack() as st:
        (keys_spread, query_placed, scores_done, max_done, pad_max, centred, exp_done, pad_done, sum_done, sum_pad,
         inverse_done, probs_done, turned, turned_kept, values_placed, pv_done, out_kept, arrived) = stage_semaphores(
            nc, ch, "keys_spread", "query_placed", "scores_done", "max_done", "pad_max", "centred", "exp_done",
            "pad_done", "sum_done", "sum_pad", "inverse_done", "probs_done", "turned", "turned_kept",
            "values_placed", "pv_done", "out_kept", "arrived")
        block = st.enter_context(stage_block(nc, ch))

        def rounds(eng, before, step):
            before()
            step(0, 0)
            with eng.Fori(0, NT // 2 - 2) as i:
                step(2 * i + 1, 1)
                step(2 * i + 2, 0)
            for t in range(NT - 3, NT):
                step(t, t % 2)

        def has(t, ahead):
            return not isinstance(t, int) or 0 <= t + ahead < NT

        if loads:
            @block.sync
            def _(sp):
                for dst, src in loads:
                    sp.dma_start(dst, src).then_inc(arrived, 16)
                sp.wait_ge(arrived, 16 * len(loads))

        @block.gpsimd
        def _(pool):
            def spread_keys(t, s):
                pool.wait_ge(scores_done, t + 1)
                k = ch["KP"][:, :, tile_cols(t, S)]
                pool.tensor_tensor(Kx[:, s, :, :, :], k.unsqueeze(2).to_broadcast([P, 2, 8, S]),
                                   ch["head_of"][:, :].unsqueeze(1).unsqueeze(3).to_broadcast([P, 2, 8, S]),
                                   ALU.mult).then_inc(keys_spread, 1)

            def normalise(t, s):
                pool.wait_ge(inverse_done, t + 1)
                pool.wait_ge(turned, t + 1)
                pool.tensor_tensor(Pn[:, s, :, :], Pr[:, s, :, :],
                                   rden[:, s, :].unsqueeze(2).to_broadcast([P, H, S]), ALU.mult)\
                    .then_inc(probs_done, 1)

            def before():
                pool.sem_inc(probs_done, 2)
                spread_keys(0, 0)
                spread_keys(1, 1)
                spread_keys(2, 0)

            def step(t, s):
                normalise(t, s)
                if has(t, 3):
                    spread_keys(t + 3, 1 - s)

            rounds(pool, before, step)

        @block.scalar
        def _(act):
            def place_query(t, s):
                act.wait_ge(scores_done, t + 1)
                for b in range(2):
                    rows = slice(64 * b, 64 * b + 64)
                    act.activation(Qd[rows, s, :, 64 * b:64 * b + 64], ch["QP"][rows, :, tile_cols(t, S)], ACT.Copy)\
                        .then_inc(query_placed, 1)

            def place_values(t, s):
                act.wait_ge(pv_done, t + 1)
                for b in range(2):
                    for odd in range(2):
                        src = ch["V"][64 * b:64 * b + 64, bass.ds(t, 1), :].rearrange(
                            "p a (g m o d) -> p (a g) m o d", g=4, m=2, o=2)[:, :, :, odd, :]
                        dst = Vd[64 * odd:64 * odd + 64, s, b, :, :].rearrange("p g (a d) -> p g a d", d=HD)
                        act.activation(dst[:, :, odd:odd + 7:6, :], src, ACT.Copy).then_inc(values_placed, 1)

            def exponentials(t, s):
                act.wait_ge(centred, t + 3)
                act.activation(Pr[:, s, :, :], Pr[:, s, :, :], ACT.Exp, scale=scale).then_inc(exp_done, 1)
                if zero_keys:
                    act.activation(pad[:, s, :], mx[:, s, :], ACT.Exp, scale=-scale).then_inc(pad_done, 1)

            def keep_turned(t, s):
                act.wait_ge(turned, t + 3)
                act.wait_ge(pv_done, t + 1)
                for m in range(2):
                    act.activation(PT[:, s, 4 * m:4 * m + 4, :].rearrange("p h q -> p (h q)"), psum[:, 4 + m, :],
                                   ACT.Copy).then_inc(turned_kept, 1)

            def keep_out(t, s):
                act.wait_ge(pv_done, t + 3)
                act.activation(AT[:, tile_cols(t)], psum[:, 6 + s, 0:P], ACT.Copy).then_inc(out_kept, 1)

            def before():
                act.sem_inc(out_kept, 2)
                act.sem_inc(turned_kept, 2)
                place_query(0, 0)
                place_values(0, 0)
                place_query(1, 1)
                place_query(2, 0)
                exponentials(0, 0)

            def step(t, s):
                if has(t, 3):
                    place_query(t + 3, 1 - s)
                if has(t, 1):
                    exponentials(t + 1, 1 - s)
                if has(t, -1):
                    keep_out(t - 1, 1 - s)
                if has(t, 1):
                    place_values(t + 1, 1 - s)
                keep_turned(t, s)

            rounds(act, before, step)
            keep_out(NT - 1, (NT - 1) % 2)
            act.wait_ge(out_kept, NT + 2)

        @block.vector
        def _(dve):
            def scores_of(s):
                return psum[:, 2 * s:2 * s + 2, :].rearrange("p a (h k) -> p (a h) k", k=S)

            def find_max(t, s):
                dve.wait_ge(scores_done, t + 3)
                dve.tensor_reduce(mx[:, s, :], scores_of(s), AX, ALU.max).then_inc(max_done, 1)
                if zero_keys:
                    dve.wait_ge(max_done, t + 1)
                    dve.tensor_scalar(mx[:, s, :], mx[:, s, :], 0.0, None, ALU.max).then_inc(pad_max, 1)

            def centre(t, s):
                dve.wait_ge(pad_max if zero_keys else max_done, t + 1)
                dve.wait_ge(probs_done, t + 1)
                dve.tensor_tensor(Pr[:, s, :, :], scores_of(s), mx[:, s, :].unsqueeze(2).to_broadcast([P, H, S]),
                                  ALU.subtract).then_inc(centred, 1)

            def invert(t, s):
                dve.wait_ge(exp_done, t + 1)
                dve.tensor_reduce(den[:, s, :], Pr[:, s, :, :], AX, ALU.add).then_inc(sum_done, 1)
                dve.wait_ge(sum_done, t + 1)
                if zero_keys:
                    dve.wait_ge(pad_done, t + 1)
                    dve.scalar_tensor_tensor(out=den[:, s, :], in0=pad[:, s, :], scalar=float(zero_keys),
                                             in1=den[:, s, :], op0=ALU.mult, op1=ALU.add).then_inc(sum_pad, 1)
                    dve.wait_ge(sum_pad, t + 1)
                dve.reciprocal(rden[:, s, :], den[:, s, :]).then_inc(inverse_done, 1)

            def before():
                dve.sem_inc(centred, 2)
                find_max(0, 0)
                centre(0, 0)

            def step(t, s):
                if has(t, 1):
                    find_max(t + 1, 1 - s)
                invert(t, s)
                if has(t, 1):
                    centre(t + 1, 1 - s)

            rounds(dve, before, step)

        @block.tensor
        def _(pe):
            def scores(t, s):
                pe.wait_ge(keys_spread, t + 1)
                pe.wait_ge(query_placed, 2 * t + 2)
                pe.wait_ge(centred, t + 1)
                for half in range(2):
                    bank = psum[:, 2 * s + half, :]
                    if causal:
                        pe.matmul(bank, ch["identb"][:, :], ch["causal"][:, :].unsqueeze(1).to_broadcast([P, 8, S]),
                                  start=True, stop=False)
                    mm = pe.matmul(bank, Qd[:, s, half, :], Kx[:, s, half, :, :].rearrange("p h k -> p (h k)"),
                                   start=not causal, stop=True)
                mm.then_inc(scores_done, 1)

            def turn(t, s):
                pe.wait_ge(probs_done, t + 3)
                pe.wait_ge(turned_kept, 2 * t + 2)
                for hp in range(8):
                    mm = pe.transpose(psum[:, 4 + hp // 4, (hp % 4) * P:(hp % 4 + 1) * P],
                                      Pn[:, s, 2 * hp:2 * hp + 2, :].rearrange("p h k -> p (h k)"), ch["identf"][:, :])
                mm.then_inc(turned, 1)

            def values(t, s):
                pe.wait_ge(turned_kept, 2 * t + 4)
                pe.wait_ge(values_placed, 4 * t + 4)
                pe.wait_ge(out_kept, t + 1)
                for b in range(2):
                    for m in range(2):
                        for g in range(4):
                            mm = pe.matmul(psum[32 * g:32 * g + 32, 6 + s, 64 * b:64 * b + 64], Vd[:, s, b, g, 32 * m:32 * m + 32],
                                           PT[:, s, 2 * g + m, 64 * b:64 * b + 64], start=(m == 0), stop=(m == 1))
                mm.then_inc(pv_done, 1)

            def before():
                pe.sem_inc(scores_done, 2)
                pe.sem_inc(pv_done, 2)
                pe.sem_inc(turned, 2)
                scores(0, 0)
                scores(1, 1)

            def step(t, s):
                if has(t, 2):
                    scores(t + 2, s)
                if has(t, -1):
                    values(t - 1, 1 - s)
                turn(t, s)

            rounds(pe, before, step)
            values(NT - 1, (NT - 1) % 2)


def project_add(nc, ch, wo, dst, adds, featT=None, feat_bias=None):
    psum, AT = ch["psum"], ch["AT"]
    with ExitStack() as st:
        proj_done, added, feat_done, feat_kept = stage_semaphores(nc, ch, "proj_done", "added", "feat_done",
                                                                  "feat_kept")
        block = st.enter_context(stage_block(nc, ch))

        @block.tensor
        def _(pe):
            for half in range(2):
                for i in range(TH):
                    mm = pe.matmul(psum[:, half, i * P:(i + 1) * P], AT[:, tile_cols(half * TH + i)], wo,
                                   start=True, stop=True)
                mm.then_inc(proj_done, 1)
            if featT is not None:
                for half in range(2):
                    pe.matmul(psum[:, 2 + half, :], wo, AT[:, half * HALF:(half + 1) * HALF], start=True, stop=True)\
                        .then_inc(feat_done, 1)

        @block.vector
        def _(dve):
            n = 0
            for half in range(2):
                dve.wait_ge(proj_done, half + 1)
                cols = slice(half * TH, (half + 1) * TH)
                cur = psum[:, half, :].rearrange("p (t d) -> p t d", d=D)
                for a in adds:
                    if n and cur is not None and n % len(adds):
                        dve.wait_ge(added, n)
                    term = a[:, cols, :] if len(a.shape) == 3 else a.unsqueeze(1).to_broadcast([P, TH, D])
                    dve.tensor_tensor(dst[:, cols, :], cur, term, ALU.add).then_inc(added, 1)
                    cur = dst[:, cols, :]
                    n += 1
            dve.wait_ge(added, n)

        if featT is not None:
            @block.scalar
            def _(act):
                for half in range(2):
                    act.wait_ge(feat_done, half + 1)
                    act.activation(featT[:, half * HALF:(half + 1) * HALF], psum[:, 2 + half, :], ACT.Identity,
                                   bias=ch["params"][:, feat_bias:feat_bias + 1]).then_inc(feat_kept, 1)
                act.wait_ge(feat_kept, 2)


def inner_steps(nc, ch, steps=8, dt=0.1):
    psum, xs, ctx = ch["psum"], ch["XT"], ch["LT"]
    with ExitStack() as st:
        w, u, drift, slowed, pulled = (st.enter_context(nc.sbuf_tensor(n, [P, 2, HALF], F32))
                                       for n in ("w", "u", "drift", "slowed", "pulled"))
        pre_done, tanh_done, speed_done, state_done, parts_done, drift_done = (
            stage_semaphores(nc, ch, f"{n}0", f"{n}1") for n in
            ("pre_done", "tanh_done", "speed_done", "state_done", "parts_done", "drift_done"))
        (cleared,) = stage_semaphores(nc, ch, "cleared")
        block = st.enter_context(stage_block(nc, ch))

        def half_of(a, h):
            return a[:, h * HALF:(h + 1) * HALF]

        @block.tensor
        def _(pe):
            with pe.Fori(0, steps) as i:
                for h in range(2):
                    pe.wait_ge(tanh_done[h], i + 1)
                    pe.matmul(psum[:, h, :], ch["wctx"][:, :], half_of(ctx, h), start=True, stop=False)
                    pe.wait_ge(state_done[h], i + 1)
                    pe.matmul(psum[:, h, :], ch["wx"][:, :], half_of(xs, h), start=False, stop=True)\
                        .then_inc(pre_done[h], 1)

        @block.scalar
        def _(act):
            def parts(h, i):
                act.wait_ge(state_done[h], i + 1)
                act.wait_ge(drift_done[h], i + 1)
                act.activation(slowed[:, h, :], w[:, h, :], ACT.Copy, scale=1.0 - dt).then_inc(parts_done[h], 1)
                act.activation(pulled[:, h, :], half_of(xs, h), ACT.Copy, scale=dt * dt).then_inc(parts_done[h], 1)

            def squash(h, i):
                act.wait_ge(pre_done[h], i + 1)
                act.wait_ge(speed_done[h], i + 1)
                act.activation(u[:, h, :], psum[:, h, :], ACT.Tanh, bias=ch["params"][:, 6:7])\
                    .then_inc(tanh_done[h], 1)

            for h in range(2):
                act.sem_inc(tanh_done[h], 1)
            act.wait_ge(cleared, 1)
            parts(0, 0)
            with act.Fori(0, steps) as i:
                squash(0, i)
                parts(1, i)
                squash(1, i)
                parts(0, i + 1)

        @block.gpsimd
        def _(pool):
            def drifts(h, i):
                pool.wait_ge(parts_done[h], 2 * i + 2)
                pool.wait_ge(speed_done[h], i + 1)
                pool.tensor_tensor(drift[:, h, :], slowed[:, h, :], pulled[:, h, :], ALU.subtract)\
                    .then_inc(drift_done[h], 1)

            pool.memset(w[:, :, :], 0.0).then_inc(cleared, 1)
            for h in range(2):
                pool.sem_inc(drift_done[h], 1)
            drifts(0, 0)
            with pool.Fori(0, steps) as i:
                drifts(1, i)
                drifts(0, i + 1)

        @block.vector
        def _(dve):
            for h in range(2):
                dve.sem_inc(speed_done[h], 1)
                dve.sem_inc(state_done[h], 1)
            with dve.Fori(0, steps) as i:
                for h in range(2):
                    dve.wait_ge(tanh_done[h], i + 2)
                    dve.wait_ge(drift_done[h], i + 2)
                    dve.scalar_tensor_tensor(out=w[:, h, :], in0=u[:, h, :], scalar=dt * dt, in1=drift[:, h, :],
                                             op0=ALU.mult, op1=ALU.add).then_inc(speed_done[h], 1)
                    dve.wait_ge(speed_done[h], i + 2)
                    dve.tensor_tensor(half_of(xs, h), half_of(xs, h), w[:, h, :], ALU.add)\
                        .then_inc(state_done[h], 1)


def turn_add(nc, ch, featT, dst, add):
    psum = ch["psum"]
    with ExitStack() as st:
        turned, added = stage_semaphores(nc, ch, "turned", "added")
        block = st.enter_context(stage_block(nc, ch))

        @block.tensor
        def _(pe):
            for half in range(2):
                for i in range(TH):
                    mm = pe.transpose(psum[:, half, i * P:(i + 1) * P], featT[:, tile_cols(half * TH + i)],
                                      ch["identf"][:, :])
                mm.then_inc(turned, 1)

        @block.vector
        def _(dve):
            for half in range(2):
                dve.wait_ge(turned, half + 1)
                cols = slice(half * TH, (half + 1) * TH)
                dve.tensor_tensor(dst[:, cols, :], psum[:, half, :].rearrange("p (t d) -> p t d", d=D),
                                  add[:, cols, :], ALU.add).then_inc(added, 1)
            dve.wait_ge(added, 2)


def gelu_mlp(nc, ch, x0, x2, dst):
    psum, XT = ch["psum"], ch["XT"]
    with ExitStack() as st:
        hidden = st.enter_context(nc.sbuf_tensor("hidden", [P, NC, NTOK], F32))
        up_done, gelu_done, down_done, rest_done, added = stage_semaphores(
            nc, ch, "up_done", "gelu_done", "down_done", "rest_done", "added")
        absum_done, total_done, scaled, ternary, ctx_turned, ctx_kept, yw_turned, ternary_turned, ready, prepared, w_high = \
            stage_semaphores(nc, ch, "absum_done", "total_done", "scaled", "ternary", "ctx_turned", "ctx_kept",
                             "yw_turned", "ternary_turned", "ready", "prepared", "w_high")
        block = st.enter_context(stage_block(nc, ch))

        @block.tensor
        def _(pe):
            def up(half):
                for c in range(NC):
                    if half:
                        pe.wait_ge(gelu_done, c + 1)
                    pe.matmul(psum[:, c, :], ch["ffw1"][:, c * P:(c + 1) * P], XT[:, half * HALF:(half + 1) * HALF],
                              start=True, stop=True).then_inc(up_done, 1)

            def down(half):
                pe.wait_ge(gelu_done, NC * (half + 1))
                for i in range(TH):
                    for c in range(NC):
                        mm = pe.matmul(psum[:, 4 + half, i * P:(i + 1) * P], hidden[:, c, tile_cols(half * TH + i)],
                                       ch["ffw2"][:, c, :], start=(c == 0), stop=(c == NC - 1))
                mm.then_inc(down_done, 1)

            up(0)
            for half in range(2):
                for i in range(TH):
                    mm = pe.transpose(psum[:, 6 + half, i * P:(i + 1) * P], ch["C"][:, half * TH + i, :],
                                      ch["identf"][:, :])
                mm.then_inc(ctx_turned, 1)
            pe.wait_ge(absum_done, 2)
            pe.matmul(psum[:, 5, 0:2], ch["ones"][:, :], ch["absum"][:, :], start=True, stop=True).then_inc(total_done, 1)
            up(1)
            pe.wait_ge(ctx_kept, 1)
            for i in range(4):
                mm = pe.transpose(psum[:, 6, i * P:(i + 1) * P], ch["ywo"][:, i, :], ch["identf"][:, :])
            mm.then_inc(yw_turned, 1)
            down(0)
            pe.wait_ge(ternary, 2)
            pe.wait_ge(ctx_kept, 2)
            for m in range(2):
                for c in range(NC):
                    at = m * FF // 2 + c * 64
                    mm = pe.transpose(psum[:, 7, at:at + 64].bitcast(BF16), ch["wtern"][:, m, c * P:(c + 1) * P],
                                      ch["identb"][:, :])
            mm.then_inc(ternary_turned, 1)
            pe.wait_ge(scaled, 1)
            down(1)

        @block.scalar
        def _(act):
            def gelu(half):
                for c in range(NC):
                    act.wait_ge(up_done, half * NC + c + 1)
                    act.activation(hidden[:, c, half * HALF:(half + 1) * HALF], psum[:, c, :], ACT.Gelu,
                                   bias=ch["params"][:, 14 + c:15 + c]).then_inc(gelu_done, 1)

            gelu(0)
            for half in range(2):
                act.wait_ge(ctx_turned, half + 1)
                act.activation(ch["CT"][:, half * HALF:(half + 1) * HALF], psum[:, 6 + half, :], ACT.Copy)\
                    .then_inc(ctx_kept, 1)
            gelu(1)
            act.wait_ge(yw_turned, 1)
            act.activation(ch["yw"][:, :], psum[:, 6, :], ACT.Copy).then_inc(ready, 1)
            act.wait_ge(ternary_turned, 1)
            act.activation(ch["wternT"][:, :, :].rearrange("p m f -> p (m f)"), psum[:, 7, :].bitcast(BF16), ACT.Copy)\
                .then_inc(ready, 1)
            act.wait_ge(ready, 2)

        @block.vector
        def _(dve):
            w1, w2 = ch["bw1"][:, :, :].rearrange("p c d -> p (c d)"), ch["bw2"][:, :]
            for m, w in enumerate((w1, w2)):
                dve.tensor_reduce(ch["absum"][:, m:m + 1], w, AX, ALU.add, apply_absolute_value=True)\
                    .then_inc(absum_done, 1)
            dve.tensor_tensor(dst[:, :, :], x0[:, :, :], x2[:, :, :], ALU.add).then_inc(rest_done, 1)
            dve.wait_ge(rest_done, 1)
            dve.tensor_tensor(dst[:, :, :], dst[:, :, :], ch["rows"][:, 2, :].unsqueeze(1).to_broadcast([P, NT, D]),
                              ALU.add).then_inc(rest_done, 1)
            dve.wait_ge(total_done, 1)
            dve.tensor_scalar(ch["wmean"][:, :], psum[:, 5, 0:2], 1.0 / (FF * D), 1e-5, ALU.mult, ALU.max)\
                .then_inc(scaled, 1)
            dve.wait_ge(scaled, 1)
            dve.reciprocal(ch["winv"][:, :], ch["wmean"][:, :]).then_inc(scaled, 1)
            dve.wait_ge(scaled, 2)
            for m, w in enumerate((w1, w2)):
                dve.tensor_scalar(w, w, ch["winv"][:, m:m + 1], ROUND, ALU.mult, ALU.add).then_inc(scaled, 1)
                dve.wait_ge(scaled, 3 + 2 * m)
                dve.tensor_scalar(w, w, -ROUND, 1.0, ALU.add, ALU.min).then_inc(scaled, 1)
                dve.wait_ge(scaled, 4 + 2 * m)
                dve.tensor_scalar(ch["wtern"][:, m, :], w, -1.0, None, ALU.max).then_inc(ternary, 1)
            dve.wait_ge(rest_done, 2)
            for half in range(2):
                dve.wait_ge(down_done, half + 1)
                cols = slice(half * TH, (half + 1) * TH)
                dve.tensor_tensor(dst[:, cols, :], psum[:, 4 + half, :].rearrange("p (t d) -> p t d", d=D),
                                  dst[:, cols, :], ALU.add).then_inc(added, 1)
            dve.wait_ge(added, 2)

        @block.gpsimd
        def _(pool):
            for m in range(2):
                pool.tensor_copy(ch["xwkr"][:, m, :].rearrange("p (h d) -> p h d", d=HD),
                                 ch["xwkv"][:, m * HD:(m + 1) * HD].unsqueeze(1).to_broadcast([P, H, HD]))\
                    .then_inc(prepared, 1)
            for m, w in enumerate(("mwq", "mwk")):
                src = ch[w][:, :].rearrange("p (h r d) -> p h r d", r=2, d=HD // 2)
                turned = ch["mrot"][:, m, :].rearrange("p (h r d) -> p h r d", r=2, d=HD // 2)
                pool.tensor_scalar(turned[:, :, 0, :], src[:, :, 1, :], -1.0, None, ALU.mult).then_inc(prepared, 1)
                pool.tensor_copy(turned[:, :, 1, :], src[:, :, 0, :]).then_inc(prepared, 1)
            for e in range(2):
                pool.tensor_copy(ch["WH"][:, e, :], ch["We"][:, e, :]).then_inc(w_high, 1)
                pool.wait_ge(w_high, e + 1)
                pool.tensor_tensor(ch["WL"][:, e, :], ch["We"][:, e, :], ch["WH"][:, e, :].bitcast(F32), ALU.subtract)\
                    .then_inc(prepared, 1)
            pool.wait_ge(prepared, 8)


def quantize(dve, chain, at, dst, src, tmp, scale, clipped=True):
    dve.tensor_scalar(tmp, src, scale, ROUND, ALU.mult, ALU.add).then_inc(chain, 1)
    dve.wait_ge(chain, at + 1)
    dve.tensor_scalar(tmp, tmp, ROUND + 127.0, ROUND - 128.0, ALU.min, ALU.max).then_inc(chain, 1)
    dve.wait_ge(chain, at + 2)
    return dve.tensor_scalar(dst, tmp, -ROUND, None, ALU.add)


def quantized_ffn(nc, ch, x, dst):
    psum, identf, identb = ch["psum"], ch["identf"], ch["identb"]
    wT = ch["wternT"]
    w1T, w2T = wT[:, 0, :], wT[:, 1, :].rearrange("p (c d) -> p c d", d=D)
    with ExitStack() as st:
        def sb(n, shape, dt=F32):
            return st.enter_context(nc.sbuf_tensor(n, [P, *shape], dt))

        xq, xqT = sb("xq", [NT, D], BF16), sb("xqT", [NTOK], BF16)
        tmp, row_scale = sb("tmp", [NTOK]), sb("row_scale", [NTOK])
        amax, inv, back = sb("amax", [2, NT]), sb("inv", [2, NT]), sb("back", [2, NT])
        grid, mix = sb("grid", [2, NTOK]), sb("mix", [NC, NTOK])
        hq, hqT = sb("hq", [2, FF], BF16), sb("hqT", [2, FF], BF16)
        htmp = sb("htmp", [2, FF])
        (chain, x_quantized, x_turned, x_kept, rows_done, rows_kept, hid_done, grid_done, centre_done, conv_done,
         silu_done, h_turned, h_quantized, hq_turned, hq_kept, down_done, added) = stage_semaphores(
            nc, ch, "chain", "x_quantized", "x_turned", "x_kept", "rows_done", "rows_kept", "hid_done", "grid_done",
            "centre_done", "conv_done", "silu_done", "h_turned", "h_quantized", "hq_turned", "hq_kept", "down_done",
            "added")
        block = st.enter_context(stage_block(nc, ch))
        UNITS = 2 * NC

        def seqs(a, c, half):
            return a[:, c, half * HALF:(half + 1) * HALF].rearrange("p (b s) -> p b s", s=S)

        def add_tile(dve, t):
            dve.wait_ge(down_done, t + 1)
            dve.scalar_tensor_tensor(out=dst[:, t, :], in0=psum[:, 6 + t % 2, 0:D], scalar=back[:, 1, t:t + 1],
                                     in1=x[:, t, :], op0=ALU.mult, op1=ALU.add).then_inc(added, 1)

        @block.vector
        def _(dve):
            n = 0

            def own(ins):
                nonlocal n
                ins.then_inc(chain, 1)
                n += 1
                dve.wait_ge(chain, n)

            own(dve.tensor_reduce(amax[:, 0, :], x[:, :, :], AX, ALU.max, apply_absolute_value=True))
            own(dve.tensor_scalar(amax[:, 0, :], amax[:, 0, :], 1e-5, None, ALU.max))
            own(dve.reciprocal(inv[:, 0, :], amax[:, 0, :]))
            own(dve.tensor_scalar(inv[:, 0, :], inv[:, 0, :], 127.0, None, ALU.mult))
            own(dve.tensor_scalar(back[:, 0, :], amax[:, 0, :], ch["wmean"][:, 0:1], 1.0 / 127.0, ALU.mult, ALU.mult))
            for t in range(NT):
                own(dve.tensor_scalar(tmp[:, tile_cols(t)], x[:, t, :], inv[:, 0, t:t + 1], ROUND, ALU.mult, ALU.add))
            own(dve.tensor_scalar(tmp[:, :], tmp[:, :], ROUND + 127.0, ROUND - 128.0, ALU.min, ALU.max))
            dve.tensor_scalar(xq[:, :, :].rearrange("p t d -> p (t d)"), tmp[:, :], -ROUND, None, ALU.add)\
                .then_inc(x_quantized, 1)
            for u in range(UNITS):
                c, half = divmod(u, 2)
                dve.wait_ge(rows_kept, 2)
                dve.wait_ge(hid_done, u + 1)
                if u >= 2:
                    dve.wait_ge(centre_done, u - 1)
                cols = slice(half * HALF, (half + 1) * HALF)
                dve.tensor_tensor(grid[:, u % 2, 0:HALF], psum[:, u % 2, :], row_scale[:, cols], ALU.mult)\
                    .then_inc(grid_done, 1)
                dve.wait_ge(grid_done, u + 1)
                dve.wait_ge(centre_done, u + 1)
                g = grid[:, u % 2, 0:HALF].rearrange("p (b s) -> p b s", s=S)
                y = seqs(mix, c, half)
                dve.scalar_tensor_tensor(out=y[:, :, 1:S], in0=g[:, :, 0:S - 1], scalar=ch["convw"][:, c, 0:1],
                                         in1=y[:, :, 1:S], op0=ALU.mult, op1=ALU.add).then_inc(conv_done, 1)
                dve.wait_ge(conv_done, 2 * u + 1)
                dve.scalar_tensor_tensor(out=y[:, :, 0:S - 1], in0=g[:, :, 1:S], scalar=ch["convw"][:, c, 2:3],
                                         in1=y[:, :, 0:S - 1], op0=ALU.mult, op1=ALU.add).then_inc(conv_done, 1)
            for t in range(NT):
                s = t % 2
                dve.wait_ge(h_turned, t + 1)
                own(dve.tensor_reduce(amax[:, 1, t:t + 1], psum[:, 2 + s, :], AX, ALU.max, apply_absolute_value=True))
                own(dve.tensor_scalar(amax[:, 1, t:t + 1], amax[:, 1, t:t + 1], 1e-5, None, ALU.max))
                own(dve.reciprocal(inv[:, 1, t:t + 1], amax[:, 1, t:t + 1]))
                own(dve.tensor_scalar(inv[:, 1, t:t + 1], inv[:, 1, t:t + 1], 127.0, None, ALU.mult))
                own(dve.tensor_scalar(back[:, 1, t:t + 1], amax[:, 1, t:t + 1], ch["wmean"][:, 1:2], 1.0 / 127.0,
                                      ALU.mult, ALU.mult))
                quantize(dve, chain, n, hq[:, s, :], psum[:, 2 + s, :], htmp[:, s, :], inv[:, 1, t:t + 1])\
                    .then_inc(h_quantized, 1)
                n += 2
                if t:
                    add_tile(dve, t - 1)
            add_tile(dve, NT - 1)
            dve.wait_ge(added, NT)

        @block.scalar
        def _(act):
            act.wait_ge(x_turned, 1)
            act.activation(xqT[:, :], psum[:, 4, :].bitcast(BF16), ACT.Copy).then_inc(x_kept, 1)
            for half in range(2):
                act.wait_ge(rows_done, half + 1)
                act.activation(row_scale[:, half * HALF:(half + 1) * HALF], psum[:, 6 + half, :], ACT.Copy)\
                    .then_inc(rows_kept, 1)

            def silu(u):
                c, half = divmod(u, 2)
                act.wait_ge(conv_done, 2 * u + 2)
                a = mix[:, c, half * HALF:(half + 1) * HALF]
                act.activation(a, a, ACT.Silu).then_inc(silu_done, 1)

            for u in range(UNITS):
                c, half = divmod(u, 2)
                act.wait_ge(grid_done, u + 1)
                act.activation(mix[:, c, half * HALF:(half + 1) * HALF], grid[:, u % 2, 0:HALF], ACT.Identity,
                               scale=ch["convw"][:, c, 1:2], bias=ch["params"][:, 14 + NC + c:15 + NC + c]).then_inc(centre_done, 1)
                if u:
                    silu(u - 1)
            silu(UNITS - 1)
            for t in range(NT):
                act.wait_ge(hq_turned, t + 1)
                if t >= 2:
                    act.wait_ge(down_done, t - 1)
                act.activation(hqT[:, t % 2, :], psum[:, 4 + t % 2, 0:FF // 2].bitcast(BF16), ACT.Copy)\
                    .then_inc(hq_kept, 1)

        @block.tensor
        def _(pe):
            pe.wait_ge(x_quantized, 1)
            for t in range(NT):
                mm = pe.transpose(psum[:, 4, t * 64:(t + 1) * 64].bitcast(BF16), xq[:, t, :], identb[:, :])
            mm.then_inc(x_turned, 1)
            for half in range(2):
                for i in range(TH):
                    t = half * TH + i
                    mm = pe.matmul(psum[:, 6 + half, i * P:(i + 1) * P], back[:, 0, t:t + 1].to_broadcast([P, P]),
                                   identf[:, :], start=True, stop=True)
                mm.then_inc(rows_done, 1)
            pe.wait_ge(x_kept, 1)
            for u in range(UNITS):
                c, half = divmod(u, 2)
                if u >= 2:
                    pe.wait_ge(grid_done, u - 1)
                pe.matmul(psum[:, u % 2, :], w1T[:, c * P:(c + 1) * P], xqT[:, half * HALF:(half + 1) * HALF],
                          start=True, stop=True).then_inc(hid_done, 1)

            def turn_hidden(t):
                pe.wait_ge(silu_done, UNITS - 1 if t < TH else UNITS)
                if t >= 2:
                    pe.wait_ge(h_quantized, t - 1)
                for c in range(NC):
                    mm = pe.transpose(psum[:, 2 + t % 2, c * P:(c + 1) * P], mix[:, c, tile_cols(t)], identf[:, :])
                mm.then_inc(h_turned, 1)

            turn_hidden(0)
            for t in range(NT):
                if t + 1 < NT:
                    turn_hidden(t + 1)
                pe.wait_ge(h_quantized, t + 1)
                pe.wait_ge(rows_kept, 2)
                if t >= 2:
                    pe.wait_ge(hq_kept, t - 1)
                for c in range(NC):
                    mm = pe.transpose(psum[:, 4 + t % 2, c * 64:(c + 1) * 64].bitcast(BF16),
                                      hq[:, t % 2, c * P:(c + 1) * P], identb[:, :])
                mm.then_inc(hq_turned, 1)
                pe.wait_ge(hq_kept, t + 1)
                if t >= 2:
                    pe.wait_ge(added, t - 1)
                for c in range(NC):
                    mm = pe.matmul(psum[:, 6 + t % 2, 0:D], hqT[:, t % 2, c * P:(c + 1) * P], w2T[:, c, :],
                                   start=(c == 0), stop=(c == NC - 1))
                mm.then_inc(down_done, 1)


def wide_attention(nc, ch, w_qkv, w_o, dst):
    psum, XT = ch["psum"], ch["XT"]
    Pr, PT, mx, den, rden = (ch[n] for n in ("Pr", "PT", "mx", "den", "rden"))
    with ExitStack() as st:
        def sb(n, shape):
            return st.enter_context(nc.sbuf_tensor(n, [P, *shape], F32))

        W, Wo = sb("W", [2, 3, 2, N1]), sb("Wo", [2, D])
        QK, Vp, ctx = sb("QK", [2, 2, NTOK]), sb("Vp", [2, 2, NT, N1]), sb("ctx", [2, NTOK])
        loaded = stage_semaphores(nc, ch, "loaded0", "loaded1")
        loaded_out = stage_semaphores(nc, ch, "loaded_out0", "loaded_out1")
        (qk_done, qk_kept, v_done, v_kept, scores_done, max_done, centred, exp_done, sum_done, inverse_done,
         probs_done, turned, turned_kept, pv_done, ctx_kept, out_done, added) = stage_semaphores(
            nc, ch, "qk_done", "qk_kept", "v_done", "v_kept", "scores_done", "max_done", "centred", "exp_done",
            "sum_done", "inverse_done", "probs_done", "turned", "turned_kept", "pv_done", "ctx_kept", "out_done",
            "added")
        (waited,) = stage_semaphores(nc, ch, "waited")
        block = st.enter_context(stage_block(nc, ch))

        def pairs(eng, before, step):
            before()
            with eng.Fori(0, NP1 // 2 - 1) as i:
                step(2 * i, i, 0, True, True)
                step(2 * i + 1, i, 1, True, True)
            step(NP1 - 2, NP1 // 2 - 1, 0, True, False)
            step(NP1 - 1, NP1 // 2 - 1, 1, False, False)

        @block.sync
        def _(sp):
            def load(j, s):
                sp.wait_ge(v_done, 2 * j + 2)
                for par in range(2):
                    h = 2 * j + par
                    sp.dma_start(W[:, s, :, par, :], w_qkv[bass.ds(h, 1)].rearrange("h a v n -> v (h a) n"))\
                        .then_inc(loaded[s], 16)
                sp.wait_ge(out_done, j + 1)
                sp.dma_start(Wo[:, s, :], w_o[bass.ds(j * P, P), :]).then_inc(loaded_out[s], 16)

            load(0, 0)
            load(1, 1)
            with sp.Fori(1, NP1 // 2) as i:
                load(2 * i, 0)
                load(2 * i + 1, 1)

        @block.tensor
        def _(pe):
            def project(j, i, s):
                pe.wait_ge(loaded[s], 32 * i + 32)
                pe.wait_ge(ctx_kept, 2 * j + 2)
                for m in range(2):
                    for half in range(2):
                        pe.wait_ge(qk_kept, 4 * j + 2 * m + half + 3)
                        pe.matmul(psum[:, half, :], W[:, s, m, :, :].rearrange("p a n -> p (a n)"),
                                  XT[:, half * HALF:(half + 1) * HALF], start=True, stop=True).then_inc(qk_done, 1)

            def project_values(j, s):
                pe.wait_ge(v_kept, 4 * j + 4)
                for half in range(2):
                    for i4 in range(TH):
                        mm = pe.matmul(psum[:, 2 + half, i4 * P:(i4 + 1) * P], XT[:, tile_cols(half * TH + i4)],
                                       W[:, s, 2, :, :].rearrange("p a n -> p (a n)"), start=True, stop=True)
                    mm.then_inc(v_done, 1)

            def scores(j, s):
                pe.wait_ge(qk_kept, 4 * j + 8)
                pe.wait_ge(centred, j + 1)
                pe.sem_inc(waited, 1)
                for t in range(NT):
                    for b in range(2):
                        for par in range(2):
                            rows, cols = slice(64 * par, 64 * par + 64), slice(t * P + 64 * b, t * P + 64 * b + 64)
                            mm = pe.matmul(psum[64 * b:64 * b + 64, 4 + par, t * S:(t + 1) * S],
                                           QK[rows, s, 0, cols], QK[rows, s, 1, cols], start=True, stop=True)
                mm.then_inc(scores_done, 1)

            def turn(j, s):
                pe.wait_ge(probs_done, j + 1)
                pe.wait_ge(added, 2 * j + 2)
                for t in range(NT):
                    mm = pe.transpose(psum[:, 6 + t // TH, (t % TH) * P:(t % TH + 1) * P],
                                      Pr[:, s, 2 * t:2 * t + 2, :].rearrange("p a k -> p (a k)"), ch["identf"][:, :])
                mm.then_inc(turned, 1)

            def values(j, s, ahead):
                pe.wait_ge(turned_kept, 2 * j + 2)
                pe.wait_ge(v_kept, 4 * j + 8)
                pe.wait_ge(qk_kept, 4 * j + 8 + 4 * ahead)
                pe.sem_inc(waited, 1)
                for t in range(NT):
                    for b in range(2):
                        for par in range(2):
                            rows = slice(64 * par, 64 * par + 64)
                            col = (t % TH) * P + 64 * b
                            mm = pe.matmul(psum[rows, t // TH, col:col + 64], Vp[rows, s, b, t, :],
                                           PT[rows, s, t, 64 * b:64 * b + 64], start=True, stop=True)
                mm.then_inc(pv_done, 1)

            def output(j, i, s):
                pe.wait_ge(loaded_out[s], 16 * i + 16)
                pe.wait_ge(ctx_kept, 2 * j + 6)
                for half in range(2):
                    for i4 in range(TH):
                        mm = pe.matmul(psum[:, 6 + half, i4 * P:(i4 + 1) * P], ctx[:, s, tile_cols(half * TH + i4)],
                                       Wo[:, s, :], start=True, stop=True)
                mm.then_inc(out_done, 1)

            def before():
                pe.sem_inc(out_done, 2)
                pe.sem_inc(v_done, 4)
                pe.sem_inc(scores_done, 2)
                pe.sem_inc(pv_done, 2)
                pe.sem_inc(turned, 2)
                project(0, 0, 0)
                project_values(0, 0)
                scores(0, 0)

            def step(j, i, s, one, two):
                if one:
                    project(j + 1, i + s, 1 - s)
                turn(j, s)
                if one:
                    project_values(j + 1, 1 - s)
                values(j, s, 1 if one else 0)
                if one:
                    scores(j + 1, 1 - s)
                output(j, i, s)

            pairs(pe, before, step)

        @block.scalar
        def _(act):
            def keep_qk(j, s):
                act.wait_ge(scores_done, j + 1)
                for m in range(2):
                    for half in range(2):
                        act.wait_ge(qk_done, 4 * j + 2 * m + half + 1)
                        act.activation(QK[:, s, m, half * HALF:(half + 1) * HALF], psum[:, half, :], ACT.Copy)\
                            .then_inc(qk_kept, 1)

            def keep_values(j, s):
                act.wait_ge(pv_done, j + 1)
                act.wait_ge(v_done, 2 * j + 6)
                v = psum[:, 2:4, :].rearrange("p a (t c n) -> p (a t) c n", c=2, n=N1)
                for b in range(2):
                    for par in range(2):
                        act.activation(Vp[64 * par:64 * par + 64, s, b, :, :], v[64 * b:64 * b + 64, :, par, :],
                                       ACT.Copy).then_inc(v_kept, 1)

            def exponentials(j, s):
                act.wait_ge(centred, j + 2)
                act.activation(Pr[:, s, :, :], Pr[:, s, :, :], ACT.Exp, scale=float(N1) ** -0.5).then_inc(exp_done, 1)

            def keep_turned(j, s):
                act.wait_ge(turned, j + 3)
                act.wait_ge(pv_done, j + 1)
                for m in range(2):
                    act.activation(PT[:, s, 4 * m:4 * m + 4, :].rearrange("p h q -> p (h q)"), psum[:, 6 + m, :],
                                   ACT.Copy).then_inc(turned_kept, 1)

            def before():
                act.sem_inc(qk_kept, 4)
                act.sem_inc(v_kept, 4)
                keep_qk(0, 0)
                keep_values(0, 0)

            def step(j, i, s, one, two):
                exponentials(j, s)
                if one:
                    keep_qk(j + 1, 1 - s)
                keep_turned(j, s)
                if one:
                    keep_values(j + 1, 1 - s)

            pairs(act, before, step)

        @block.gpsimd
        def _(pool):
            def step(j, i, s, one, two):
                pool.wait_ge(inverse_done, j + 1)
                pool.tensor_tensor(Pr[:, s, :, :], Pr[:, s, :, :], rden[:, s, :].unsqueeze(2).to_broadcast([P, 16, S]),
                                   ALU.mult).then_inc(probs_done, 1)

            pairs(pool, lambda: None, step)

        @block.vector
        def _(dve):
            def centre(j, s):
                dve.wait_ge(scores_done, j + 3)
                sc = psum[:, 4:6, :].rearrange("p a (t k) -> p a t k", k=S)
                dve.tensor_reduce(mx[:, s, :].rearrange("p (a t) -> p a t", a=2), sc, AX, ALU.max)\
                    .then_inc(max_done, 1)
                dve.wait_ge(max_done, j + 1)
                dve.wait_ge(turned, j + 1)
                m = mx[:, s, :].rearrange("p (a t) -> p a t", a=2).unsqueeze(3).to_broadcast([P, 2, NT, S])
                dve.tensor_tensor(Pr[:, s, :, :].rearrange("p (t a) k -> p a t k", a=2), sc, m, ALU.subtract)\
                    .then_inc(centred, 1)

            def before():
                dve.sem_inc(centred, 1)
                dve.sem_inc(ctx_kept, 4)
                dve.sem_inc(added, 2)
                centre(0, 0)

            def step(j, i, s, one, two):
                dve.wait_ge(exp_done, j + 1)
                dve.tensor_reduce(den[:, s, :], Pr[:, s, :, :], AX, ALU.add).then_inc(sum_done, 1)
                dve.wait_ge(sum_done, j + 1)
                dve.reciprocal(rden[:, s, :], den[:, s, :]).then_inc(inverse_done, 1)
                dve.wait_ge(pv_done, j + 3)
                dve.wait_ge(out_done, j + 1)
                for half in range(2):
                    dve.tensor_copy(ctx[:, s, half * HALF:(half + 1) * HALF], psum[:, half, :])\
                        .then_inc(ctx_kept, 1)
                if one:
                    centre(j + 1, 1 - s)
                dve.wait_ge(out_done, j + 3)
                for half in range(2):
                    rows = dst[:, half * TH:(half + 1) * TH, :]
                    dve.wait_ge(added, 2 * j + half + 1)
                    dve.tensor_tensor(rows, psum[:, 6 + half, :].rearrange("p (t d) -> p t d", d=D), rows, ALU.add)\
                        .then_inc(added, 1)

            pairs(dve, before, step)


def split_product(pe, out, lhs, rhs, start=True, stop=True):
    (lhs_high, lhs_low), (rhs_high, rhs_low) = lhs, rhs
    pe.matmul(out, lhs_high, rhs_high, start=start, stop=False)
    pe.matmul(out, lhs_high, rhs_low, start=False, stop=False)
    return pe.matmul(out, lhs_low, rhs_high, start=False, stop=stop)


def experts(nc, ch, wg, wu, wd, dst):
    psum, XT, comb = ch["psum"], ch["XT"], ch["comb"]
    W, Wd, WH, WL = ch["We"], ch["Wd"], ch["WH"], ch["WL"]
    with ExitStack() as st:
        def sb(n, shape, dt=F32):
            return st.enter_context(nc.sbuf_tensor(f"{n}_{ch.stage}", [P, *shape], dt))

        XH, XL = sb("XH", [NTOK], F32R), sb("XL", [NTOK], F32R)
        rows = (XH, XL)
        sg, prod = sb("sg", [HC, HALF]), sb("prod", [2, HC, HALF])
        prob, top, at, atf = sb("prob", [NT, NE]), sb("top", [NT, 8]), sb("at", [NT, 8], U32), sb("atf", [NT, 8])
        hi, total, pick, iota = sb("hi", [NT]), sb("total", [NT]), sb("pick", [2, NT, NE]), ch["iota8"]
        loaded = stage_semaphores(nc, ch, "loaded0", "loaded1")
        logits_done, chain, exp_done = stage_semaphores(nc, ch, "logits_done", "chain", "exp_done")
        w_high, w_low, x_high, x_low = stage_semaphores(nc, ch, "w_high", "w_low", "x_high", "x_low")
        gate_done, up_done, silu_done, prod_done, down_done, added = stage_semaphores(
            nc, ch, "gate_done", "up_done", "silu_done", "prod_done", "down_done", "added")
        block = st.enter_context(stage_block(nc, ch))

        def units(eng, step):
            with eng.Fori(0, NE // 2 - 1) as i:
                for k in range(4):
                    step(4 * i + k, i, k, True)
            for k in range(4):
                step(2 * NE - 4 + k, NE // 2 - 1, k, k < 3)

        def parts(high, low, *at):
            return high[at], low[at]

        @block.sync
        def _(sp):
            def load(e, s):
                for n, w in enumerate((wg, wu)):
                    sp.dma_start(W[:, s, n * HID:(n + 1) * HID].unsqueeze(1),
                                 w[bass.ds(e, 1)].rearrange("e d n -> d e n")).then_inc(loaded[s], 16)
                sp.dma_start(Wd[:, s, :, :], wd[bass.ds(e, 1)].rearrange("e (c p) d -> p (e c) d", p=P))\
                    .then_inc(loaded[s], 16)

            with sp.Fori(1, NE // 2) as i:
                for s in range(2):
                    sp.wait_ge(down_done, 4 * i + 2 * s)
                    load(2 * i + s, s)

        @block.gpsimd
        def _(pool):
            def split(i, s):
                pool.wait_ge(loaded[s], 48 * i)
                pool.tensor_tensor(WH[:, s, :], W[:, s, :], ch["ones"][:, 0:1].to_broadcast([P, 2 * HID]), ALU.mult).then_inc(w_high, 1)
                pool.wait_ge(w_high, 2 * i + s + 1)
                pool.tensor_tensor(WL[:, s, :], W[:, s, :], WH[:, s, :].bitcast(F32), ALU.subtract).then_inc(w_low, 1)

            pool.sem_inc(w_high, 2)
            pool.sem_inc(w_low, 2)
            with pool.Fori(1, NE // 2) as i:
                split(i, 0)
                split(i, 1)

        @block.tensor
        def _(pe):
            def up(u, i, k):
                s, half = (k // 2) % 2, k % 2
                pe.wait_ge(x_low, half + 1)
                pe.wait_ge(w_low, 2 * i + s + 1)
                rhs = parts(*rows, slice(None), slice(half * HALF, (half + 1) * HALF))
                for c in range(HC):
                    gate = parts(WH, WL, slice(None), s, slice(c * P, (c + 1) * P))
                    lift = parts(WH, WL, slice(None), s, slice(HID + c * P, HID + (c + 1) * P))
                    pe.wait_ge(silu_done, 3 * u + c + 1)
                    split_product(pe, psum[:, c, :], gate, rhs).then_inc(gate_done, 1)
                    pe.wait_ge(prod_done, 3 * u + c + 1)
                    split_product(pe, psum[:, HC + c, :], lift, rhs).then_inc(up_done, 1)

            def down(u, k):
                s = k // 2
                pe.wait_ge(prod_done, 3 * u + 6)
                pe.wait_ge(added, 4 * u + 4)
                for i4 in range(TH):
                    for c in range(HC):
                        mm = pe.matmul(psum[:, 6 + k % 2, i4 * P:(i4 + 1) * P], prod[:, k % 2, c, tile_cols(i4)],
                                       Wd[:, s, c, :], start=(c == 0), stop=(c == HC - 1))
                mm.then_inc(down_done, 1)

            def step(u, i, k, ahead):
                if ahead:
                    up(u + 1, i + (k + 1) // 4, (k + 1) % 4)
                down(u, k)

            for t in range(NT):
                mm = pe.matmul(psum[:, 7, t * NE:(t + 1) * NE], XT[:, tile_cols(t)], ch["wrout"][:, :], start=True,
                               stop=True)
            mm.then_inc(logits_done, 1)
            pe.sem_inc(down_done, 2)
            up(0, 0, 0)
            units(pe, step)

        @block.scalar
        def _(act):
            def gate(u, k):
                for c in range(HC):
                    act.wait_ge(gate_done, 3 * u + c + 1)
                    act.wait_ge(prod_done, 3 * u + c + 1)
                    act.activation(sg[:, c, :], psum[:, c, :], ACT.Silu).then_inc(silu_done, 1)

            for half in range(2):
                cols = slice(half * HALF, (half + 1) * HALF)
                act.activation(XH[:, cols], XT[:, cols], ACT.Copy).then_inc(x_high, 1)
            act.wait_ge(chain, 2)
            act.activation(prob[:, :, :], prob[:, :, :], ACT.Exp).then_inc(exp_done, 1)
            act.sem_inc(silu_done, 3)
            gate(0, 0)
            units(act, lambda u, i, k, ahead: gate(u + 1, (k + 1) % 4) if ahead else None)

        @block.vector
        def _(dve):
            def multiply(u, k):
                dve.wait_ge(down_done, u + 1)
                for c in range(HC):
                    dve.wait_ge(silu_done, 3 * u + c + 4)
                    dve.wait_ge(up_done, 3 * u + c + 1)
                    dve.tensor_tensor(prod[:, k % 2, c, :], psum[:, HC + c, :], sg[:, c, :], ALU.mult)\
                        .then_inc(prod_done, 1)

            def add(u, i, k):
                half = k % 2
                dve.wait_ge(down_done, u + 3)
                dve.wait_ge(added, 4 * u + 4)
                for i4 in range(TH):
                    t = half * TH + i4
                    dve.scalar_tensor_tensor(out=dst[:, t, :], in0=psum[:, 6 + half, i4 * P:(i4 + 1) * P],
                                             scalar=comb[:, t, bass.ds(2 * i + k // 2, 1)], in1=dst[:, t, :],
                                             op0=ALU.mult, op1=ALU.add).then_inc(added, 1)

            def step(u, i, k, ahead):
                if ahead:
                    multiply(u + 1, (k + 1) % 4)
                add(u, i, k)

            dve.sem_inc(prod_done, 3)
            for half in range(2):
                cols = slice(half * HALF, (half + 1) * HALF)
                dve.wait_ge(x_high, half + 1)
                dve.tensor_tensor(XL[:, cols], XT[:, cols], XH[:, cols].bitcast(F32), ALU.subtract).then_inc(x_low, 1)
            n = 0

            def own(*ins):
                nonlocal n
                for x in ins:
                    x.then_inc(chain, 1)
                n += len(ins)
                dve.wait_ge(chain, n)

            def wide(a):
                return a.unsqueeze(2).to_broadcast([P, NT, NE])

            dve.wait_ge(logits_done, 1)
            logits = psum[:, 7, 0:NT * NE].rearrange("p (t e) -> p t e", e=NE)
            own(dve.tensor_reduce(hi[:, :], logits, AX, ALU.max))
            own(dve.tensor_tensor(prob[:, :, :], logits, wide(hi[:, :]), ALU.subtract))
            dve.wait_ge(exp_done, 1)
            own(dve.tensor_reduce(total[:, :], prob[:, :, :], AX, ALU.add))
            own(dve.reciprocal(total[:, :], total[:, :]))
            own(dve.tensor_tensor(prob[:, :, :], prob[:, :, :], wide(total[:, :]), ALU.mult))
            own(*[dve.max(top[:, t, :], prob[:, t, :]) for t in range(NT)])
            own(*[dve.max_index(at[:, t, :], top[:, t, :], prob[:, t, :]) for t in range(NT)])
            own(dve.tensor_copy(atf[:, :, :], at[:, :, :]))
            own(dve.tensor_tensor(total[:, :], top[:, :, 0], top[:, :, 1], ALU.add))
            own(dve.reciprocal(total[:, :], total[:, :]))
            for k in range(2):
                own(dve.tensor_tensor(pick[:, k, :, :], wide(atf[:, :, k]),
                                      iota[:, :].unsqueeze(1).to_broadcast([P, NT, NE]), ALU.is_equal))
                own(dve.tensor_tensor(pick[:, k, :, :], pick[:, k, :, :], wide(top[:, :, k]), ALU.mult))
            own(dve.tensor_tensor(pick[:, 0, :, :], pick[:, 0, :, :], pick[:, 1, :, :], ALU.add))
            own(dve.tensor_tensor(comb[:, :, :], pick[:, 0, :, :], wide(total[:, :]), ALU.mult))
            dve.sem_inc(added, 8)
            multiply(0, 0)
            units(dve, step)


def decoder(nc, ins, cst, out):
    with ExitStack() as stack:
        ch = Chip(nc, stack)
        ch.buf["psum"] = stack.enter_context(nc.psum_tensor("psum", [P, 8, 512], F32))
        for name in ("X", "A", "R"):
            ch.sb(name, [NT, D])
        for name in ("XT", "CT", "AT", "LT"):
            ch.sb(name, [NTOK])
        for name in ("QP", "KP"):
            ch.sb(name, [2, HALF])
        ch.sb("V", [NT, D])
        ch.sb("rot", [4, HALF])
        ch.sb("Kx", [2, 2, 8, S])
        ch.sb("Qd", [2, 2, P])
        ch.sb("Vd", [2, 2, 4, 64])
        ch.sb("Pr", [2, H, S])
        ch.sb("Pn", [2, H, S])
        ch.sb("PT", [2, 8, P])
        for name in ("mx", "den", "rden", "pad"):
            ch.sb(name, [2, H])
        ch.sb("stats", [NT, 6])
        ch.sb("mv", [NT, 2])
        for name in ("rstd", "var", "minus_half"):
            ch.sb(name, [NT])
        ch.sb("identf", [P])
        ch.sb("identb", [P], BF16)
        ch.sb("ones", [P])
        ch.sb("causal", [S], BF16)
        ch.sb("causalf", [S])
        ch.sb("head_of", [8])
        ch.sb("iota8", [NE])
        ch.sb("cos", [S])
        ch.sb("sin", [S])
        ch.sb("wqkv0", [3 * D])
        for name in ("wo0", "wctx", "wx", "xwq", "xwo", "mwq", "mwk", "mwv", "mwo"):
            ch.sb(name, [D])
        ch.sb("xwkv", [2 * HD])
        ch.sb("C", [NT, D])
        ch.sb("We", [2, 2 * HID])
        ch.sb("Wd", [2, HC, D])
        ch.sb("WH", [2, 2 * HID], F32R)
        ch.sb("WL", [2, 2 * HID], F32R)
        ch.sb("xwkr", [2, D])
        ch.sb("ffw1", [FF])
        ch.sb("ffw2", [NC, D])
        ch.sb("bw1", [NC, D])
        ch.sb("bw2", [FF])
        ch.sb("wtern", [2, FF], BF16)
        ch.sb("wternT", [2, FF], BF16)
        ch.sb("convw", [NC, 3])
        ch.sb("absum", [2])
        ch.sb("wmean", [2])
        ch.sb("winv", [2])
        ch.sb("ywo", [4, D])
        ch.sb("yw", [4 * D])
        ch.sb("mrot", [2, D])
        ch.sb("wrout", [NE])
        ch.sb("comb", [NT, NE])
        ch.sb("rows", [3, D])
        ch.sb("prow", [P])
        ch.sb("params", [NPAR])
        X, R, A, XT, CT, LT = (ch[n] for n in ("X", "R", "A", "XT", "CT", "LT"))

        later_loads = load_inputs(nc, ch, ins, cst)
        w = ch["wqkv0"]
        norm(nc, ch, X, R, XT, gain=0, shift=1)
        small_qkv(nc, ch, w[:, 0:D], w[:, D:2 * D], w[:, 2 * D:3 * D], XT, XT, bias=True)
        small_attention(nc, ch, causal=True, loads=later_loads)
        project_add(nc, ch, ch["wo0"][:, :], A, [X, ch["rows"][:, 1, :]], featT=LT, feat_bias=7)
        norm(nc, ch, A, R, XT, gain=2, shift=3)
        inner_steps(nc, ch)
        turn_add(nc, ch, XT, A, A)
        norm(nc, ch, A, R, XT, gain=4, shift=5)
        gelu_mlp(nc, ch, X, A, R)
        norm(nc, ch, R, X, XT)
        small_qkv(nc, ch, ch["xwq"][:, :], ch["xwkr"][:, 0, :], ch["xwkr"][:, 1, :], XT, CT)
        small_attention(nc, ch, zero_keys=2 * S)
        project_add(nc, ch, ch["xwo"][:, :], R, [X])
        norm(nc, ch, R, X)
        quantized_ffn(nc, ch, X, R)
        norm(nc, ch, R, X, XT)
        wide_attention(nc, ch, ins["L1_attn_w_qkv"], ins["L1_attn_w_o"], X)
        norm(nc, ch, X, X, XT)
        yw = ch["yw"]
        small_qkv(nc, ch, yw[:, 0:D], yw[:, D:2 * D], yw[:, 2 * D:3 * D], XT, CT)
        small_attention(nc, ch)
        project_add(nc, ch, yw[:, 3 * D:4 * D], R, [X])
        norm(nc, ch, R, X)
        norm(nc, ch, X, R, XT, gain=8, eps=1e-6, rms=True)
        small_qkv(nc, ch, ch["mwq"][:, :], ch["mwk"][:, :], ch["mwv"][:, :], XT, XT,
                  rotated=(ch["mrot"][:, 0, :], ch["mrot"][:, 1, :]))
        small_attention(nc, ch, causal=True)
        project_add(nc, ch, ch["mwo"][:, :], R, [X])
        norm(nc, ch, R, A, XT, gain=9, eps=1e-6, rms=True)
        experts(nc, ch, ins["L1_ffn_wg"], ins["L1_ffn_wu"], ins["L1_ffn_wd"], R)
        sum_rows(nc, ch, R, X)
        norm(nc, ch, R, X, out=out)
        nc.clear_and_free_semaphores(ch.past)


def sum_rows(nc, ch, dst, add):
    with ExitStack() as st:
        (added,) = stage_semaphores(nc, ch, "added")
        block = st.enter_context(stage_block(nc, ch))

        @block.vector
        def _(dve):
            dve.tensor_tensor(dst[:, :, :], dst[:, :, :], add[:, :, :], ALU.add).then_inc(added, 1)
            dve.wait_ge(added, 1)


def constants():
    p = np.arange(P)
    inv_freq = 1.0 / 10000.0 ** (np.arange(0, HD, 2, dtype=np.float32) / HD)
    freqs = np.einsum("i,j->ij", np.arange(S, dtype=np.float32), inv_freq)
    emb = np.concatenate([freqs, freqs], axis=-1)
    return {
        "identf": np.eye(P, dtype=np.float32),
        "causal": np.where(np.arange(S)[None, :] > (p % S)[:, None], MASKED, 0.0).astype(np.float32),
        "head_of": ((p[:, None] // HD) % 8 == np.arange(8)[None, :]).astype(np.float32),
        "iota8": np.tile(np.arange(NE, dtype=np.float32), (P, 1)),
        "cos": np.ascontiguousarray(np.cos(emb).astype(np.float32)[:, p % HD].T),
        "sin": np.ascontiguousarray(np.sin(emb).astype(np.float32)[:, p % HD].T),
    }


def kernel(**inputs):
    import numpy as _np
    import concourse.bacc as _bacc
    from concourse import mybir as _mybir
    from concourse.bass_utils import run_bass_kernel_spmd as _run

    nc = _bacc.Bacc("TRN2", target_bir_lowering=False, num_devices=1)
    arrays, ins, cst = {}, {}, {}
    for group, given in ((ins, inputs), (cst, constants())):
        for name, a in given.items():
            a = _np.ascontiguousarray(a)
            arrays[f"in_{name}_dram"] = a
            group[name] = nc.dram_tensor(f"in_{name}_dram", a.shape, _mybir.dt.from_np(a.dtype),
                                         kind="ExternalInput").ap()
    out = nc.dram_tensor("out_0_dram", (B, S, D), F32, kind="ExternalOutput").ap()
    decoder(nc, ins, cst, out)
    r = _run(nc, [arrays], core_ids=[0])
    return r.results[0]["out_0_dram"]
```

```python
from contextlib import ExitStack, contextmanager

import numpy as np

import concourse.bass as bass
from concourse import mybir

F32 = mybir.dt.float32
BF16 = mybir.dt.bfloat16
F32R = mybir.dt.float32r
U32 = mybir.dt.uint32
ALU = mybir.AluOpType
ACT = mybir.ActivationFunctionType
AX = mybir.AxisListType.X

P = 128
B, S, D = 16, 64, 128
NTOK = B * S
NT = NTOK // P
HALF = NTOK // 2
TH = NT // 2
H, HD = 16, 8
FF = 512
NC = FF // P
NP1, N1 = 8, 64
NE, HID = 8, 384
HC = HID // P
NPAR = 14 + 2 * NC
ROUND = 1.5 * 2.0**23
MASKED = -1e30


class Chip:

    def __init__(self, nc, stack):
        self.nc, self.stack, self.buf = nc, stack, {}
        self.current, self.past, self.stage, self.parts, self.block = [], [], 0, 0, None

    def sb(self, name, shape, dt=F32):
        self.buf[name] = self.stack.enter_context(self.nc.sbuf_tensor(name, [P, *shape], dt))
        return self.buf[name]

    def __getitem__(self, name):
        return self.buf[name]


def stage_semaphores(nc, ch, *names):
    sems = [nc.alloc_semaphore(f"{n}_{ch.stage}_{ch.parts}") for n in names]
    ch.parts += 1
    ch.current += sems
    return sems


@contextmanager
def stage_block(nc, ch):
    if ch.block is not None:
        yield ch.block
        return
    if ch.past:
        nc.clear_and_free_semaphores(ch.past)
    with nc.Block() as block:
        yield block
    ch.past, ch.current = ch.current, []
    ch.stage += 1


@contextmanager
def joined_stages(nc, ch):
    with nc.Block() as block:
        ch.block = block
        yield
        ch.block = None
    ch.past, ch.current = ch.past + ch.current, []
    ch.stage += 1


def half_ready(eng, after, half):
    if after is not None:
        sem, each, start = after
        eng.wait_ge(sem, start + each * (half + 1))


def all_ready(eng, *afters):
    for after in afters:
        half_ready(eng, after, 1)


def tile_cols(t, n=P):
    return bass.ds(t * n, n)


def load_inputs(nc, ch, ins, cst):
    def line(v):
        return v.rearrange("(a n) -> a n", a=1)

    def row(v):
        return v.rearrange("(a n) -> a n", a=1).to_broadcast([P, v.shape[0]])

    prow = ch["prow"]
    first = [
        (ch["X"][:, :, :], ins["x"].rearrange("(t b) s d -> (b s) t d", b=2)),
        (ch["identf"][:, :], cst["identf"]),
        (ch["wqkv0"][:, :], ins["L0_attn_qkv_w"]),
        (ch["causalf"][:, :], cst["causal"]), (ch["head_of"][:, :], cst["head_of"]),
        (ch["rows"][:, 0, :], row(ins["L0_attn_qkv_b"][2 * D:3 * D])),
    ]
    for n, name in enumerate(["L0_attn_g_attn", "L0_attn_b_attn", "L0_attn_g1", "L0_attn_b1", "L0_attn_g2",
                              "L0_attn_b2", "L0_attn_b_inl", "L0_attn_out_b", "L1_ffn_g1", "L1_ffn_g2"]):
        first.append((prow[n:n + 1, :], line(ins[name])))
    first.append((prow[10:14, :].rearrange("n (b d) -> n b d", b=2),
                  ins["L0_attn_qkv_b"][0:2 * D].rearrange("(n a d) -> n a d", a=1, d=64).to_broadcast([4, 2, 64])))
    first.append((prow[14:14 + NC, :], ins["L0_attn_ff_b1"].rearrange("(c p) -> c p", p=P)))
    first.append((prow[14 + NC:NPAR, :], ins["L0_ffn_conv_b"].rearrange("(c p) -> c p", p=P)))
    later = [
        (ch["wo0"][:, :], ins["L0_attn_out_w"]),
        (ch["rows"][:, 1, :], row(ins["L0_attn_out_b"])),
        (ch["wctx"][:, :], ins["L0_attn_w_ctx"]), (ch["wx"][:, :], ins["L0_attn_w_x"]),
        (ch["ffw1"][:, :], ins["L0_attn_ff_w1"]),
        (ch["ffw2"][:, :, :], ins["L0_attn_ff_w2"].rearrange("(c p) d -> p c d", p=P)),
        (ch["rows"][:, 2, :], row(ins["L0_attn_ff_b2"])),
        (ch["C"][:, :, :], ins["ctx_1024"].rearrange("(t b) s d -> (b s) t d", b=2)),
        (ch["xwq"][:, :], ins["L0_xattn_Wq"]), (ch["xwkv"][:, :], ins["L0_xattn_Wkv"]),
        (ch["xwo"][:, :], ins["L0_xattn_Wo"]),
        (ch["bw1"][:, :, :], ins["L0_ffn_w1"].rearrange("(c p) d -> p c d", p=P)),
        (ch["bw2"][:, :], ins["L0_ffn_w2"]),
        (ch["convw"][:, :, :], ins["L0_ffn_conv_w"].rearrange("(c p) a k -> p c (a k)", p=P)),
        (ch["cos"][:, :], cst["cos"]), (ch["sin"][:, :], cst["sin"]),
        (ch["iota8"][:, :], cst["iota8"]),
        (ch["ywo"][:, 0, :], ins["L1_xattn_w_q"]), (ch["ywo"][:, 1, :], ins["L1_xattn_w_k"]),
        (ch["ywo"][:, 2, :], ins["L1_xattn_w_v"]), (ch["ywo"][:, 3, :], ins["L1_xattn_w_o"]),
        (ch["mwq"][:, :], ins["L1_ffn_wq"]), (ch["mwk"][:, :], ins["L1_ffn_wk"]),
        (ch["mwv"][:, :], ins["L1_ffn_wv"]), (ch["mwo"][:, :], ins["L1_ffn_wo"]),
        (ch["wrout"][:, :], ins["L1_ffn_w_router"]),
    ]
    for h in range(4):
        later.append((ch["Wa"][:, h // 2, :, h % 2, :], ins["L1_attn_w_qkv"][h].rearrange("a v n -> v a n")))
    for e in range(2):
        for n, name in enumerate(("L1_ffn_wg", "L1_ffn_wu")):
            later.append((ch["We"][:, e, n * HID:(n + 1) * HID], ins[name][e]))
        later.append((ch["Wd"][:, e, :, :], ins["L1_ffn_wd"][e].rearrange("(c p) d -> p c d", p=P)))
    with ExitStack() as st:
        loaded, small_done, ones_set, turned, kept = stage_semaphores(
            nc, ch, "loaded", "small_done", "ones_set", "turned", "kept")
        psum = ch["psum"]
        block = st.enter_context(stage_block(nc, ch))
        all_loaded = 16 * len(first)

        @block.sync
        def _(sp):
            for dst, src in first[0::2]:
                sp.dma_start(dst, src).then_inc(loaded, 16)

        @block.gpsimd
        def _(pool):
            pool.memset(ch["minus_half"][:, :], -0.5).then_inc(small_done, 1)
            pool.memset(ch["unround"][:, :], -ROUND).then_inc(small_done, 1)
            pool.memset(ch["Qd"][:, :, :, :], 0.0).then_inc(small_done, 1)
            pool.memset(ch["Vd"][:, :, :, :, :], 0.0).then_inc(small_done, 1)
            pool.wait_ge(loaded, all_loaded)
            pool.tensor_copy(ch["identb"][:, :], ch["identf"][:, :]).then_inc(small_done, 1)
            pool.tensor_copy(ch["causal"][:, :], ch["causalf"][:, :]).then_inc(small_done, 1)
            pool.wait_ge(small_done, 6)

        @block.scalar
        def _(act):
            for dst, src in first[1::2]:
                act.dma_start(dst, src).then_inc(loaded, 16)
            act.wait_ge(turned, 1)
            act.activation(ch["params"][:, :], psum[:, 6, 0:NPAR], ACT.Copy).then_inc(kept, 1)
            act.wait_ge(kept, 1)

        @block.vector
        def _(dve):
            dve.memset(ch["ones"][:, :], 1.0).then_inc(ones_set, 1)
            dve.wait_ge(ones_set, 1)

        @block.tensor
        def _(pe):
            pe.wait_ge(loaded, all_loaded)
            pe.transpose(psum[:, 6, 0:NPAR], prow[0:NPAR, :], ch["identf"][0:NPAR, 0:NPAR]).then_inc(turned, 1)
    return later


def norm(nc, ch, src, dst, featT=None, gain=None, shift=None, eps=1e-5, rms=False, out=None, after=None):
    psum, par = ch["psum"], ch["params"]
    with ExitStack() as st:
        def sb(n, shape):
            return st.enter_context(nc.sbuf_tensor(f"{n}_{ch.stage}_{ch.parts}", [P, *shape], F32))

        stats, mv, rstd, var = sb("stats", [NT, 6]), sb("mv", [NT, 2]), sb("rstd", [NT]), sb("var", [NT])
        stats_done, agg_done, var_done, root_done, normed, turned, feat_kept, stored = stage_semaphores(
            nc, ch, "stats_done", "agg_done", "var_done", "root_done", "normed", "turned", "feat_kept", "stored")
        block = st.enter_context(stage_block(nc, ch))

        @block.vector
        def _(dve):
            for half in range(2):
                tiles = range(half * TH, (half + 1) * TH)
                cols = slice(half * TH, (half + 1) * TH)
                half_ready(dve, after, half)
                for t in tiles:
                    dve.bn_stats(stats[:, t, :], src[:, t, :]).then_inc(stats_done, 1)
                for t in tiles:
                    dve.wait_ge(stats_done, t + 1)
                    dve.bn_aggr(mv[:, t, :], stats[:, t, :]).then_inc(agg_done, 1)
                dve.wait_ge(agg_done, TH * (half + 1))
                if rms:
                    dve.tensor_tensor(var[:, cols], mv[:, cols, 0], mv[:, cols, 0], ALU.mult).then_inc(var_done, 1)
                    dve.wait_ge(var_done, 2 * half + 1)
                    dve.scalar_tensor_tensor(out=var[:, cols], in0=var[:, cols], scalar=eps, in1=mv[:, cols, 1],
                                             op0=ALU.add, op1=ALU.add).then_inc(var_done, 1)
                else:
                    dve.tensor_scalar(var[:, cols], mv[:, cols, 1], eps, None, ALU.add).then_inc(var_done, 2)
            for half in range(2):
                dve.wait_ge(root_done, half + 1)
                for t in range(half * TH, (half + 1) * TH):
                    if rms:
                        dve.tensor_scalar(dst[:, t, :], src[:, t, :], rstd[:, t:t + 1], None, ALU.mult)\
                            .then_inc(normed, 1)
                    else:
                        dve.tensor_scalar(dst[:, t, :], src[:, t, :], mv[:, t, 0:1], rstd[:, t:t + 1], ALU.subtract,
                                          ALU.mult).then_inc(normed, 1)
            dve.wait_ge(normed, NT)

        @block.gpsimd
        def _(pool):
            for half in range(2):
                cols = slice(half * TH, (half + 1) * TH)
                pool.wait_ge(var_done, 2 * half + 2)
                pool.tensor_tensor(rstd[:, cols], var[:, cols], ch["minus_half"][:, cols], ALU.pow)\
                    .then_inc(root_done, 1)

        if featT is not None:
            @block.tensor
            def _(pe):
                for half in range(2):
                    for i in range(TH):
                        t = half * TH + i
                        pe.wait_ge(normed, t + 1)
                        mm = pe.transpose(psum[:, 6 + half, i * P:(i + 1) * P], dst[:, t, :], ch["identf"][:, :])
                    mm.then_inc(turned, 1)

            @block.scalar
            def _(act):
                for half in range(2):
                    act.wait_ge(turned, half + 1)
                    cols = featT[:, half * HALF:(half + 1) * HALF]
                    scale = par[:, gain:gain + 1] if gain is not None else 1.0
                    bias = par[:, shift:shift + 1] if shift is not None else 0.0
                    act.activation(cols, psum[:, 6 + half, :], ACT.Identity, scale=scale, bias=bias)\
                        .then_inc(feat_kept, 1)
                act.wait_ge(feat_kept, 2)

        if out is not None:
            @block.sync
            def _(sp):
                rows = out.rearrange("(t b) s d -> (b s) t d", b=2)
                for half in range(2):
                    sp.wait_ge(normed, TH * (half + 1))
                    sp.dma_start(rows[:, half * TH:(half + 1) * TH, :], dst[:, half * TH:(half + 1) * TH, :])\
                        .then_inc(stored, 16)
                sp.wait_ge(stored, 32)
    return (normed, TH, 0), (feat_kept, 1, 0)


def small_qkv(nc, ch, q=None, k=None, v=None, bias=False, rotated=None, after=None):
    psum, par = ch["psum"], ch["params"]
    QK = (ch["QP"], ch["KP"])
    asked = [(m, *given) for m, given in enumerate((q, k)) if given is not None]

    def packed(src, b):
        return src[:, :].rearrange("p (t b s) -> p b t s", b=2, s=S)[:, b]

    with ExitStack() as st:
        qk_done, qk_kept, v_done, v_kept, rot_done, rot_kept, mixed, mixed_k = stage_semaphores(
            nc, ch, "qk_done", "qk_kept", "v_done", "v_kept", "rot_done", "rot_kept", "mixed", "mixed_k")
        block = st.enter_context(stage_block(nc, ch))

        @block.tensor
        def _(pe):
            if v is not None:
                for half in range(2):
                    half_ready(pe, after, half)
                    for i in range(TH):
                        mm = pe.matmul(psum[:, 4 + half, i * P:(i + 1) * P], v[1][:, tile_cols(half * TH + i)], v[0],
                                       start=True, stop=True)
                    mm.then_inc(v_done, 1)
            all_ready(pe, after)
            for m, weights, src in asked:
                for half in range(2):
                    for b in range(2):
                        mm = pe.matmul(psum[64 * b:64 * b + 64, 2 * m + half, :], weights[:, 64 * half:64 * half + 64],
                                       packed(src, b), start=True, stop=True)
                    mm.then_inc(qk_done, 1)
            if rotated is not None:
                for m, _weights, src in asked:
                    for half in range(2):
                        pe.wait_ge(qk_kept, 2 * m + half + 1)
                        for b in range(2):
                            mm = pe.matmul(psum[64 * b:64 * b + 64, 2 * m + half, :],
                                           rotated[m][:, 64 * half:64 * half + 64], packed(src, b), start=True, stop=True)
                        mm.then_inc(rot_done, 1)

        @block.scalar
        def _(act):
            if v is not None and q is None:
                for half in range(2):
                    act.wait_ge(v_done, half + 1)
                    act.activation(ch["V"][:, half * TH:(half + 1) * TH, :],
                                   psum[:, 4 + half, :].rearrange("p (t d) -> p t d", d=D), ACT.Copy).then_inc(v_kept, 1)
            n = 0
            for m, _weights, _src in asked:
                for half in range(2):
                    n += 1
                    act.wait_ge(qk_done, n)
                    act.activation(QK[m][:, half, :], psum[:, 2 * m + half, :], ACT.Identity,
                                   bias=par[:, 10 + 2 * m + half:11 + 2 * m + half] if bias else 0.0).then_inc(qk_kept, 1)
            if rotated is not None:
                for n in range(4):
                    act.wait_ge(rot_done, n + 1)
                    act.activation(ch["rot"][:, n, :], psum[:, n, :], ACT.Copy).then_inc(rot_kept, 1)
                act.wait_ge(rot_kept, 4)
            act.wait_ge(qk_kept, 2 * len(asked))

        if v is not None and q is not None:
            @block.vector
            def _(dve):
                for half in range(2):
                    dve.wait_ge(v_done, half + 1)
                    to = ch["V"][:, half * TH:(half + 1) * TH, :]
                    p = psum[:, 4 + half, :].rearrange("p (t d) -> p t d", d=D)
                    if bias:
                        dve.tensor_tensor(to, p, ch["rows"][:, 0, :].unsqueeze(1).to_broadcast([P, TH, D]), ALU.add)\
                            .then_inc(v_kept, 1)
                    else:
                        dve.tensor_copy(to, p).then_inc(v_kept, 1)
                if rotated is not None:
                    for n in range(4):
                        x = QK[n // 2][:, n % 2, :].rearrange("p (t s) -> p t s", s=S)
                        r = ch["rot"][:, n, :].rearrange("p (t s) -> p t s", s=S)
                        dve.wait_ge(qk_kept, n + 1)
                        dve.tensor_tensor(x, x, ch["cos"][:, :].unsqueeze(1).to_broadcast([P, NT, S]), ALU.mult)\
                            .then_inc(mixed, 1)
                        dve.wait_ge(mixed_k, n + 1)
                        dve.wait_ge(mixed, 2 * n + 1)
                        dve.tensor_tensor(x, x, r, ALU.add).then_inc(mixed, 1)
                    dve.wait_ge(mixed, 8)
                dve.wait_ge(v_kept, 2)

        if rotated is not None:
            @block.gpsimd
            def _(pool):
                for n in range(4):
                    r = ch["rot"][:, n, :].rearrange("p (t s) -> p t s", s=S)
                    pool.wait_ge(rot_kept, n + 1)
                    pool.tensor_tensor(r, r, ch["sin"][:, :].unsqueeze(1).to_broadcast([P, NT, S]), ALU.mult)\
                        .then_inc(mixed_k, 1)
    ready = [(mixed, 4, 0) if rotated is not None else (qk_kept, len(asked), 0)]
    if v is not None:
        ready.append((v_kept, 1, 0))
    return ready


def small_attention(nc, ch, causal=False, zero_keys=0, loads=(), after=()):
    psum = ch["psum"]
    scale = float(HD) ** -0.5
    Qd, Kx, Vd, Pr, Pn, PT, mx, den, rden = (ch[n] for n in ("Qd", "Kx", "Vd", "Pr", "Pn", "PT", "mx", "den", "rden"))
    pad, AT = ch["pad"], ch["AT"]
    with ExitStack() as st:
        (keys_spread, query_placed, scores_done, max_done, pad_max, centred, exp_done, pad_done, sum_done, sum_pad,
         inverse_done, probs_done, turned, turned_kept, values_placed, pv_done, out_kept, first_spread, arrived) = stage_semaphores(
            nc, ch, "keys_spread", "query_placed", "scores_done", "max_done", "pad_max", "centred", "exp_done",
            "pad_done", "sum_done", "sum_pad", "inverse_done", "probs_done", "turned", "turned_kept",
            "values_placed", "pv_done", "out_kept", "first_spread", "arrived")
        block = st.enter_context(stage_block(nc, ch))

        def rounds(eng, before, step):
            before()
            step(0, 0)
            with eng.Fori(0, NT // 2 - 2) as i:
                step(2 * i + 1, 1)
                step(2 * i + 2, 0)
            for t in range(NT - 3, NT):
                step(t, t % 2)

        def has(t, ahead):
            return not isinstance(t, int) or 0 <= t + ahead < NT

        if loads:
            @block.sync
            def _(sp):
                for dst, src in loads:
                    sp.dma_start(dst, src).then_inc(arrived, 16)
                sp.wait_ge(arrived, 16 * len(loads))

        def spread(eng, t, s):
            k = ch["KP"][:, :, tile_cols(t, S)]
            return eng.tensor_tensor(Kx[:, s, :, :, :], k.unsqueeze(2).to_broadcast([P, 2, 8, S]),
                                     ch["head_of"][:, :].unsqueeze(1).unsqueeze(3).to_broadcast([P, 2, 8, S]), ALU.mult)

        @block.gpsimd
        def _(pool):
            def spread_keys(t, s):
                pool.wait_ge(scores_done, t + 1)
                spread(pool, t, s).then_inc(keys_spread, 1)

            def normalise(t, s):
                pool.wait_ge(inverse_done, t + 1)
                pool.wait_ge(turned, t + 1)
                pool.tensor_tensor(Pn[:, s, :, :], Pr[:, s, :, :],
                                   rden[:, s, :].unsqueeze(2).to_broadcast([P, H, S]), ALU.mult)\
                    .then_inc(probs_done, 1)

            def before():
                pool.sem_inc(probs_done, 2)
                pool.sem_inc(keys_spread, 1)
                all_ready(pool, *after)
                spread_keys(1, 1)
                spread_keys(2, 0)

            def step(t, s):
                if has(t, 3):
                    spread_keys(t + 3, 1 - s)
                normalise(t, s)

            rounds(pool, before, step)

        @block.scalar
        def _(act):
            def place_query(t, s):
                act.wait_ge(scores_done, t + 1)
                for b in range(2):
                    rows = slice(64 * b, 64 * b + 64)
                    act.activation(Qd[rows, s, :, 64 * b:64 * b + 64], ch["QP"][rows, :, tile_cols(t, S)], ACT.Copy)\
                        .then_inc(query_placed, 1)

            def place_values(t, s):
                act.wait_ge(pv_done, t + 1)
                for b in range(2):
                    for odd in range(2):
                        src = ch["V"][64 * b:64 * b + 64, bass.ds(t, 1), :].rearrange(
                            "p a (g m o d) -> p (a g) m o d", g=4, m=2, o=2)[:, :, :, odd, :]
                        dst = Vd[64 * odd:64 * odd + 64, s, b, :, :].rearrange("p g (a d) -> p g a d", d=HD)
                        act.activation(dst[:, :, odd:odd + 7:6, :], src, ACT.Copy).then_inc(values_placed, 1)

            def exponentials(t, s):
                act.wait_ge(centred, t + 3)
                act.activation(Pr[:, s, :, :], Pr[:, s, :, :], ACT.Exp, scale=scale).then_inc(exp_done, 1)
                if zero_keys:
                    act.activation(pad[:, s, :], mx[:, s, :], ACT.Exp, scale=-scale).then_inc(pad_done, 1)

            def keep_turned(t, s):
                act.wait_ge(turned, t + 3)
                act.wait_ge(pv_done, t + 1)
                for m in range(2):
                    act.activation(PT[:, s, 4 * m:4 * m + 4, :].rearrange("p h q -> p (h q)"), psum[:, 4 + m, :],
                                   ACT.Copy).then_inc(turned_kept, 1)

            def keep_out(t, s):
                act.wait_ge(pv_done, t + 3)
                act.activation(AT[:, tile_cols(t)], psum[:, 6 + s, 0:P], ACT.Copy).then_inc(out_kept, 1)

            def before():
                act.sem_inc(out_kept, 2)
                act.sem_inc(turned_kept, 2)
                all_ready(act, *after)
                place_query(0, 0)
                place_values(0, 0)
                place_query(1, 1)
                place_query(2, 0)
                exponentials(0, 0)

            def step(t, s):
                if has(t, 3):
                    place_query(t + 3, 1 - s)
                if has(t, 1):
                    exponentials(t + 1, 1 - s)
                if has(t, -1):
                    keep_out(t - 1, 1 - s)
                if has(t, 1):
                    place_values(t + 1, 1 - s)
                keep_turned(t, s)

            rounds(act, before, step)
            keep_out(NT - 1, (NT - 1) % 2)
            act.wait_ge(out_kept, NT + 2)

        @block.vector
        def _(dve):
            def scores_of(s):
                return psum[:, 2 * s:2 * s + 2, :].rearrange("p a (h k) -> p (a h) k", k=S)

            def find_max(t, s):
                dve.wait_ge(scores_done, t + 3)
                dve.tensor_reduce(mx[:, s, :], scores_of(s), AX, ALU.max).then_inc(max_done, 1)
                if zero_keys:
                    dve.wait_ge(max_done, t + 1)
                    dve.tensor_scalar(mx[:, s, :], mx[:, s, :], 0.0, None, ALU.max).then_inc(pad_max, 1)

            def centre(t, s):
                dve.wait_ge(pad_max if zero_keys else max_done, t + 1)
                dve.wait_ge(probs_done, t + 1)
                dve.tensor_tensor(Pr[:, s, :, :], scores_of(s), mx[:, s, :].unsqueeze(2).to_broadcast([P, H, S]),
                                  ALU.subtract).then_inc(centred, 1)

            def invert(t, s):
                dve.wait_ge(exp_done, t + 1)
                dve.tensor_reduce(den[:, s, :], Pr[:, s, :, :], AX, ALU.add).then_inc(sum_done, 1)
                dve.wait_ge(sum_done, t + 1)
                if zero_keys:
                    dve.wait_ge(pad_done, t + 1)
                    dve.scalar_tensor_tensor(out=den[:, s, :], in0=pad[:, s, :], scalar=float(zero_keys),
                                             in1=den[:, s, :], op0=ALU.mult, op1=ALU.add).then_inc(sum_pad, 1)
                    dve.wait_ge(sum_pad, t + 1)
                dve.reciprocal(rden[:, s, :], den[:, s, :]).then_inc(inverse_done, 1)

            def before():
                dve.sem_inc(centred, 2)
                all_ready(dve, *after)
                spread(dve, 0, 0).then_inc(first_spread, 1)
                find_max(0, 0)
                centre(0, 0)

            def step(t, s):
                if has(t, 1):
                    find_max(t + 1, 1 - s)
                invert(t, s)
                if has(t, 1):
                    centre(t + 1, 1 - s)

            rounds(dve, before, step)

        @block.tensor
        def _(pe):
            def scores(t, s):
                pe.wait_ge(keys_spread, t + 1)
                pe.wait_ge(query_placed, 2 * t + 2)
                pe.wait_ge(centred, t + 1)
                for half in range(2):
                    bank = psum[:, 2 * s + half, :]
                    if causal:
                        pe.matmul(bank, ch["identb"][:, :], ch["causal"][:, :].unsqueeze(1).to_broadcast([P, 8, S]),
                                  start=True, stop=False)
                    mm = pe.matmul(bank, Qd[:, s, half, :], Kx[:, s, half, :, :].rearrange("p h k -> p (h k)"),
                                   start=not causal, stop=True)
                mm.then_inc(scores_done, 1)

            def turn(t, s):
                pe.wait_ge(probs_done, t + 3)
                pe.wait_ge(turned_kept, 2 * t + 2)
                for hp in range(8):
                    mm = pe.transpose(psum[:, 4 + hp // 4, (hp % 4) * P:(hp % 4 + 1) * P],
                                      Pn[:, s, 2 * hp:2 * hp + 2, :].rearrange("p h k -> p (h k)"), ch["identf"][:, :])
                mm.then_inc(turned, 1)

            def values(t, s):
                pe.wait_ge(turned_kept, 2 * t + 4)
                pe.wait_ge(values_placed, 4 * t + 4)
                pe.wait_ge(out_kept, t + 1)
                for b in range(2):
                    for m in range(2):
                        for g in range(4):
                            mm = pe.matmul(psum[32 * g:32 * g + 32, 6 + s, 64 * b:64 * b + 64], Vd[:, s, b, g, 32 * m:32 * m + 32],
                                           PT[:, s, 2 * g + m, 64 * b:64 * b + 64], start=(m == 0), stop=(m == 1))
                mm.then_inc(pv_done, 1)

            def before():
                pe.sem_inc(scores_done, 2)
                pe.sem_inc(pv_done, 2)
                pe.sem_inc(turned, 2)
                all_ready(pe, *after)
                pe.wait_ge(first_spread, 1)
                scores(0, 0)
                scores(1, 1)

            def step(t, s):
                if has(t, 2):
                    scores(t + 2, s)
                if has(t, -1):
                    values(t - 1, 1 - s)
                turn(t, s)

            rounds(pe, before, step)
            values(NT - 1, (NT - 1) % 2)
    return out_kept, TH, 2


def project_add(nc, ch, wo, dst, adds, featT=None, feat_bias=None, after=None):
    psum, AT = ch["psum"], ch["AT"]
    with ExitStack() as st:
        proj_done, added, feat_done, feat_kept = stage_semaphores(nc, ch, "proj_done", "added", "feat_done",
                                                                  "feat_kept")
        block = st.enter_context(stage_block(nc, ch))

        @block.tensor
        def _(pe):
            for half in range(2):
                half_ready(pe, after, half)
                for i in range(TH):
                    mm = pe.matmul(psum[:, half, i * P:(i + 1) * P], AT[:, tile_cols(half * TH + i)], wo,
                                   start=True, stop=True)
                mm.then_inc(proj_done, 1)
            if featT is not None:
                for half in range(2):
                    pe.matmul(psum[:, 2 + half, :], wo, AT[:, half * HALF:(half + 1) * HALF], start=True, stop=True)\
                        .then_inc(feat_done, 1)

        @block.vector
        def _(dve):
            n = 0
            for half in range(2):
                dve.wait_ge(proj_done, half + 1)
                cols = slice(half * TH, (half + 1) * TH)
                cur = psum[:, half, :].rearrange("p (t d) -> p t d", d=D)
                for a in adds:
                    if n and cur is not None and n % len(adds):
                        dve.wait_ge(added, n)
                    term = a[:, cols, :] if len(a.shape) == 3 else a.unsqueeze(1).to_broadcast([P, TH, D])
                    dve.tensor_tensor(dst[:, cols, :], cur, term, ALU.add).then_inc(added, 1)
                    cur = dst[:, cols, :]
                    n += 1
            dve.wait_ge(added, n)

        if featT is not None:
            @block.scalar
            def _(act):
                for half in range(2):
                    act.wait_ge(feat_done, half + 1)
                    act.activation(featT[:, half * HALF:(half + 1) * HALF], psum[:, 2 + half, :], ACT.Identity,
                                   bias=ch["params"][:, feat_bias:feat_bias + 1]).then_inc(feat_kept, 1)
                act.wait_ge(feat_kept, 2)
    return added, len(adds), 0


def inner_steps(nc, ch, steps=8, dt=0.1):
    psum, xs, ctx = ch["psum"], ch["XT"], ch["LT"]
    with ExitStack() as st:
        w, u, drift, slowed, pulled = (st.enter_context(nc.sbuf_tensor(n, [P, 2, HALF], F32))
                                       for n in ("w", "u", "drift", "slowed", "pulled"))
        pre_done, tanh_done, speed_done, state_done, parts_done, drift_done = (
            stage_semaphores(nc, ch, f"{n}0", f"{n}1") for n in
            ("pre_done", "tanh_done", "speed_done", "state_done", "parts_done", "drift_done"))
        (cleared,) = stage_semaphores(nc, ch, "cleared")
        block = st.enter_context(stage_block(nc, ch))

        def half_of(a, h):
            return a[:, h * HALF:(h + 1) * HALF]

        @block.tensor
        def _(pe):
            with pe.Fori(0, steps) as i:
                for h in range(2):
                    pe.wait_ge(tanh_done[h], i + 1)
                    pe.matmul(psum[:, h, :], ch["wctx"][:, :], half_of(ctx, h), start=True, stop=False)
                    pe.wait_ge(state_done[h], i + 1)
                    pe.matmul(psum[:, h, :], ch["wx"][:, :], half_of(xs, h), start=False, stop=True)\
                        .then_inc(pre_done[h], 1)

        @block.scalar
        def _(act):
            def parts(h, i):
                act.wait_ge(speed_done[h], i + 1)
                act.wait_ge(drift_done[h], i + 1)
                act.activation(slowed[:, h, :], w[:, h, :], ACT.Copy, scale=1.0 - dt).then_inc(parts_done[h], 1)
                act.wait_ge(state_done[h], i + 1)
                act.activation(pulled[:, h, :], half_of(xs, h), ACT.Copy, scale=dt * dt).then_inc(parts_done[h], 1)

            def squash(h, i):
                act.wait_ge(pre_done[h], i + 1)
                act.wait_ge(speed_done[h], i + 1)
                act.activation(u[:, h, :], psum[:, h, :], ACT.Tanh, bias=ch["params"][:, 6:7])\
                    .then_inc(tanh_done[h], 1)

            for h in range(2):
                act.sem_inc(tanh_done[h], 1)
            act.wait_ge(cleared, 1)
            parts(0, 0)
            with act.Fori(0, steps) as i:
                squash(0, i)
                parts(1, i)
                squash(1, i)
                parts(0, i + 1)

        @block.gpsimd
        def _(pool):
            def drifts(h, i):
                pool.wait_ge(parts_done[h], 2 * i + 2)
                pool.wait_ge(speed_done[h], i + 1)
                pool.tensor_tensor(drift[:, h, :], slowed[:, h, :], pulled[:, h, :], ALU.subtract)\
                    .then_inc(drift_done[h], 1)

            pool.memset(w[:, :, :], 0.0).then_inc(cleared, 1)
            for h in range(2):
                pool.sem_inc(drift_done[h], 1)
            drifts(0, 0)
            with pool.Fori(0, steps) as i:
                drifts(1, i)
                drifts(0, i + 1)

        @block.vector
        def _(dve):
            for h in range(2):
                dve.sem_inc(speed_done[h], 1)
                dve.sem_inc(state_done[h], 1)
            with dve.Fori(0, steps) as i:
                for h in range(2):
                    dve.wait_ge(tanh_done[h], i + 2)
                    dve.wait_ge(drift_done[h], i + 2)
                    dve.scalar_tensor_tensor(out=w[:, h, :], in0=u[:, h, :], scalar=dt * dt, in1=drift[:, h, :],
                                             op0=ALU.mult, op1=ALU.add).then_inc(speed_done[h], 1)
                    dve.wait_ge(speed_done[h], i + 2)
                    dve.tensor_tensor(half_of(xs, h), half_of(xs, h), w[:, h, :], ALU.add)\
                        .then_inc(state_done[h], 1)


def turn_add(nc, ch, featT, dst, add):
    psum = ch["psum"]
    with ExitStack() as st:
        turned, added = stage_semaphores(nc, ch, "turned", "added")
        block = st.enter_context(stage_block(nc, ch))

        @block.tensor
        def _(pe):
            for half in range(2):
                for i in range(TH):
                    mm = pe.transpose(psum[:, half, i * P:(i + 1) * P], featT[:, tile_cols(half * TH + i)],
                                      ch["identf"][:, :])
                mm.then_inc(turned, 1)

        @block.vector
        def _(dve):
            for half in range(2):
                dve.wait_ge(turned, half + 1)
                cols = slice(half * TH, (half + 1) * TH)
                dve.tensor_tensor(dst[:, cols, :], psum[:, half, :].rearrange("p (t d) -> p t d", d=D),
                                  add[:, cols, :], ALU.add).then_inc(added, 1)
            dve.wait_ge(added, 2)
    return added, 1, 0


def gelu_mlp(nc, ch, x0, x2, dst):
    psum, XT = ch["psum"], ch["XT"]
    with ExitStack() as st:
        hidden = st.enter_context(nc.sbuf_tensor("hidden", [P, NC, NTOK], F32))
        up_done, gelu_done, down_done, rest_done, added = stage_semaphores(
            nc, ch, "up_done", "gelu_done", "down_done", "rest_done", "added")
        absum_done, total_done, scaled, ternary, ctx_turned, ctx_kept, yw_turned, ternary_turned, ready, prepared, w_high = \
            stage_semaphores(nc, ch, "absum_done", "total_done", "scaled", "ternary", "ctx_turned", "ctx_kept",
                             "yw_turned", "ternary_turned", "ready", "prepared", "w_high")
        block = st.enter_context(stage_block(nc, ch))

        @block.tensor
        def _(pe):
            def up(half):
                for c in range(NC):
                    if half:
                        pe.wait_ge(gelu_done, c + 1)
                    pe.matmul(psum[:, c, :], ch["ffw1"][:, c * P:(c + 1) * P], XT[:, half * HALF:(half + 1) * HALF],
                              start=True, stop=True).then_inc(up_done, 1)

            def down(half):
                pe.wait_ge(gelu_done, NC * (half + 1))
                for i in range(TH):
                    for c in range(NC):
                        mm = pe.matmul(psum[:, 4 + half, i * P:(i + 1) * P], hidden[:, c, tile_cols(half * TH + i)],
                                       ch["ffw2"][:, c, :], start=(c == 0), stop=(c == NC - 1))
                mm.then_inc(down_done, 1)

            up(0)
            for half in range(2):
                for i in range(TH):
                    mm = pe.transpose(psum[:, 6 + half, i * P:(i + 1) * P], ch["C"][:, half * TH + i, :],
                                      ch["identf"][:, :])
                mm.then_inc(ctx_turned, 1)
            pe.wait_ge(absum_done, 2)
            pe.matmul(psum[:, 5, 0:2], ch["ones"][:, :], ch["absum"][:, :], start=True, stop=True).then_inc(total_done, 1)
            up(1)
            pe.wait_ge(ctx_kept, 1)
            for i in range(4):
                mm = pe.transpose(psum[:, 6, i * P:(i + 1) * P], ch["ywo"][:, i, :], ch["identf"][:, :])
            mm.then_inc(yw_turned, 1)
            down(0)
            pe.wait_ge(ternary, 2)
            pe.wait_ge(ctx_kept, 2)
            for m in range(2):
                for c in range(NC):
                    at = m * FF // 2 + c * 64
                    mm = pe.transpose(psum[:, 7, at:at + 64].bitcast(BF16), ch["wtern"][:, m, c * P:(c + 1) * P],
                                      ch["identb"][:, :])
            mm.then_inc(ternary_turned, 1)
            pe.wait_ge(scaled, 1)
            down(1)

        @block.scalar
        def _(act):
            def gelu(half):
                for c in range(NC):
                    act.wait_ge(up_done, half * NC + c + 1)
                    act.activation(hidden[:, c, half * HALF:(half + 1) * HALF], psum[:, c, :], ACT.Gelu,
                                   bias=ch["params"][:, 14 + c:15 + c]).then_inc(gelu_done, 1)

            gelu(0)
            for half in range(2):
                act.wait_ge(ctx_turned, half + 1)
                act.activation(ch["CT"][:, half * HALF:(half + 1) * HALF], psum[:, 6 + half, :], ACT.Copy)\
                    .then_inc(ctx_kept, 1)
            gelu(1)
            act.wait_ge(yw_turned, 1)
            act.activation(ch["yw"][:, :], psum[:, 6, :], ACT.Copy).then_inc(ready, 1)
            act.wait_ge(ternary_turned, 1)
            act.activation(ch["wternT"][:, :, :].rearrange("p m f -> p (m f)"), psum[:, 7, :].bitcast(BF16), ACT.Copy)\
                .then_inc(ready, 1)
            act.wait_ge(ready, 2)

        @block.vector
        def _(dve):
            w1, w2 = ch["bw1"][:, :, :].rearrange("p c d -> p (c d)"), ch["bw2"][:, :]
            for m, w in enumerate((w1, w2)):
                dve.tensor_reduce(ch["absum"][:, m:m + 1], w, AX, ALU.add, apply_absolute_value=True)\
                    .then_inc(absum_done, 1)
            dve.tensor_tensor(dst[:, :, :], x0[:, :, :], x2[:, :, :], ALU.add).then_inc(rest_done, 1)
            dve.wait_ge(rest_done, 1)
            dve.tensor_tensor(dst[:, :, :], dst[:, :, :], ch["rows"][:, 2, :].unsqueeze(1).to_broadcast([P, NT, D]),
                              ALU.add).then_inc(rest_done, 1)
            dve.wait_ge(total_done, 1)
            dve.tensor_scalar(ch["wmean"][:, :], psum[:, 5, 0:2], 1.0 / (FF * D), 1e-5, ALU.mult, ALU.max)\
                .then_inc(scaled, 1)
            dve.wait_ge(scaled, 1)
            dve.reciprocal(ch["winv"][:, :], ch["wmean"][:, :]).then_inc(scaled, 1)
            dve.wait_ge(scaled, 2)
            for m, w in enumerate((w1, w2)):
                dve.tensor_scalar(w, w, ch["winv"][:, m:m + 1], ROUND, ALU.mult, ALU.add).then_inc(scaled, 1)
                dve.wait_ge(scaled, 3 + 2 * m)
                dve.tensor_scalar(w, w, -ROUND, 1.0, ALU.add, ALU.min).then_inc(scaled, 1)
                dve.wait_ge(scaled, 4 + 2 * m)
                dve.tensor_scalar(ch["wtern"][:, m, :], w, -1.0, None, ALU.max).then_inc(ternary, 1)
            dve.wait_ge(rest_done, 2)
            for half in range(2):
                dve.wait_ge(down_done, half + 1)
                cols = slice(half * TH, (half + 1) * TH)
                dve.tensor_tensor(dst[:, cols, :], psum[:, 4 + half, :].rearrange("p (t d) -> p t d", d=D),
                                  dst[:, cols, :], ALU.add).then_inc(added, 1)
            dve.wait_ge(added, 2)

        @block.gpsimd
        def _(pool):
            for m in range(2):
                pool.tensor_copy(ch["xwkr"][:, m, :].rearrange("p (h d) -> p h d", d=HD),
                                 ch["xwkv"][:, m * HD:(m + 1) * HD].unsqueeze(1).to_broadcast([P, H, HD]))\
                    .then_inc(prepared, 1)
            for m, w in enumerate(("mwq", "mwk")):
                src = ch[w][:, :].rearrange("p (h r d) -> p h r d", r=2, d=HD // 2)
                turned = ch["mrot"][:, m, :].rearrange("p (h r d) -> p h r d", r=2, d=HD // 2)
                pool.tensor_scalar(turned[:, :, 0, :], src[:, :, 1, :], -1.0, None, ALU.mult).then_inc(prepared, 1)
                pool.tensor_copy(turned[:, :, 1, :], src[:, :, 0, :]).then_inc(prepared, 1)
            for e in range(2):
                pool.tensor_copy(ch["WH"][:, e, :], ch["We"][:, e, :]).then_inc(w_high, 1)
                pool.wait_ge(w_high, e + 1)
                pool.tensor_tensor(ch["WL"][:, e, :], ch["We"][:, e, :], ch["WH"][:, e, :].bitcast(F32), ALU.subtract)\
                    .then_inc(prepared, 1)
            pool.wait_ge(prepared, 8)


def quantized_ffn(nc, ch, x, dst, after=None):
    psum, identf, identb = ch["psum"], ch["identf"], ch["identb"]
    wT = ch["wternT"]
    w1T, w2T = wT[:, 0, :], wT[:, 1, :].rearrange("p (c d) -> p c d", d=D)
    with ExitStack() as st:
        def sb(n, shape, dt=F32):
            return st.enter_context(nc.sbuf_tensor(f"{n}_{ch.stage}", [P, *shape], dt))

        xq, xqT = sb("xq", [NT, D], BF16), sb("xqT", [NTOK], BF16)
        tmp, row_scale = sb("tmp", [NT, D]), sb("row_scale", [NTOK])
        amax, inv, back = sb("amax", [2, NT]), sb("inv", [2, NT]), sb("back", [2, NT])
        grid, mix = sb("grid", [2, HALF]), sb("mix", [NC, NTOK])
        htmp, hq, hqT = sb("htmp", [TH, FF]), sb("hq", [TH, FF], BF16), sb("hqT", [2, FF], BF16)
        (chain, x_clipped, x_quantized, x_turned, x_kept, rows_done, rows_kept, hid_done, grid_done, centre_done,
         left_done, conv_done, silu_done, h_turned, h_rounded, h_clipped, h_quantized, hq_turned, hq_kept, down_done,
         added) = stage_semaphores(
            nc, ch, "chain", "x_clipped", "x_quantized", "x_turned", "x_kept", "rows_done", "rows_kept", "hid_done",
            "grid_done", "centre_done", "left_done", "conv_done", "silu_done", "h_turned", "h_rounded", "h_clipped",
            "h_quantized", "hq_turned", "hq_kept", "down_done", "added")
        block = st.enter_context(stage_block(nc, ch))
        UNITS = 2 * NC

        def hidden_bank(t):
            return (2, 3, 4, 5, 0, 1, 4, 5)[t]

        def seqs(half, c):
            return mix[:, c, half * HALF:(half + 1) * HALF].rearrange("p (b s) -> p b s", s=S)

        def taps(u):
            return grid[:, u % 2, :].rearrange("p (b s) -> p b s", s=S)

        @block.vector
        def _(dve):
            n = 0

            def own(ins):
                nonlocal n
                ins.then_inc(chain, 1)
                n += 1
                dve.wait_ge(chain, n)

            def scales(m, cols):
                own(dve.tensor_scalar(amax[:, m, cols], amax[:, m, cols], 1e-5, None, ALU.max))
                own(dve.reciprocal(inv[:, m, cols], amax[:, m, cols]))
                own(dve.tensor_scalar(inv[:, m, cols], inv[:, m, cols], 127.0, None, ALU.mult))
                own(dve.tensor_scalar(back[:, m, cols], amax[:, m, cols], ch["wmean"][:, m:m + 1], 1.0 / 127.0, ALU.mult,
                                      ALU.mult))

            def add_tile(t):
                dve.wait_ge(down_done, t + 1)
                dve.scalar_tensor_tensor(out=dst[:, t, :], in0=psum[:, 2 + t % 2, tile_cols(t // 2)],
                                         scalar=back[:, 1, t:t + 1], in1=x[:, t, :], op0=ALU.mult, op1=ALU.add)\
                    .then_inc(added, 1)

            half_ready(dve, after, 1)
            own(dve.tensor_reduce(amax[:, 0, :], x[:, :, :], AX, ALU.max, apply_absolute_value=True))
            scales(0, slice(0, NT))
            for half in range(2):
                for t in range(half * TH, (half + 1) * TH):
                    dve.tensor_scalar(tmp[:, t, :], x[:, t, :], inv[:, 0, t:t + 1], ROUND, ALU.mult, ALU.add)\
                        .then_inc(chain, 1)
                n += TH
                dve.wait_ge(chain, n)
                cols = slice(half * TH, (half + 1) * TH)
                dve.tensor_scalar(tmp[:, cols, :], tmp[:, cols, :], ROUND + 127.0, ROUND - 128.0, ALU.min, ALU.max)\
                    .then_inc(x_clipped, 1)
            def scale_unit(u):
                half = u // NC
                dve.wait_ge(rows_kept, half + 1)
                dve.wait_ge(hid_done, u + 1)
                if u >= 2:
                    dve.wait_ge(centre_done, u - 1)
                    dve.wait_ge(conv_done, u - 1)
                dve.tensor_tensor(grid[:, u % 2, :], psum[:, u % 2, :], row_scale[:, half * HALF:(half + 1) * HALF],
                                  ALU.mult).then_inc(grid_done, 1)

            def add_taps(u):
                half, c = divmod(u, NC)
                y = seqs(half, c)
                dve.wait_ge(grid_done, u + 1)
                dve.wait_ge(centre_done, u + 1)
                dve.scalar_tensor_tensor(out=y[:, :, 1:S], in0=taps(u)[:, :, 0:S - 1], scalar=ch["convw"][:, c, 0:1],
                                         in1=y[:, :, 1:S], op0=ALU.mult, op1=ALU.add).then_inc(left_done, 1)
                dve.wait_ge(left_done, u + 1)
                dve.scalar_tensor_tensor(out=y[:, :, 0:S - 1], in0=taps(u)[:, :, 1:S], scalar=ch["convw"][:, c, 2:3],
                                         in1=y[:, :, 0:S - 1], op0=ALU.mult, op1=ALU.add).then_inc(conv_done, 1)

            scale_unit(0)
            for u in range(UNITS):
                if u + 1 < UNITS:
                    scale_unit(u + 1)
                add_taps(u)
            for half in range(2):
                tiles, cols = range(half * TH, (half + 1) * TH), slice(half * TH, (half + 1) * TH)
                for t in tiles:
                    dve.wait_ge(h_turned, t + 1)
                    dve.tensor_reduce(amax[:, 1, t:t + 1], psum[:, hidden_bank(t), :], AX, ALU.max,
                                      apply_absolute_value=True).then_inc(chain, 1)
                n += TH
                dve.wait_ge(chain, n)
                scales(1, cols)
                for t in tiles:
                    if half:
                        dve.wait_ge(h_quantized, t - TH + 1)
                    dve.tensor_scalar(htmp[:, t % TH, :], psum[:, hidden_bank(t), :], inv[:, 1, t:t + 1], ROUND,
                                      ALU.mult, ALU.add).then_inc(h_rounded, 1)
                    dve.wait_ge(h_rounded, t + 1)
                    dve.tensor_scalar(htmp[:, t % TH, :], htmp[:, t % TH, :], ROUND + 127.0, ROUND - 128.0, ALU.min,
                                      ALU.max).then_inc(h_clipped, 1)
                    if half:
                        add_tile(t - TH)
            for t in range(TH, NT):
                add_tile(t)
            dve.wait_ge(added, NT)

        @block.scalar
        def _(act):
            for half in range(2):
                cols = slice(half * TH, (half + 1) * TH)
                act.wait_ge(x_clipped, half + 1)
                act.activation(xq[:, cols, :], tmp[:, cols, :], ACT.Identity, bias=ch["unround"][:, :])\
                    .then_inc(x_quantized, 1)
            for half in range(2):
                cols = slice(half * HALF, (half + 1) * HALF)
                act.wait_ge(rows_done, half + 1)
                act.activation(row_scale[:, cols], psum[:, 6 + half, :], ACT.Copy).then_inc(rows_kept, 1)
                act.wait_ge(x_turned, half + 1)
                act.activation(xqT[:, cols], psum[:, 4 + half, 0:HALF // 2].bitcast(BF16), ACT.Copy).then_inc(x_kept, 1)

            def silu(u):
                half, c = divmod(u, NC)
                act.wait_ge(conv_done, u + 1)
                act.activation(seqs(half, c), seqs(half, c), ACT.Silu).then_inc(silu_done, 1)

            for u in range(UNITS):
                half, c = divmod(u, NC)
                act.wait_ge(grid_done, u + 1)
                act.activation(seqs(half, c), taps(u), ACT.Identity, scale=ch["convw"][:, c, 1:2],
                               bias=ch["params"][:, 14 + NC + c:15 + NC + c]).then_inc(centre_done, 1)
                if u >= 2:
                    silu(u - 2)
            silu(UNITS - 2)
            silu(UNITS - 1)

            def keep(t):
                act.wait_ge(hq_turned, t + 1)
                if t >= 2:
                    act.wait_ge(down_done, t - 1)
                act.activation(hqT[:, t % 2, :], psum[:, 6 + t % 2, 0:FF // 2].bitcast(BF16), ACT.Copy)\
                    .then_inc(hq_kept, 1)

            for t in range(NT):
                act.wait_ge(h_clipped, t + 1)
                if t >= TH:
                    act.wait_ge(hq_turned, t - TH + 1)
                act.activation(hq[:, t % TH, :], htmp[:, t % TH, :], ACT.Identity, bias=ch["unround"][:, :])\
                    .then_inc(h_quantized, 1)
                if t:
                    keep(t - 1)
            keep(NT - 1)

        @block.tensor
        def _(pe):
            pe.wait_ge(chain, 5)
            for half in range(2):
                for i in range(TH):
                    t = half * TH + i
                    mm = pe.matmul(psum[:, 6 + half, i * P:(i + 1) * P], back[:, 0, t:t + 1].to_broadcast([P, P]),
                                   identf[:, :], start=True, stop=True)
                mm.then_inc(rows_done, 1)
            for half in range(2):
                pe.wait_ge(x_quantized, half + 1)
                for i in range(TH):
                    mm = pe.transpose(psum[:, 4 + half, i * 64:(i + 1) * 64].bitcast(BF16), xq[:, half * TH + i, :],
                                      identb[:, :])
                mm.then_inc(x_turned, 1)

            def turn_hidden(t):
                pe.wait_ge(silu_done, NC if t < TH else UNITS)
                if t < TH:
                    pe.wait_ge(x_kept, 2)
                else:
                    pe.wait_ge(grid_done, UNITS)
                    if t >= TH + 2:
                        pe.wait_ge(h_rounded, TH)
                for c in range(NC):
                    mm = pe.transpose(psum[:, hidden_bank(t), c * P:(c + 1) * P], mix[:, c, tile_cols(t)], identf[:, :])
                mm.then_inc(h_turned, 1)

            for u in range(UNITS):
                half, c = divmod(u, NC)
                pe.wait_ge(x_kept, half + 1)
                if u >= 2:
                    pe.wait_ge(grid_done, u - 1)
                pe.matmul(psum[:, u % 2, :], w1T[:, c * P:(c + 1) * P], xqT[:, half * HALF:(half + 1) * HALF],
                          start=True, stop=True).then_inc(hid_done, 1)
            for t in range(NT):
                turn_hidden(t)

            def turn_rows(t):
                pe.wait_ge(h_quantized, t + 1)
                if t >= 2:
                    pe.wait_ge(hq_kept, t - 1)
                for c in range(NC):
                    mm = pe.transpose(psum[:, 6 + t % 2, c * 64:(c + 1) * 64].bitcast(BF16),
                                      hq[:, t % TH, c * P:(c + 1) * P], identb[:, :])
                mm.then_inc(hq_turned, 1)

            for t in range(NT):
                if t == 0:
                    pe.wait_ge(rows_kept, 2)
                    turn_rows(t)
                if t + 1 < NT:
                    turn_rows(t + 1)
                pe.wait_ge(hq_kept, t + 1)
                pe.wait_ge(h_rounded, TH)
                if t >= 2:
                    pe.wait_ge(added, t - 1)
                for c in range(NC):
                    mm = pe.matmul(psum[:, 2 + t % 2, tile_cols(t // 2)], hqT[:, t % 2, c * P:(c + 1) * P],
                                   w2T[:, c, :], start=(c == 0), stop=(c == NC - 1))
                mm.then_inc(down_done, 1)
    return added, TH, 0


def wide_attention(nc, ch, w_qkv, w_o, dst):
    psum, XT = ch["psum"], ch["XT"]
    Pr, PT, mx, den, rden = (ch[n] for n in ("Pr", "PT", "mx", "den", "rden"))
    with ExitStack() as st:
        def sb(n, shape):
            return st.enter_context(nc.sbuf_tensor(n, [P, *shape], F32))

        W, Wo = ch["Wa"], sb("Wo", [2, D])
        QK, Vp, ctx = sb("QK", [2, 2, NTOK]), sb("Vp", [2, 2, NT, N1]), sb("ctx", [2, NTOK])
        loaded = stage_semaphores(nc, ch, "loaded0", "loaded1")
        loaded_out = stage_semaphores(nc, ch, "loaded_out0", "loaded_out1")
        (qk_done, qk_kept, v_done, v_kept, scores_done, max_done, centred, exp_done, sum_done, inverse_done,
         probs_done, turned, turned_kept, pv_done, ctx_kept, out_done, added) = stage_semaphores(
            nc, ch, "qk_done", "qk_kept", "v_done", "v_kept", "scores_done", "max_done", "centred", "exp_done",
            "sum_done", "inverse_done", "probs_done", "turned", "turned_kept", "pv_done", "ctx_kept", "out_done",
            "added")
        (waited,) = stage_semaphores(nc, ch, "waited")
        block = st.enter_context(stage_block(nc, ch))

        def pairs(eng, before, step):
            before()
            with eng.Fori(0, NP1 // 2 - 1) as i:
                step(2 * i, i, 0, True, True)
                step(2 * i + 1, i, 1, True, True)
            step(NP1 - 2, NP1 // 2 - 1, 0, True, False)
            step(NP1 - 1, NP1 // 2 - 1, 1, False, False)

        @block.sync
        def _(sp):
            def load_in(j, s):
                sp.wait_ge(v_done, 2 * j + 2)
                for par in range(2):
                    h = 2 * j + par
                    sp.dma_start(W[:, s, :, par, :], w_qkv[bass.ds(h, 1)].rearrange("h a v n -> v (h a) n"))\
                        .then_inc(loaded[s], 16)

            def load_out(j, s):
                sp.wait_ge(out_done, j + 1)
                sp.dma_start(Wo[:, s, :], w_o[bass.ds(j * P, P), :]).then_inc(loaded_out[s], 16)

            load_out(0, 0)
            with sp.Fori(1, NP1 // 2) as i:
                load_in(2 * i, 0)
                load_out(2 * i - 1, 1)
                load_in(2 * i + 1, 1)
                load_out(2 * i, 0)
            load_out(NP1 - 1, 1)

        @block.tensor
        def _(pe):
            def project(j, i, s):
                if not isinstance(j, int) or j >= 2:
                    pe.wait_ge(loaded[s], 32 * i)
                pe.wait_ge(ctx_kept, 2 * j + 2)
                for m in range(2):
                    for half in range(2):
                        pe.wait_ge(qk_kept, 4 * j + 2 * m + half + 3)
                        pe.matmul(psum[:, half, :], W[:, s, m, :, :].rearrange("p a n -> p (a n)"),
                                  XT[:, half * HALF:(half + 1) * HALF], start=True, stop=True).then_inc(qk_done, 1)

            def project_values(j, s, half):
                pe.wait_ge(v_kept, 4 * j + 4)
                for i4 in range(TH):
                    mm = pe.matmul(psum[:, 2 + half, i4 * P:(i4 + 1) * P], XT[:, tile_cols(half * TH + i4)],
                                   W[:, s, 2, :, :].rearrange("p a n -> p (a n)"), start=True, stop=True)
                mm.then_inc(v_done, 1)

            def scores(j, s):
                pe.wait_ge(qk_kept, 4 * j + 8)
                pe.wait_ge(centred, j + 1)
                pe.sem_inc(waited, 1)
                for t in range(NT):
                    for b in range(2):
                        for par in range(2):
                            rows, cols = slice(64 * par, 64 * par + 64), slice(t * P + 64 * b, t * P + 64 * b + 64)
                            mm = pe.matmul(psum[64 * b:64 * b + 64, 4 + par, t * S:(t + 1) * S],
                                           QK[rows, s, 0, cols], QK[rows, s, 1, cols], start=True, stop=True)
                mm.then_inc(scores_done, 1)

            def turn(j, s):
                pe.wait_ge(probs_done, j + 1)
                pe.wait_ge(added, 2 * j + 2)
                for t in range(NT):
                    mm = pe.transpose(psum[:, 6 + t // TH, (t % TH) * P:(t % TH + 1) * P],
                                      Pr[:, s, 2 * t:2 * t + 2, :].rearrange("p a k -> p (a k)"), ch["identf"][:, :])
                mm.then_inc(turned, 1)

            def values(j, s, ahead):
                pe.wait_ge(turned_kept, 2 * j + 2)
                pe.wait_ge(v_kept, 4 * j + 8)
                pe.wait_ge(qk_kept, 4 * j + 8 + 4 * ahead)
                pe.sem_inc(waited, 1)
                for t in range(NT):
                    for b in range(2):
                        for par in range(2):
                            rows = slice(64 * par, 64 * par + 64)
                            col = (t % TH) * P + 64 * b
                            mm = pe.matmul(psum[rows, t // TH, col:col + 64], Vp[rows, s, b, t, :],
                                           PT[rows, s, t, 64 * b:64 * b + 64], start=True, stop=True)
                mm.then_inc(pv_done, 1)

            def output(j, i, s):
                pe.wait_ge(loaded_out[s], 16 * i + 16)
                for half in range(2):
                    pe.wait_ge(ctx_kept, 2 * j + 7 + half)
                    for i4 in range(TH):
                        mm = pe.matmul(psum[:, 6 + half, i4 * P:(i4 + 1) * P], ctx[:, s, tile_cols(half * TH + i4)],
                                       Wo[:, s, :], start=True, stop=True)
                mm.then_inc(out_done, 1)

            def before():
                pe.sem_inc(out_done, 2)
                pe.sem_inc(v_done, 4)
                pe.sem_inc(scores_done, 2)
                pe.sem_inc(pv_done, 2)
                pe.sem_inc(turned, 2)
                project(0, 0, 0)
                scores(0, 0)
                for half in range(2):
                    project_values(0, 0, half)
                project(1, 0, 1)
                for half in range(2):
                    project_values(1, 1, half)

            def step(j, i, s, one, two):
                if one:
                    scores(j + 1, 1 - s)
                turn(j, s)
                if two:
                    project(j + 2, i + 1, s)
                    project_values(j + 2, s, 0)
                values(j, s, one + two)
                if two:
                    project_values(j + 2, s, 1)
                output(j, i, s)

            pairs(pe, before, step)

        @block.scalar
        def _(act):
            def keep_qk(j, s, m):
                act.wait_ge(scores_done, j + 1)
                for half in range(2):
                    act.wait_ge(qk_done, 4 * j + 2 * m + half + 1)
                    act.activation(QK[:, s, m, half * HALF:(half + 1) * HALF], psum[:, half, :], ACT.Copy)\
                        .then_inc(qk_kept, 1)

            def keep_values(j, s):
                act.wait_ge(pv_done, j + 1)
                act.wait_ge(v_done, 2 * j + 6)
                v = psum[:, 2:4, :].rearrange("p a (t c n) -> p (a t) c n", c=2, n=N1)
                for b in range(2):
                    for par in range(2):
                        act.activation(Vp[64 * par:64 * par + 64, s, b, :, :], v[64 * b:64 * b + 64, :, par, :],
                                       ACT.Copy).then_inc(v_kept, 1)

            def exponentials(j, s):
                act.wait_ge(centred, j + 2)
                act.activation(Pr[:, s, :, :], Pr[:, s, :, :], ACT.Exp, scale=float(N1) ** -0.5).then_inc(exp_done, 1)

            def keep_turned(j, s):
                act.wait_ge(turned, j + 3)
                act.wait_ge(pv_done, j + 1)
                for m in range(2):
                    act.activation(PT[:, s, 4 * m:4 * m + 4, :].rearrange("p h q -> p (h q)"), psum[:, 6 + m, :],
                                   ACT.Copy).then_inc(turned_kept, 1)

            def before():
                act.sem_inc(qk_kept, 4)
                act.sem_inc(v_kept, 4)
                for m in range(2):
                    keep_qk(0, 0, m)
                exponentials(0, 0)
                keep_values(0, 0)
                for m in range(2):
                    keep_qk(1, 1, m)
                keep_values(1, 1)

            def step(j, i, s, one, two):
                keep_turned(j, s)
                if two:
                    keep_qk(j + 2, s, 0)
                if one:
                    exponentials(j + 1, 1 - s)
                if two:
                    keep_qk(j + 2, s, 1)
                    keep_values(j + 2, s)

            pairs(act, before, step)

        @block.gpsimd
        def _(pool):
            def step(j, i, s, one, two):
                pool.wait_ge(inverse_done, j + 1)
                pool.tensor_tensor(Pr[:, s, :, :], Pr[:, s, :, :], rden[:, s, :].unsqueeze(2).to_broadcast([P, 16, S]),
                                   ALU.mult).then_inc(probs_done, 1)

            pairs(pool, lambda: None, step)

        @block.vector
        def _(dve):
            def centre(j, s):
                dve.wait_ge(scores_done, j + 3)
                sc = psum[:, 4:6, :].rearrange("p a (t k) -> p a t k", k=S)
                dve.tensor_reduce(mx[:, s, :].rearrange("p (a t) -> p a t", a=2), sc, AX, ALU.max)\
                    .then_inc(max_done, 1)
                dve.wait_ge(max_done, j + 1)
                dve.wait_ge(turned, j + 1)
                m = mx[:, s, :].rearrange("p (a t) -> p a t", a=2).unsqueeze(3).to_broadcast([P, 2, NT, S])
                dve.tensor_tensor(Pr[:, s, :, :].rearrange("p (t a) k -> p a t k", a=2), sc, m, ALU.subtract)\
                    .then_inc(centred, 1)

            def invert(j, s):
                dve.wait_ge(exp_done, j + 1)
                dve.tensor_reduce(den[:, s, :], Pr[:, s, :, :], AX, ALU.add).then_inc(sum_done, 1)
                dve.wait_ge(sum_done, j + 1)
                dve.reciprocal(rden[:, s, :], den[:, s, :]).then_inc(inverse_done, 1)

            def before():
                dve.sem_inc(centred, 1)
                dve.sem_inc(ctx_kept, 6)
                dve.sem_inc(added, 2)
                centre(0, 0)
                invert(0, 0)

            def step(j, i, s, one, two):
                if one:
                    centre(j + 1, 1 - s)
                    invert(j + 1, 1 - s)
                dve.wait_ge(pv_done, j + 3)
                dve.wait_ge(out_done, j + 1)
                for half in range(2):
                    dve.tensor_copy(ctx[:, s, half * HALF:(half + 1) * HALF], psum[:, half, :])\
                        .then_inc(ctx_kept, 1)
                dve.wait_ge(out_done, j + 3)
                for half in range(2):
                    rows = dst[:, half * TH:(half + 1) * TH, :]
                    dve.wait_ge(added, 2 * j + half + 1)
                    dve.tensor_tensor(rows, psum[:, 6 + half, :].rearrange("p (t d) -> p t d", d=D), rows, ALU.add)\
                        .then_inc(added, 1)

            pairs(dve, before, step)


def split_product(pe, out, lhs, rhs, start=True, stop=True):
    (lhs_high, lhs_low), (rhs_high, rhs_low) = lhs, rhs
    pe.matmul(out, lhs_high, rhs_high, start=start, stop=False)
    pe.matmul(out, lhs_high, rhs_low, start=False, stop=False)
    return pe.matmul(out, lhs_low, rhs_high, start=False, stop=stop)


def experts(nc, ch, wg, wu, wd, dst):
    psum, XT, comb = ch["psum"], ch["XT"], ch["comb"]
    W, Wd, WH, WL = ch["We"], ch["Wd"], ch["WH"], ch["WL"]
    with ExitStack() as st:
        def sb(n, shape, dt=F32):
            return st.enter_context(nc.sbuf_tensor(f"{n}_{ch.stage}", [P, *shape], dt))

        XH, XL = sb("XH", [NTOK], F32R), sb("XL", [NTOK], F32R)
        rows = (XH, XL)
        sg, prod = sb("sg", [HC, HALF]), sb("prod", [2, HC, HALF])
        prob, top, at, atf = sb("prob", [NT, NE]), sb("top", [NT, 8]), sb("at", [NT, 8], U32), sb("atf", [NT, 8])
        hi, total, pick, iota = sb("hi", [NT]), sb("total", [NT]), sb("pick", [2, NT, NE]), ch["iota8"]
        loaded = stage_semaphores(nc, ch, "loaded0", "loaded1")
        logits_done, chain, exp_done = stage_semaphores(nc, ch, "logits_done", "chain", "exp_done")
        w_high, w_low, x_high, x_low = stage_semaphores(nc, ch, "w_high", "w_low", "x_high", "x_low")
        gate_done, up_done, silu_done, prod_done, down_done, added = stage_semaphores(
            nc, ch, "gate_done", "up_done", "silu_done", "prod_done", "down_done", "added")
        block = st.enter_context(stage_block(nc, ch))

        def units(eng, step):
            with eng.Fori(0, NE // 2 - 1) as i:
                for k in range(4):
                    step(4 * i + k, i, k, True)
            for k in range(4):
                step(2 * NE - 4 + k, NE // 2 - 1, k, k < 3)

        def parts(high, low, *at):
            return high[at], low[at]

        @block.sync
        def _(sp):
            def load(e, s):
                for n, w in enumerate((wg, wu)):
                    sp.dma_start(W[:, s, n * HID:(n + 1) * HID].unsqueeze(1),
                                 w[bass.ds(e, 1)].rearrange("e d n -> d e n")).then_inc(loaded[s], 16)
                sp.dma_start(Wd[:, s, :, :], wd[bass.ds(e, 1)].rearrange("e (c p) d -> p (e c) d", p=P))\
                    .then_inc(loaded[s], 16)

            with sp.Fori(1, NE // 2) as i:
                for s in range(2):
                    sp.wait_ge(down_done, 4 * i + 2 * s)
                    load(2 * i + s, s)

        @block.gpsimd
        def _(pool):
            def split(i, s):
                pool.wait_ge(loaded[s], 48 * i)
                pool.tensor_tensor(WH[:, s, :], W[:, s, :], ch["ones"][:, 0:1].to_broadcast([P, 2 * HID]), ALU.mult).then_inc(w_high, 1)
                pool.wait_ge(w_high, 2 * i + s + 1)
                pool.tensor_tensor(WL[:, s, :], W[:, s, :], WH[:, s, :].bitcast(F32), ALU.subtract).then_inc(w_low, 1)

            pool.sem_inc(w_high, 2)
            pool.sem_inc(w_low, 2)
            with pool.Fori(1, NE // 2) as i:
                split(i, 0)
                split(i, 1)

        @block.tensor
        def _(pe):
            def up(u, i, k):
                s, half = (k // 2) % 2, k % 2
                pe.wait_ge(x_low, half + 1)
                pe.wait_ge(w_low, 2 * i + s + 1)
                rhs = parts(*rows, slice(None), slice(half * HALF, (half + 1) * HALF))
                for c in range(HC):
                    gate = parts(WH, WL, slice(None), s, slice(c * P, (c + 1) * P))
                    lift = parts(WH, WL, slice(None), s, slice(HID + c * P, HID + (c + 1) * P))
                    pe.wait_ge(silu_done, 3 * u + c + 1)
                    split_product(pe, psum[:, c, :], gate, rhs).then_inc(gate_done, 1)
                    pe.wait_ge(prod_done, 3 * u + c + 1)
                    split_product(pe, psum[:, HC + c, :], lift, rhs).then_inc(up_done, 1)

            def down(u, k):
                s = k // 2
                pe.wait_ge(prod_done, 3 * u + 6)
                pe.wait_ge(added, 4 * u + 4)
                for i4 in range(TH):
                    for c in range(HC):
                        mm = pe.matmul(psum[:, 6 + k % 2, i4 * P:(i4 + 1) * P], prod[:, k % 2, c, tile_cols(i4)],
                                       Wd[:, s, c, :], start=(c == 0), stop=(c == HC - 1))
                mm.then_inc(down_done, 1)

            def step(u, i, k, ahead):
                if ahead:
                    up(u + 1, i + (k + 1) // 4, (k + 1) % 4)
                down(u, k)

            for t in range(NT):
                mm = pe.matmul(psum[:, 7, t * NE:(t + 1) * NE], XT[:, tile_cols(t)], ch["wrout"][:, :], start=True,
                               stop=True)
            mm.then_inc(logits_done, 1)
            pe.sem_inc(down_done, 2)
            up(0, 0, 0)
            units(pe, step)

        @block.scalar
        def _(act):
            def gate(u, k):
                for c in range(HC):
                    act.wait_ge(gate_done, 3 * u + c + 1)
                    act.wait_ge(prod_done, 3 * u + c + 1)
                    act.activation(sg[:, c, :], psum[:, c, :], ACT.Silu).then_inc(silu_done, 1)

            for half in range(2):
                cols = slice(half * HALF, (half + 1) * HALF)
                act.activation(XH[:, cols], XT[:, cols], ACT.Copy).then_inc(x_high, 1)
            act.wait_ge(chain, 2)
            act.activation(prob[:, :, :], prob[:, :, :], ACT.Exp).then_inc(exp_done, 1)
            act.sem_inc(silu_done, 3)
            gate(0, 0)
            units(act, lambda u, i, k, ahead: gate(u + 1, (k + 1) % 4) if ahead else None)

        @block.vector
        def _(dve):
            def multiply(u, k):
                dve.wait_ge(down_done, u + 1)
                for c in range(HC):
                    dve.wait_ge(silu_done, 3 * u + c + 4)
                    dve.wait_ge(up_done, 3 * u + c + 1)
                    dve.tensor_tensor(prod[:, k % 2, c, :], psum[:, HC + c, :], sg[:, c, :], ALU.mult)\
                        .then_inc(prod_done, 1)

            def add(u, i, k):
                half = k % 2
                dve.wait_ge(down_done, u + 3)
                dve.wait_ge(added, 4 * u + 4)
                for i4 in range(TH):
                    t = half * TH + i4
                    dve.scalar_tensor_tensor(out=dst[:, t, :], in0=psum[:, 6 + half, i4 * P:(i4 + 1) * P],
                                             scalar=comb[:, t, bass.ds(2 * i + k // 2, 1)], in1=dst[:, t, :],
                                             op0=ALU.mult, op1=ALU.add).then_inc(added, 1)

            def step(u, i, k, ahead):
                if ahead:
                    multiply(u + 1, (k + 1) % 4)
                add(u, i, k)

            dve.sem_inc(prod_done, 3)
            for half in range(2):
                cols = slice(half * HALF, (half + 1) * HALF)
                dve.wait_ge(x_high, half + 1)
                dve.tensor_tensor(XL[:, cols], XT[:, cols], XH[:, cols].bitcast(F32), ALU.subtract).then_inc(x_low, 1)
            n = 0

            def own(*ins):
                nonlocal n
                for x in ins:
                    x.then_inc(chain, 1)
                n += len(ins)
                dve.wait_ge(chain, n)

            def wide(a):
                return a.unsqueeze(2).to_broadcast([P, NT, NE])

            dve.wait_ge(logits_done, 1)
            logits = psum[:, 7, 0:NT * NE].rearrange("p (t e) -> p t e", e=NE)
            own(dve.tensor_reduce(hi[:, :], logits, AX, ALU.max))
            own(dve.tensor_tensor(prob[:, :, :], logits, wide(hi[:, :]), ALU.subtract))
            dve.wait_ge(exp_done, 1)
            own(dve.tensor_reduce(total[:, :], prob[:, :, :], AX, ALU.add))
            own(dve.reciprocal(total[:, :], total[:, :]))
            own(dve.tensor_tensor(prob[:, :, :], prob[:, :, :], wide(total[:, :]), ALU.mult))
            own(*[dve.max(top[:, t, :], prob[:, t, :]) for t in range(NT)])
            own(*[dve.max_index(at[:, t, :], top[:, t, :], prob[:, t, :]) for t in range(NT)])
            own(dve.tensor_copy(atf[:, :, :], at[:, :, :]))
            own(dve.tensor_tensor(total[:, :], top[:, :, 0], top[:, :, 1], ALU.add))
            own(dve.reciprocal(total[:, :], total[:, :]))
            for k in range(2):
                own(dve.tensor_tensor(pick[:, k, :, :], wide(atf[:, :, k]),
                                      iota[:, :].unsqueeze(1).to_broadcast([P, NT, NE]), ALU.is_equal))
                own(dve.tensor_tensor(pick[:, k, :, :], pick[:, k, :, :], wide(top[:, :, k]), ALU.mult))
            own(dve.tensor_tensor(pick[:, 0, :, :], pick[:, 0, :, :], pick[:, 1, :, :], ALU.add))
            own(dve.tensor_tensor(comb[:, :, :], pick[:, 0, :, :], wide(total[:, :]), ALU.mult))
            dve.sem_inc(added, 8)
            multiply(0, 0)
            units(dve, step)


def decoder(nc, ins, cst, out):
    with ExitStack() as stack:
        ch = Chip(nc, stack)
        ch.buf["psum"] = stack.enter_context(nc.psum_tensor("psum", [P, 8, 512], F32))
        for name in ("X", "A", "R"):
            ch.sb(name, [NT, D])
        for name in ("XT", "CT", "AT", "LT"):
            ch.sb(name, [NTOK])
        for name in ("QP", "KP"):
            ch.sb(name, [2, HALF])
        ch.sb("V", [NT, D])
        ch.sb("rot", [4, HALF])
        ch.sb("Kx", [2, 2, 8, S])
        ch.sb("Qd", [2, 2, P])
        ch.sb("Vd", [2, 2, 4, 64])
        ch.sb("Pr", [2, H, S])
        ch.sb("Pn", [2, H, S])
        ch.sb("PT", [2, 8, P])
        for name in ("mx", "den", "rden", "pad"):
            ch.sb(name, [2, H])
        ch.sb("minus_half", [NT])
        ch.sb("unround", [1])
        ch.sb("identf", [P])
        ch.sb("identb", [P], BF16)
        ch.sb("ones", [P])
        ch.sb("causal", [S], BF16)
        ch.sb("causalf", [S])
        ch.sb("head_of", [8])
        ch.sb("iota8", [NE])
        ch.sb("cos", [S])
        ch.sb("sin", [S])
        ch.sb("wqkv0", [3 * D])
        for name in ("wo0", "wctx", "wx", "xwq", "xwo", "mwq", "mwk", "mwv", "mwo"):
            ch.sb(name, [D])
        ch.sb("xwkv", [2 * HD])
        ch.sb("C", [NT, D])
        ch.sb("Wa", [2, 3, 2, N1])
        ch.sb("We", [2, 2 * HID])
        ch.sb("Wd", [2, HC, D])
        ch.sb("WH", [2, 2 * HID], F32R)
        ch.sb("WL", [2, 2 * HID], F32R)
        ch.sb("xwkr", [2, D])
        ch.sb("ffw1", [FF])
        ch.sb("ffw2", [NC, D])
        ch.sb("bw1", [NC, D])
        ch.sb("bw2", [FF])
        ch.sb("wtern", [2, FF], BF16)
        ch.sb("wternT", [2, FF], BF16)
        ch.sb("convw", [NC, 3])
        ch.sb("absum", [2])
        ch.sb("wmean", [2])
        ch.sb("winv", [2])
        ch.sb("ywo", [4, D])
        ch.sb("yw", [4 * D])
        ch.sb("mrot", [2, D])
        ch.sb("wrout", [NE])
        ch.sb("comb", [NT, NE])
        ch.sb("rows", [3, D])
        ch.sb("prow", [P])
        ch.sb("params", [NPAR])
        X, R, A, XT, CT, LT = (ch[n] for n in ("X", "R", "A", "XT", "CT", "LT"))

        later_loads = load_inputs(nc, ch, ins, cst)
        w = ch["wqkv0"]
        with joined_stages(nc, ch):
            _, feat = norm(nc, ch, X, R, XT, gain=0, shift=1)
            qkv = small_qkv(nc, ch, (w[:, 0:D], XT), (w[:, D:2 * D], XT), (w[:, 2 * D:3 * D], XT), bias=True, after=feat)
            small_attention(nc, ch, causal=True, loads=later_loads, after=qkv)
        with joined_stages(nc, ch):
            rows = project_add(nc, ch, ch["wo0"][:, :], A, [X, ch["rows"][:, 1, :]], featT=LT, feat_bias=7)
            norm(nc, ch, A, R, XT, gain=2, shift=3, after=rows)
        inner_steps(nc, ch)
        with joined_stages(nc, ch):
            rows = turn_add(nc, ch, XT, A, A)
            norm(nc, ch, A, R, XT, gain=4, shift=5, after=rows)
        gelu_mlp(nc, ch, X, A, R)
        with joined_stages(nc, ch):
            kv = small_qkv(nc, ch, k=(ch["xwkr"][:, 0, :], CT), v=(ch["xwkr"][:, 1, :], CT))
            _, feat = norm(nc, ch, R, X, XT)
            q = small_qkv(nc, ch, q=(ch["xwq"][:, :], XT), after=feat)
            heads = small_attention(nc, ch, zero_keys=2 * S, after=kv + q)
            rows = project_add(nc, ch, ch["xwo"][:, :], R, [X], after=heads)
            rows, _ = norm(nc, ch, R, X, after=rows)
            rows = quantized_ffn(nc, ch, X, R, after=rows)
            norm(nc, ch, R, X, XT, after=rows)
        wide_attention(nc, ch, ins["L1_attn_w_qkv"], ins["L1_attn_w_o"], X)
        yw = ch["yw"]
        with joined_stages(nc, ch):
            kv = small_qkv(nc, ch, k=(yw[:, D:2 * D], CT), v=(yw[:, 2 * D:3 * D], CT))
            _, feat = norm(nc, ch, X, X, XT)
            q = small_qkv(nc, ch, q=(yw[:, 0:D], XT), after=feat)
            heads = small_attention(nc, ch, after=kv + q)
            rows = project_add(nc, ch, yw[:, 3 * D:4 * D], R, [X], after=heads)
            rows, _ = norm(nc, ch, R, X, after=rows)
            _, feat = norm(nc, ch, X, R, XT, gain=8, eps=1e-6, rms=True, after=rows)
            qkv = small_qkv(nc, ch, (ch["mwq"][:, :], XT), (ch["mwk"][:, :], XT), (ch["mwv"][:, :], XT),
                            rotated=(ch["mrot"][:, 0, :], ch["mrot"][:, 1, :]), after=feat)
            heads = small_attention(nc, ch, causal=True, after=qkv)
            rows = project_add(nc, ch, ch["mwo"][:, :], R, [X], after=heads)
            norm(nc, ch, R, A, XT, gain=9, eps=1e-6, rms=True, after=rows)
        experts(nc, ch, ins["L1_ffn_wg"], ins["L1_ffn_wu"], ins["L1_ffn_wd"], R)
        with joined_stages(nc, ch):
            rows = sum_rows(nc, ch, R, X)
            norm(nc, ch, R, X, out=out, after=rows)
        nc.clear_and_free_semaphores(ch.past)


def sum_rows(nc, ch, dst, add):
    with ExitStack() as st:
        (added,) = stage_semaphores(nc, ch, "added")
        block = st.enter_context(stage_block(nc, ch))

        @block.vector
        def _(dve):
            for half in range(2):
                cols = slice(half * TH, (half + 1) * TH)
                dve.tensor_tensor(dst[:, cols, :], dst[:, cols, :], add[:, cols, :], ALU.add).then_inc(added, 1)
            dve.wait_ge(added, 2)
    return added, 1, 0



def constants():
    p = np.arange(P)
    inv_freq = 1.0 / 10000.0 ** (np.arange(0, HD, 2, dtype=np.float32) / HD)
    freqs = np.einsum("i,j->ij", np.arange(S, dtype=np.float32), inv_freq)
    emb = np.concatenate([freqs, freqs], axis=-1)
    return {
        "identf": np.eye(P, dtype=np.float32),
        "causal": np.where(np.arange(S)[None, :] > (p % S)[:, None], MASKED, 0.0).astype(np.float32),
        "head_of": ((p[:, None] // HD) % 8 == np.arange(8)[None, :]).astype(np.float32),
        "iota8": np.tile(np.arange(NE, dtype=np.float32), (P, 1)),
        "cos": np.ascontiguousarray(np.cos(emb).astype(np.float32)[:, p % HD].T),
        "sin": np.ascontiguousarray(np.sin(emb).astype(np.float32)[:, p % HD].T),
    }


def kernel(**inputs):
    import numpy as _np
    import concourse.bacc as _bacc
    from concourse import mybir as _mybir
    from concourse.bass_utils import run_bass_kernel_spmd as _run

    nc = _bacc.Bacc("TRN2", target_bir_lowering=False, num_devices=1)
    arrays, ins, cst = {}, {}, {}
    for group, given in ((ins, inputs), (cst, constants())):
        for name, a in given.items():
            a = _np.ascontiguousarray(a)
            arrays[f"in_{name}_dram"] = a
            group[name] = nc.dram_tensor(f"in_{name}_dram", a.shape, _mybir.dt.from_np(a.dtype),
                                         kind="ExternalInput").ap()
    out = nc.dram_tensor("out_0_dram", (B, S, D), F32, kind="ExternalOutput").ap()
    decoder(nc, ins, cst, out)
    r = _run(nc, [arrays], core_ids=[0])
    return r.results[0]["out_0_dram"]
```
